# Optimizing a Trainium2 kernel written in Bass

```python
import numpy as np
import jax
import jax.numpy as jnp

def _softmax(x, axis=-1):
    return jax.nn.softmax(x, axis=axis)

def _gelu(x):
    return jax.nn.gelu(x, approximate=True)

def _silu(x):
    return jax.nn.silu(x)

def _sigmoid(x):
    return jax.nn.sigmoid(x)

def _layernorm(x, axis=-1, eps=1e-05):
    m = jnp.mean(x, axis=axis, keepdims=True)
    v = jnp.var(x, axis=axis, keepdims=True)
    return (x - m) / jnp.sqrt(v + eps)

def _scatter_add(tgt, idx, src, axis=0):
    return tgt.at[idx].add(src)

def _segment_sum(src, seg, n):
    return jax.ops.segment_sum(src, seg, n)
kernel_name = 'mk_gnn_ffn_d1_gnn_r32_d83b63'

def setup_inputs(seed: int=0):
    np.random.seed(seed)
    _w = jnp.asarray

    def _rec_inputs():
        import jax
        import jax.numpy as jnp
        _gk = jax.random.key(seed)
        x = -0.0003713 + 1 * jax.random.normal(jax.random.fold_in(_gk, 1), (3125, 256), jnp.float32)
        _s = jax.random.randint(jax.random.fold_in(_gk, 2), (25000,), 0, 3125, jnp.int32)
        _d = jax.random.randint(jax.random.fold_in(_gk, 3), (25000,), 0, 3125, jnp.int32)
        _loop = jnp.arange(3125, dtype=jnp.int32)
        src = jnp.concatenate([_s, _d, _loop])
        dst = jnp.concatenate([_d, _s, _loop])
        _o = jnp.argsort(dst, stable=True)
        src = src[_o]
        dst = dst[_o]
        return (x, src, dst)
    x, src, dst = _rec_inputs()

    def _L0_gnn_setup():
        import jax, jax.numpy as jnp
        import numpy as np
        N_NODES = 50000
        N_EDGES = 25000
        D = 256
        NUM_STEPS = 6
        key = jax.random.key(seed)
        ks = jax.random.split(key, 12)
        s = 1.0 / np.sqrt(D)
        return {'node_feats': jax.random.normal(ks[0], (N_NODES, D), jnp.float32), 'W1': jax.random.normal(ks[1], (D, D), jnp.float32) * s, 'b1': jax.random.normal(ks[2], (D,), jnp.float32) * s, 'W2': jax.random.normal(ks[3], (D, D), jnp.float32) * s, 'b2': jax.random.normal(ks[4], (D,), jnp.float32) * s, 'W_ih': jax.random.normal(ks[5], (3 * D, D), jnp.float32) * s, 'b_ih': jax.random.normal(ks[6], (3 * D,), jnp.float32) * s, 'W_hh': jax.random.normal(ks[7], (3 * D, D), jnp.float32) * s, 'b_hh': jax.random.normal(ks[8], (3 * D,), jnp.float32) * s, 'src': jax.random.randint(ks[9], (N_EDGES,), 0, N_NODES, jnp.int32), 'dst': jax.random.randint(ks[10], (N_EDGES,), 0, N_NODES, jnp.int32)}
    _L0_gnn_all = _L0_gnn_setup()
    _L0_gnn_in = {k: v for k, v in _L0_gnn_all.items() if k in ('W1', 'b1', 'W2', 'b2', 'W_ih', 'b_ih', 'W_hh', 'b_hh')}
    del _L0_gnn_all

    def _L0_ffn_setup():
        import jax, jax.numpy as jnp
        import numpy as np
        D_MODEL = 256
        EXPERT_DIM = 512
        NUM_EXPERTS = 8
        TOP_K = 2
        SEQ_LEN = 64
        BATCH = 2
        key = jax.random.key(seed)
        ks = jax.random.split(key, 8)
        s = 0.02
        x = jax.random.normal(ks[0], (SEQ_LEN, BATCH, D_MODEL), dtype=jnp.float32)
        Wg = jax.random.normal(ks[1], (D_MODEL, NUM_EXPERTS), dtype=jnp.float32) * s
        bg = jax.random.normal(ks[2], (NUM_EXPERTS,), dtype=jnp.float32) * s
        bias = jnp.zeros((NUM_EXPERTS,), dtype=jnp.float32)
        W1 = jax.random.normal(ks[3], (NUM_EXPERTS, D_MODEL, EXPERT_DIM), dtype=jnp.float32) * s
        b1 = jax.random.normal(ks[4], (NUM_EXPERTS, EXPERT_DIM), dtype=jnp.float32) * s
        W2 = jax.random.normal(ks[5], (NUM_EXPERTS, EXPERT_DIM, D_MODEL), dtype=jnp.float32) * s
        b2 = jax.random.normal(ks[6], (NUM_EXPERTS, D_MODEL), dtype=jnp.float32) * s
        return {'x': x, 'Wg': Wg, 'bg': bg, 'bias': bias, 'W1': W1, 'b1': b1, 'W2': W2, 'b2': b2}
    _L0_ffn_all = _L0_ffn_setup()
    _L0_ffn_in = {k: v for k, v in _L0_ffn_all.items() if k in ('Wg', 'bg', 'bias', 'W1', 'b1', 'W2', 'b2')}
    del _L0_ffn_all
    return {'x': x, 'src': src, 'dst': dst, 'L0_gnn_W1': _L0_gnn_in['W1'], 'L0_gnn_b1': _L0_gnn_in['b1'], 'L0_gnn_W2': _L0_gnn_in['W2'], 'L0_gnn_b2': _L0_gnn_in['b2'], 'L0_gnn_W_ih': _L0_gnn_in['W_ih'], 'L0_gnn_b_ih': _L0_gnn_in['b_ih'], 'L0_gnn_W_hh': _L0_gnn_in['W_hh'], 'L0_gnn_b_hh': _L0_gnn_in['b_hh'], 'L0_ffn_Wg': _L0_ffn_in['Wg'], 'L0_ffn_bg': _L0_ffn_in['bg'], 'L0_ffn_bias': _L0_ffn_in['bias'], 'L0_ffn_W1': _L0_ffn_in['W1'], 'L0_ffn_b1': _L0_ffn_in['b1'], 'L0_ffn_W2': _L0_ffn_in['W2'], 'L0_ffn_b2': _L0_ffn_in['b2']}

def reference(x, src, dst, L0_gnn_W1, L0_gnn_b1, L0_gnn_W2, L0_gnn_b2, L0_gnn_W_ih, L0_gnn_b_ih, L0_gnn_W_hh, L0_gnn_b_hh, L0_ffn_Wg, L0_ffn_bg, L0_ffn_bias, L0_ffn_W1, L0_ffn_b1, L0_ffn_W2, L0_ffn_b2):
    import jax
    import jax.numpy as jnp

    def _L0_gnn_ref(node_feats, W1, b1, W2, b2, W_ih, b_ih, W_hh, b_hh, src, dst):
        import jax, jax.numpy as jnp
        import numpy as np
        N_NODES = 50000
        N_EDGES = 25000
        D = 256
        NUM_STEPS = 6
        n_nodes = node_feats.shape[0]
        for _ in range(NUM_STEPS):
            h = jnp.maximum(node_feats @ W1.T + b1, 0.0) @ W2.T + b2
            msg = jax.ops.segment_sum(h[src], dst, num_segments=n_nodes)
            gx = msg @ W_ih.T + b_ih
            gh = node_feats @ W_hh.T + b_hh
            xr, xz, xn = jnp.split(gx, 3, axis=-1)
            hr, hz, hn = jnp.split(gh, 3, axis=-1)
            r = jax.nn.sigmoid(xr + hr)
            z = jax.nn.sigmoid(xz + hz)
            n = jnp.tanh(xn + r * hn)
            node_feats = (1.0 - z) * n + z * node_feats
        return node_feats

    def _L0_ffn_ref(x, Wg, bg, bias, W1, b1, W2, b2):
        import jax, jax.numpy as jnp
        import numpy as np
        D_MODEL = 256
        EXPERT_DIM = 512
        NUM_EXPERTS = 8
        TOP_K = 2
        SEQ_LEN = 64
        BATCH = 2
        x_flat = x.reshape(-1, D_MODEL)
        gate_logits = x_flat @ Wg + bg + bias
        topk_vals, topk_idx = jax.lax.top_k(gate_logits, TOP_K)
        topk_w = jax.nn.softmax(topk_vals, axis=-1)
        combine = (jax.nn.one_hot(topk_idx, NUM_EXPERTS, dtype=x.dtype) * topk_w[..., None]).sum(axis=1)
        h = jax.nn.relu(jnp.einsum('td,edh->teh', x_flat, W1) + b1)
        y = jnp.einsum('teh,ehd->ted', h, W2) + b2
        out = jnp.einsum('ted,te->td', y, combine)
        return out.reshape(x.shape)
    x = x + _L0_gnn_ref(_layernorm(x, axis=-1), L0_gnn_W1, L0_gnn_b1, L0_gnn_W2, L0_gnn_b2, L0_gnn_W_ih, L0_gnn_b_ih, L0_gnn_W_hh, L0_gnn_b_hh, src, dst)
    x = x + _L0_ffn_ref(_layernorm(x, axis=-1)[None], L0_ffn_Wg, L0_ffn_bg, L0_ffn_bias, L0_ffn_W1, L0_ffn_b1, L0_ffn_W2, L0_ffn_b2)[0]
    return x

_drawn_inputs = setup_inputs


def setup_inputs(seed=0):
    import zlib

    import numpy as np

    out = dict(_drawn_inputs(seed))
    spreads = {'L0_ffn_bias': (0.0, 0.1)}
    factors = {'L0_ffn_bg': 7.317, 'L0_ffn_b1': 8.0, 'L0_ffn_b2': 6.003}
    for name, (base, spread) in spreads.items():
        noise = np.random.default_rng([zlib.crc32(name.encode()), seed]).standard_normal(out[name].shape)
        drawn = base * np.exp(spread * noise) if base else spread * noise
        out[name] = jnp.asarray(drawn.astype(out[name].dtype))
    for name, factor in factors.items():
        out[name] = (out[name] * factor).astype(out[name].dtype)
    return out
```

```python
from contextlib import ExitStack

import concourse.bass as bass
from concourse import mybir

F32 = mybir.dt.float32
F32R = mybir.dt.float32r
F16 = mybir.dt.float16
F8 = mybir.dt.float8e4
I32 = mybir.dt.int32
U16 = mybir.dt.uint16
U32 = mybir.dt.uint32
ALU = mybir.AluOpType
ACT = mybir.ActivationFunctionType
AX = mybir.AxisListType

P = 128
N = 3125
D = 256
E = 53125
STEPS = 6
DT = D // P
NT = (N + P - 1) // P
NPAD = NT * P
TAIL = N - (NT - 1) * P
G3 = 3 * D
GT = G3 // P

WIN_TILES = (4, 4, 4, 4, 3, 3, 3)
NW = len(WIN_TILES)
WIN_T0 = [sum(WIN_TILES[:w]) for w in range(NW)]
WIN_COL = [t * P for t in WIN_T0]
WIN_LEN = [n * P for n in WIN_TILES]
WIN_LEN[-1] = N + N % 2 - WIN_COL[-1]

SW = 16
NSL = (N + SW - 1) // SW
NSL += NSL % 2
ACOLS = NSL * SW
KEY = 512
NCH = (E + P - 1) // P
CG = (NCH + P - 1) // P
FIRST = 3
NCHP = NCH + 2 * FIRST
EXACT8 = 16

USES = (NT + 1) // 2
USE_WIN = [max(w for w in range(NW) if WIN_T0[w] <= min(2 * u + 1, NT - 1)) for u in range(USES)]
EARLY = max(u for u in range(USES) if USE_WIN[u] < NW - 1) + 1
FILL_A = sum(USE_WIN[u] < 3 for u in range(USES))
FILL_B = sum(USE_WIN[u] < 5 for u in range(USES))

GATE_OPS = 9
NX = 8
HID = 512
HT = HID // P
FW = 448
FN = (N + FW - 1) // FW
PIECES = 4
FP = FW // PIECES
FLAST = N - (FN - 1) * FW - (PIECES - 1) * FP
COMB_BANK = (0, 1, 2, 3, 6, 7, 5)
BLOCKS = NX * HT
CHUNKS = 2 * DT * NX
LEAD = 6


def gnn_ffn(nc, x, src, dst, W1, b1, W2, b2, W_ih, b_ih, W_hh, b_hh, Wg, bg, bias, F1, fb1, F2, fb2, out):
    stack = ExitStack()
    with stack:
        sems = {}

        def sem(name):
            if name not in sems:
                sems[name] = stack.enter_context(nc.semaphore(name))
            return sems[name]

        def allocator(scope):
            return lambda name, shape, dt: scope.enter_context(nc.sbuf_tensor(name, shape, dt))

        sb = allocator(stack)
        bank = [stack.enter_context(nc.psum_tensor(f"bank{i}", [P, 512], F32)) for i in range(8)]

        ident = sb("ident", [P, P], F32)
        x_hi = sb("x_hi", [P, DT, NPAD], F32R)
        x_lo = sb("x_lo", [P, DT, NPAD], F32R)

        gnn = ExitStack()
        gb = allocator(gnn)
        w1t = [gb(f"w1t_{p}", [P, DT, D], F32R) for p in ("hi", "lo")]
        wct = [gb(f"wct_{p}", [P, DT, G3], F32R) for p in ("hi", "lo")]
        wht = [gb(f"wht_{p}", [P, DT, G3], F32R) for p in ("hi", "lo")]
        b1_rows = gb("b1_rows", [P, D], F32R)
        ones_r = gb("ones_r", [P, P], F32R)
        gate_bias = gb("gate_bias", [P, GT], F32)
        hn_bias = gb("hn_bias", [P, DT], F32)
        deg_w = gb("deg_w", [P, GT], F32)
        degree = gb("degree", [P, ACOLS], U16)

        prep = ExitStack()
        pp = allocator(prep)
        xa = pp("xa", [P, NT, D], F32)
        w1n = pp("w1n", [P, DT, D], F32)
        w2n = pp("w2n", [P, DT, D], F32)
        win = pp("win", [P, GT, D], F32)
        whn = pp("whn", [P, GT, D], F32)
        wit = pp("wit", [P, DT, G3], F32)
        e_src = pp("e_src", [P, CG, P], I32)
        e_dst = pp("e_dst", [P, CG, P], I32)
        e_tmp = pp("e_tmp", [P, CG, P], I32)
        e_f = [pp(f"e_f{i}", [P, CG, P], F32) for i in range(3)]
        lim = pp("lim", [P, 2, CG], F32)
        diag = pp("diag", [P, 2, CG, P], F32)
        lim_b = pp("lim_b", [P, 2, CG * P], F32)
        chunk_id = pp("chunk_id", [P, CG * P], F32)
        mask = pp("mask", [P, CG * P], F32)
        prep.close()
        adj_scope = ExitStack()
        adj = allocator(adj_scope)("adj", [P, NT, ACOLS], F8)

        bs = ExitStack()
        bb = allocator(bs)
        key_t = bb("key_t", [P, NCHP], F32)
        row_t = bb("row_t", [P, NCHP], F32)
        iota_key = bb("iota_key", [P, NT * SW], F16)
        iota_row = bb("iota_row", [P, P], F16)
        slice_off = bb("slice_off", [P, NSL], F32)
        hot_key = [bb(f"hot_key{s}", [P, NT * SW], F16) for s in range(FIRST + 1)]
        hot_row = [bb(f"hot_row{s}", [P, P], F16) for s in range(FIRST + 1)]
        stage = [bb(f"stage{i}", [P, NT, SW], F8) for i in range(2)]
        trash = [bb(f"trash{i}", [P, NT * SW], F16) for i in range(2)]
        over = bb("over", [P, NSL], F32)
        bound_row = bb("bound_row", [1, 2 * 2 * P], I32)
        bound = bb("bound", [P, 2, 2], I32)
        slice_id = bb("slice_id", [P, 2], F32)
        bnd = bb("bnd", [P, 2, 2], F32)
        small = bb("small", [P, 16], F32)
        smalli = bb("smalli", [P, 16], I32)
        b1_col = bb("b1_col", [P, DT], F32)
        b2_col = bb("b2_col", [P, DT], F32)
        bih_col = bb("bih_col", [P, GT], F32)
        bhh_col = bb("bhh_col", [P, GT], F32)
        b1_diag = bb("b1_diag", [P, 2, D], F32)
        st = bb("st", [P, NT, 6], F32)
        mv = bb("mv", [P, NT, 2], F32)
        rstd = bb("rstd", [P, NT], F32)
        expo = bb("expo", [P, NT], F32)
        ones_h = bb("ones_h", [P, P], F16)
        ones_f = bb("ones_f", [P, P], F32)
        over_bias = bb("over_bias", [P, 1], F32)
        bs.close()

        steps = ExitStack()
        ss = allocator(steps)
        r_hi = ss("r_hi", [P, NT, D], F16)
        r_lo = ss("r_lo", [P, NT, D], F16)
        m_hi = ss("m_hi", [P, DT, 512], F32R)
        m_lo = ss("m_lo", [P, DT, 512], F32R)
        gate_a = ss("gate_a", [P, 512], F32)
        gate_z = ss("gate_z", [P, 512], F32)
        x_new = ss("x_new", [P, DT, 512], F32)
        steps.close()
        adj_scope.close()
        gnn.close()

        ffn = ExitStack()
        fb = allocator(ffn)
        f1w = [fb(f"f1w_{p}", [P, DT, NX, HID], F32R) for p in ("hi", "lo")]
        f2w = [fb(f"f2w_{p}", [P, HT, NX, D], F32R) for p in ("hi", "lo")]
        ident_r = fb("ident_r", [P, P], F32R)
        hid_bias = fb("hid_bias", [P, BLOCKS], F32)
        out_bias = fb("out_bias", [NX, D], F32)
        norm2 = ExitStack()
        nb = allocator(norm2)
        x1 = nb("x1", [P, NT, D], F32)
        st2 = nb("st2", [P, NT, 6], F32)
        mv2 = nb("mv2", [P, NT, 2], F32)
        rstd2 = nb("rstd2", [P, NT], F32)
        expo2 = nb("expo2", [P, NT], F32)
        norm2.close()
        gate = ExitStack()
        tb = allocator(gate)
        wg = tb("wg", [P, DT, NX], F32)
        wg_r = [tb(f"wg_{p}", [P, DT, NX], F32R) for p in ("hi", "lo")]
        bg_b = tb("bg_b", [P, 2, NX], F32)
        eid = tb("eid", [P, NT, NX], F32)
        logit = tb("logit", [P, NT, NX], F32)
        cand = tb("cand", [P, NT, NX], F32)
        hot1 = tb("hot1", [P, NT, NX], F32)
        hot2 = tb("hot2", [P, NT, NX], F32)
        top = tb("top", [P, 6, NT], F32)
        comb_t = tb("comb_t", [NX, NPAD], F32)
        hid_bias_rows = tb("hid_bias_rows", [BLOCKS, P], F32)
        raw = [tb(f"raw{i}", [P, HID], F32) for i in range(4)]
        gate.close()
        hb_ = ExitStack()
        hb = allocator(hb_)
        act_h = [hb(f"act_h{i}", [P, FW], F32) for i in range(2)]
        h_hi = [hb(f"h_hi{i}", [P, FW], F32R) for i in range(2)]
        h_lo = [hb(f"h_lo{i}", [P, FW], F32R) for i in range(2)]
        comb_b = [hb(f"comb_b{i}", [P, FW], F32) for i in range(4)]
        comb_w = hb("comb_w", [NX, FW], F32)
        y_t = hb("y_t", [P, DT, FW], F32)
        y_rows = hb("y_rows", [FP, PIECES, D], F32)
        hb_.close()
        ffn.close()

        x1_dram = nc.dram_tensor("x1_scratch", (NPAD, D), F32, kind="Internal").ap()
        comb_dram = nc.dram_tensor("comb_scratch", (NX, NPAD), F32, kind="Internal").ap()
        bound_dram = nc.dram_tensor("bound_scratch", (2 * P, 2), I32, kind="Internal").ap()
        inputs = sem("inputs")
        block = stack.enter_context(nc.Block())

        def half(s, w, f):
            return s * (2 * NW) + 2 * w + f

        @block.sync
        def _(sp):
            sp.wait_ge(sem("edges_clear"), 2)
            full = (NCH - 1) // P * P
            rest = E // P - full
            for buf, inp in ((e_src, src), (e_dst, dst)):
                sp.dma_start(buf[:, 0:full // P, :], inp[0:full * P].rearrange("(g p e) -> p g e", p=P, e=P)).then_inc(sem("edges"), 16)
                sp.dma_start(buf[0:rest, full // P, :], inp[full * P:(full + rest) * P].rearrange("(p e) -> p e", e=P)).then_inc(sem("edges"), 16)
            last = E - (full + rest) * P
            sp.dma_start(e_src[rest:rest + 1, full // P, P - last:P], src[E - last:E].rearrange("(a e) -> a e", a=1)).then_inc(sem("edges"), 16)
            sp.dma_start(e_dst[rest:rest + 1, full // P, :], dst[E - P:E].rearrange("(a e) -> a e", a=1)).then_inc(sem("edges"), 16)
            sp.dma_start(w1n[:], W1.rearrange("(t p) i -> p t i", p=P)).then_inc(inputs, 16)
            sp.dma_start(w2n[:], W2.rearrange("(t p) i -> p t i", p=P)).then_inc(inputs, 16)
            sp.dma_start(win[:], W_ih.rearrange("(t p) i -> p t i", p=P)).then_inc(inputs, 16)
            sp.dma_start(whn[:], W_hh.rearrange("(t p) i -> p t i", p=P)).then_inc(inputs, 16)
            for buf, inp in ((b1_col, b1), (b2_col, b2), (bih_col, b_ih), (bhh_col, b_hh)):
                sp.dma_start(buf[:], inp.rearrange("(t p) -> p t", p=P), allow_slow_non_contiguous=True).then_inc(inputs, 16)
            sp.wait_ge(sem("xa_clear"), 1)
            sp.dma_start(xa[:, 0:NT - 1, :], x[0:(NT - 1) * P, :].rearrange("(t p) d -> p t d", p=P)).then_inc(sem("x_in"), 16)
            sp.dma_start(xa[0:TAIL, NT - 1, :], x[(NT - 1) * P:N, :]).then_inc(sem("x_in"), 16)
            sp.wait_ge(sem("bound_col"), 1)
            sp.dma_start(bound_dram.rearrange("(t p) b -> p t b", p=P), bound[:]).then_inc(sem("bound_out"), 16)
            sp.wait_ge(sem("bound_out"), 16)
            sp.dma_start(bound_row[:], bound_dram.rearrange("(a p) b -> a (p b)", a=1)).then_inc(sem("bound_in"), 16)
            sp.wait_ge(sem("x1_clear"), 1)
            sp.dma_start(x1[:, 0:NT - 1, :], x[0:(NT - 1) * P, :].rearrange("(t p) d -> p t d", p=P)).then_inc(sem("x_again"), 16)
            sp.dma_start(x1[0:TAIL, NT - 1, :], x[(NT - 1) * P:N, :]).then_inc(sem("x_again"), 16)
            sp.dma_start(out_bias[:], fb2[:]).then_inc(sem("out_bias_in"), 16)
            sp.wait_ge(sem("x1_sum"), USES)
            sp.dma_start(x1_dram.rearrange("(t p) d -> p t d", p=P), x1[:]).then_inc(sem("x1_out"), 16)
            sp.wait_ge(sem("x2t"), USES)
            sp.dma_start(wg[:], Wg.rearrange("(t p) e -> p t e", p=P)).then_inc(sem("gate_in"), 16)
            sp.dma_start(bg_b[:, 0, :], bg.rearrange("(a e) -> a e", a=1).broadcast_to([P, NX])).then_inc(sem("gate_in"), 16)
            sp.dma_start(bg_b[:, 1, :], bias.rearrange("(a e) -> a e", a=1).broadcast_to([P, NX])).then_inc(sem("gate_in"), 16)
            sp.dma_start(hid_bias_rows[:], fb1.rearrange("e (t p) -> (e t) p", p=P)).then_inc(sem("gate_in"), 16)
            for c in range(CHUNKS):
                e, k = c // 4, c % 4
                if c >= 4:
                    sp.wait_ge(sem("chunk_lo"), c - 3)
                if c == CHUNKS // 2:
                    sp.wait_ge(sem("comb_sb"), 1)
                    sp.dma_start(comb_dram[:], comb_t[:]).then_inc(sem("comb_out"), 16)
                if k < DT:
                    sp.dma_start(raw[c % 4][:], F1[e, k * P:(k + 1) * P, :]).then_inc(sem(f"chunk_in{c % 4}"), 16)
                else:
                    h0 = (k - DT) * 2 * P
                    sp.dma_start(raw[c % 4][:].rearrange("p (t d) -> p t d", t=2),
                                 F2[e, h0:h0 + 2 * P, :].rearrange("(t p) d -> p t d", p=P)).then_inc(sem(f"chunk_in{c % 4}"), 16)
            sp.wait_ge(sem("chunk_lo"), CHUNKS)
            sp.wait_ge(sem("comb_out"), 16)

            def load_comb(e, c0):
                sp.dma_start(comb_b[e % 4][:], comb_dram[e:e + 1, bass.ds(c0, FW)].broadcast_to([P, FW]))\
                  .then_inc(sem(f"comb_in{e % 4}"), 16)

            for e in range(4):
                load_comb(e, 0)

            def load_rows(w):
                sp.dma_start(comb_w[:], comb_dram[:, bass.ds(w * FW, FW)]).then_inc(sem("comb_w_in"), 16)
                sp.dma_start(y_rows[:], x1_dram[bass.ds(w * FW, FW), :].rearrange("(j p) d -> p j d", p=FP)).then_inc(sem("x1_in"), 16)

            def feed(w, experts):
                for e in experts:
                    sp.wait_ge(sem("h_scaled"), BLOCKS * w + HT * (e + 1))
                    n = e + 4
                    load_comb(n % NX, (w + n // NX) * FW)
                sp.wait_ge(sem("y_ready"), (PIECES // 2) * (w + 1))

            load_rows(0)
            with sp.Fori(0, FN - 1) as w:
                feed(w, range(NX))
                sp.dma_start(out[bass.ds(w * FW, FW), :].rearrange("(j p) d -> p j d", p=FP), y_rows[:]).then_inc(sem("y_stored"), 16)
                sp.wait_ge(sem("y_stored"), 16 * (w + 1))
                load_rows(w + 1)
            feed(FN - 1, range(NX - 4))
            r0 = (FN - 1) * FW
            r1 = r0 + (PIECES - 1) * FP
            sp.dma_start(out[r0:r1, :].rearrange("(j p) d -> p j d", p=FP), y_rows[:, 0:PIECES - 1, :]).then_inc(sem("y_stored"), 16)
            sp.dma_start(out[r1:N, :], y_rows[0:FLAST, PIECES - 1, :]).then_inc(sem("y_stored"), 16)
            sp.wait_ge(sem("y_stored"), 16 * (FN + 1))

        INPUTS = 16 * 8

        @block.gpsimd
        def _(pool):
            pool.memset(ones_f[:], 1.0).then_inc(sem("ones_ready"), 1)
            pool.memset(e_src[:], -1).then_inc(sem("edges_clear"), 1)
            pool.memset(e_dst[:], 0).then_inc(sem("edges_clear"), 1)
            pool.memset(xa[:, NT - 1, :], 0.0).then_inc(sem("xa_clear"), 1)
            pool.memset(ident[:], 0.0).then_inc(sem("p0"), 1)
            pool.wait_ge(sem("p0"), 1)
            pool.affine_select(out=ident[:], in_=ident[:], compare_op=ALU.not_equal, fill=1.0, base=0,
                               pattern=[[-1, P]], channel_multiplier=1).then_inc(sem("ident_ready"), 1)
            pool.iota(chunk_id[:], [[1, CG * P]], base=0, channel_multiplier=0, allow_small_or_imprecise_dtypes=True).then_inc(sem("iotas"), 1)
            pool.iota(slice_id[:], [[P, 2]], base=0, channel_multiplier=1, allow_small_or_imprecise_dtypes=True).then_inc(sem("iotas"), 1)
            pool.iota(iota_key[:], [[1, NT * SW]], base=0, channel_multiplier=0, allow_small_or_imprecise_dtypes=True).then_inc(sem("iotas"), 1)
            pool.iota(iota_row[:], [[1, P]], base=0, channel_multiplier=0, allow_small_or_imprecise_dtypes=True).then_inc(sem("iotas"), 1)
            pool.iota(slice_off[:], [[KEY, NSL]], base=0, channel_multiplier=0, allow_small_or_imprecise_dtypes=True).then_inc(sem("iotas"), 1)
            pool.memset(over_bias[:], -float(EXACT8)).then_inc(sem("stage_free"), 2)
            pool.memset(expo[:], -0.5).then_inc(sem("p0"), 1)
            pool.wait_ge(sem("p0"), 2)
            pool.wait_ge(sem("var_ready"), 1)
            pool.tensor_tensor(rstd[:], rstd[:], expo[:], ALU.pow).then_inc(sem("rstd_ready"), 1)
            with pool.Fori(0, NSL // 2) as i:
                for b in range(2):
                    pool.wait_ge(sem("stage_full"), 2 * i + (b + 3))
                    pool.tensor_copy(adj[:].bitcast(U32)[:, :, bass.ds(i * (2 * SW // 4) + b * SW // 4, SW // 4)],
                                     stage[b][:].bitcast(U32)).then_inc(sem("stage_free"), 1)
            pool.wait_ge(sem("state_lo"), NW * (STEPS + 1))
            pool.memset(x1[:, NT - 1, :], 0.0).then_inc(sem("x1_clear"), 1)
            pool.memset(expo2[:], -0.5).then_inc(sem("p0"), 1)
            pool.wait_ge(sem("p0"), 3)
            pool.wait_ge(sem("var_ready"), 2)
            pool.tensor_tensor(rstd2[:], rstd2[:], expo2[:], ALU.pow).then_inc(sem("rstd_ready"), 1)
            pool.wait_ge(sem("x2t"), USES)
            pool.iota(eid[:], [[0, NT], [1, NX]], base=0, channel_multiplier=0, allow_small_or_imprecise_dtypes=True).then_inc(sem("iotas"), 1)

        def chunk_dst(c):
            e, k = c // 4, c % 4
            if k < DT:
                return [w[:, k, e, :] for w in f1w]
            return [w[:, 2 * (k - DT):2 * (k - DT) + 2, e, :] for w in f2w]

        @block.vector
        def _(dve):
            chain = [0]

            def link(ins):
                chain[0] += 1
                ins.then_inc(sem("dve_prep"), 1)
                dve.wait_ge(sem("dve_prep"), chain[0])

            v = nc.vector
            dve.wait_ge(sem("edges"), 16 * 6)
            link(v.tensor_scalar(e_tmp[:], e_dst[:], -SW, (KEY // SW).bit_length() - 1, ALU.bitwise_and, ALU.arith_shift_left))
            link(v.scalar_tensor_tensor(e_tmp[:], e_dst[:], SW - 1, e_tmp[:], ALU.bitwise_and, ALU.bitwise_or))
            link(v.tensor_copy(e_f[2][:], e_dst[:]))
            link(v.tensor_scalar(e_dst[:], e_src[:], 127, None, ALU.bitwise_and))
            link(v.tensor_copy(e_f[1][:], e_dst[:]))
            link(v.tensor_scalar(e_src[:], e_src[:], -P, (P // SW).bit_length() - 1, ALU.bitwise_and, ALU.arith_shift_right))
            link(v.tensor_tensor(e_tmp[:], e_tmp[:], e_src[:], ALU.bitwise_or))
            v.tensor_copy(e_f[0][:], e_tmp[:]).then_inc(sem("keys"), 1)
            v.tensor_reduce(lim[:, 0, :], e_f[2][:], AX.X, ALU.min).then_inc(sem("lims"), 1)
            v.tensor_reduce(lim[:, 1, :], e_f[2][:], AX.X, ALU.max).then_inc(sem("lims"), 1)
            dve.wait_ge(sem("lims"), 2)
            dve.wait_ge(sem("ident_ready"), 1)
            for m in range(2):
                for g in range(CG):
                    last = v.tensor_scalar(diag[:, m, g, :], ident[:], lim[:, m, g:g + 1], None, ALU.mult)
            last.then_inc(sem("diags"), 1)
            v.memset(key_t[:], -1.0)
            v.memset(row_t[:], 0.0).then_inc(sem("dve_prep"), 1)
            chain[0] += 1
            dve.wait_ge(sem("dve_prep"), chain[0])
            dve.wait_ge(sem("keys_t"), 1)
            v.tensor_copy(key_t[:, 0:NCH], bank[0][:, 0:NCH])
            v.tensor_copy(row_t[:, 0:NCH], bank[1][:, 0:NCH]).then_inc(sem("edge_table"), 1)
            dve.wait_ge(sem("lims_b"), 1)
            v.tensor_copy(lim_b[:, 0, :], bank[2][:])
            link(v.tensor_copy(lim_b[:, 1, :], bank[3][:]))
            dve.wait_ge(sem("iotas"), 5)
            for t in range(2):
                link(v.tensor_scalar(small[:, 0:1], slice_id[:, t:t + 1], float(SW), float(SW - 1), ALU.mult, ALU.add))
                link(v.tensor_scalar(small[:, 1:2], slice_id[:, t:t + 1], float(SW), None, ALU.mult))
                link(v.tensor_scalar(mask[:, 0:NCH], lim_b[:, 0, 0:NCH], small[:, 0:1], None, ALU.is_le))
                link(v.scalar_tensor_tensor(mask[:, 0:NCH], lim_b[:, 1, 0:NCH], small[:, 1:2], mask[:, 0:NCH], ALU.is_ge, ALU.mult))
                link(v.scalar_tensor_tensor(e_f[2][:].rearrange("p g e -> p (g e)")[:, 0:NCH], chunk_id[:, 0:NCH], float(-NCH), mask[:, 0:NCH], ALU.add, ALU.mult))
                link(v.tensor_reduce(small[:, 2:3], e_f[2][:].rearrange("p g e -> p (g e)")[:, 0:NCH], AX.X, ALU.min))
                link(v.scalar_tensor_tensor(e_f[2][:].rearrange("p g e -> p (g e)")[:, 0:NCH], chunk_id[:, 0:NCH], 1.0, mask[:, 0:NCH], ALU.add, ALU.mult))
                link(v.tensor_reduce(bnd[:, t, 1:2], e_f[2][:].rearrange("p g e -> p (g e)")[:, 0:NCH], AX.X, ALU.max))
                link(v.tensor_scalar(bnd[:, t, 0:1], small[:, 2:3], float(NCH), None, ALU.add))
            v.tensor_copy(bound[:], bnd[:]).then_inc(sem("bound_col"), 1)

            dve.wait_ge(sem("x_in"), 32)
            for t in range(NT):
                last = v.bn_stats(st[:, t, :], xa[:, t, :])
            link(last)
            for t in range(NT):
                last = v.bn_aggr(mv[:, t, :], st[:, t, :])
            link(last)
            v.tensor_scalar(rstd[:], mv[:, :, 1], 1e-5, None, ALU.add).then_inc(sem("var_ready"), 1)

            dve.wait_ge(inputs, INPUTS)
            for t in range(DT):
                link(v.tensor_reduce(small[:, t:t + 1], w1n[:, t, :], AX.X, ALU.add, apply_absolute_value=True))
            link(v.tensor_reduce(small[:, 2:4], b1_col[:].rearrange("p (t a) -> p t a", a=1), AX.X, ALU.add, apply_absolute_value=True))
            link(v.scalar_tensor_tensor(small[:, 4:6], small[:, 0:2], 16.0, small[:, 2:4], ALU.mult, ALU.add))
            link(v.tensor_scalar(smalli[:, 0:2], small[:, 4:6].bitcast(I32), 0xFF << 23, None, ALU.bitwise_and))
            link(v.tensor_scalar(smalli[:, 0:2], smalli[:, 0:2], float(20 << 23), None, ALU.max))
            link(v.tensor_scalar(smalli[:, 2:4], smalli[:, 0:2], -1.0, float(268 << 23), ALU.mult, ALU.add))
            link(v.tensor_scalar(smalli[:, 4:6], smalli[:, 0:2], float(-(14 << 23)), None, ALU.add))
            sc = smalli[:].bitcast(F32)
            for t in range(DT):
                link(v.tensor_scalar(w1n[:, t, :], w1n[:, t, :], sc[:, 2 + t:3 + t], None, ALU.mult))
                link(v.tensor_scalar(small[:, 6 + t:7 + t], b1_col[:, t:t + 1], sc[:, 2 + t:3 + t], None, ALU.mult))
            for t in range(DT):
                for h in range(DT):
                    if h == t:
                        link(v.tensor_scalar(b1_diag[:, t, h * P:(h + 1) * P], ident[:], small[:, 6 + t:7 + t], None, ALU.mult))
                    else:
                        link(v.memset(b1_diag[:, t, h * P:(h + 1) * P], 0.0))
            link(v.memset(ones_h[:], 1.0))
            link(v.tensor_copy(ones_r[:], ones_h[:]))
            v.memset(b1_rows[:].bitcast(F32), 0.0).then_inc(sem("w1_scaled"), 1)
            v.tensor_tensor(gate_bias[:, 0:4], bih_col[:, 0:4], bhh_col[:, 0:4], ALU.add)
            v.tensor_copy(gate_bias[:, 4:6], bih_col[:, 4:6])
            v.tensor_copy(hn_bias[:], bhh_col[:, 4:6])

            dve.wait_ge(sem("rstd_ready"), 1)
            for t in range(NT):
                v.tensor_scalar(xa[:, t, :], xa[:, t, :], mv[:, t, 0:1], rstd[:, t:t + 1], ALU.subtract, ALU.mult)\
                 .then_inc(sem("x_norm"), 1)

            dve.wait_ge(sem("w_hi"), 1)
            v.tensor_tensor(w1t[1][:], bank[4][:].rearrange("p (t j) -> p t j", t=DT), w1t[0][:].bitcast(F32), ALU.subtract).then_inc(sem("w_lo"), 1)
            dve.wait_ge(sem("w_tr"), 2)
            v.tensor_copy(b1_rows[0:1, :], bank[5][0:1, 0:D])
            link(v.tensor_copy(b1_rows[32:33, :], bank[5][32:33, 0:D]))
            v.tensor_tensor(b1_rows[32:33, :], bank[5][32:33, 0:D], b1_rows[32:33, :].bitcast(F32), ALU.subtract).then_inc(sem("b1_done"), 1)
            for j in range(4):
                t, c = j // 2, j % 2
                dve.wait_ge(sem("w_tr"), 3 + j)
                v.tensor_copy(wit[:, t, c * 384:(c + 1) * 384], bank[6 + j % 2][:, 0:384]).then_inc(sem("wit_ready"), 1)
            for j in range(4):
                t, c = j // 2, j % 2
                dve.wait_ge(sem("w_hi"), 2 + j)
                v.tensor_tensor(wht[1][:, t, c * 384:(c + 1) * 384], bank[j % 2][:, 0:384],
                                wht[0][:, t, c * 384:(c + 1) * 384].bitcast(F32), ALU.subtract).then_inc(sem("w_lo"), 1)
            dve.wait_ge(sem("w_tr"), 11)
            v.tensor_copy(deg_w[:], bank[2][:, 0:GT])
            for j in range(4):
                t, c = j // 2, j % 2
                dve.wait_ge(sem("w_tr"), 12 + j)
                if j:
                    dve.wait_ge(sem("w_lo"), 5 + j)
                ins = v.tensor_scalar(e_f[0][:].rearrange("p g e -> p (g e)")[:, 0:384], bank[4 + j % 2][:, 0:384], sc[:, 4 + t:5 + t], None, ALU.mult)
                ins.then_inc(sem("wc_scaled"), 1)
                dve.wait_ge(sem("w_hi"), 6 + j)
                v.tensor_tensor(wct[1][:, t, c * 384:(c + 1) * 384], e_f[0][:].rearrange("p g e -> p (g e)")[:, 0:384],
                                wct[0][:, t, c * 384:(c + 1) * 384].bitcast(F32), ALU.subtract).then_inc(sem("w_lo"), 1)
            for u in range(USES):
                m = min(2, NT - 2 * u) * P
                dve.wait_ge(sem("xt_hi"), u + 1)
                ins = v.tensor_tensor(x_lo[:, :, 2 * P * u:2 * P * u + m],
                                      bank[6 + u % 2][:, 0:DT * m].rearrange("p (t n) -> p t n", t=DT),
                                      x_hi[:, :, 2 * P * u:2 * P * u + m].bitcast(F32), ALU.subtract)
                ins.then_inc(*((sem("xt_lo"), 1) if u < USES - 1 else (sem("state_lo"), NW)))

            dve.wait_ge(sem("bound_in"), 16)
            extra = dve.alloc_register("dve_extra")
            dve.reg_mov(extra, 0)

            def hot(slot, c, sl):
                v.tensor_scalar(hot_row[slot][:], iota_row[:], row_t[:, bass.ds(c, 1)], None, ALU.is_equal)
                return v.tensor_scalar(hot_key[slot][:], iota_key[:], slice_off[:, bass.ds(sl, 1)], key_t[:, bass.ds(c, 1)],
                                       ALU.add, ALU.is_equal)

            dve.wait_ge(sem("edge_table"), 1)
            with dve.Fori(0, NSL) as sl:
                first = dve.value_load(bound_row[0:1, bass.ds(2 * sl, 1)], min_val=0, max_val=NCH)
                end = dve.value_load(bound_row[0:1, bass.ds(2 * sl + 1, 1)], min_val=0, max_val=NCH)
                for s in range(FIRST):
                    dve.wait_ge(sem(f"hot_free{s}"), sl + 1)
                    hot(s, first + s, sl).then_inc(sem(f"hot_full{s}"), 1)
                with dve.If(end > first + FIRST):
                    with dve.Fori(first + FIRST, end) as c:
                        dve.wait_ge(sem(f"hot_free{FIRST}"), dve.snap(extra) + 1)
                        hot(FIRST, c, sl).then_inc(sem(f"hot_full{FIRST}"), 1)
                        dve.reg_add(extra, extra, 1)

            for w in range(NW):
                dve.wait_ge(sem("deg_sum"), w + 1)
                v.tensor_copy(degree[:, WIN_COL[w]:WIN_COL[w] + WIN_LEN[w]], bank[4 + w % 4][:, 0:WIN_LEN[w]]).then_inc(sem("deg_done"), 1)

            v.memset(x_new[:, 0, 0:2], 0.0).then_inc(sem("gate_ops"), LEAD)
            dve.wait_ge(sem("deg_done"), NW)
            dve.wait_ge(sem("gate_ops"), LEAD)

            def relu_lo(g, u):
                m = min(2, NT - 2 * u)
                dve.wait_ge(sem("relu_hi"), g + 1)
                v.scalar_tensor_tensor(r_lo[:, 2 * u:2 * u + m, :].rearrange("p t d -> p (t d)"), bank[2 + u % 2][:, 0:m * D], 0.0,
                                       r_hi[:, 2 * u:2 * u + m, :].rearrange("p t d -> p (t d)"), ALU.max, ALU.subtract)\
                 .then_inc(sem("relu_lo"), 1)

            def msg_lo(s, w):
                for f in range(DT):
                    n = WIN_LEN[w]
                    dve.wait_ge(sem("msg_hi"), half(s, w, f) + 1)
                    v.tensor_tensor(m_lo[:, f, 0:n], bank[2 * (w % 2) + f][:, 0:n], m_hi[:, f, 0:n].bitcast(F32), ALU.subtract)\
                     .then_inc(sem("msg_lo"), 1)

            def gates(s, w, f):
                n, c0 = WIN_LEN[w], WIN_COL[w]
                h = dve.snap(half(s, w, f)) if not isinstance(s, int) else half(s, w, f)
                mine = h * GATE_OPS + LEAD
                mine = dve.snap(mine) if not isinstance(s, int) else mine
                theirs = h * 3
                full = h * 4
                dg = degree[:, c0:c0 + n]
                a, z, xn = gate_a[:, 0:n], gate_z[:, 0:n], x_new[:, f, 0:n]

                def op(ins):
                    ins.then_inc(sem("gate_ops"), 1)

                dve.wait_ge(sem("gate_ops"), mine)
                dve.wait_ge(sem("gate_sums"), full + 1)
                op(v.scalar_tensor_tensor(a, dg, deg_w[:, f:f + 1], bank[4][:, 0:n], ALU.mult, ALU.add))
                dve.wait_ge(sem("gate_sums"), full + 2)
                op(v.scalar_tensor_tensor(z, dg, deg_w[:, 2 + f:3 + f], bank[5][:, 0:n], ALU.mult, ALU.add))
                dve.wait_ge(sem("gate_sums"), full + 3)
                dve.wait_ge(sem("gate_acts"), theirs + 1)
                op(v.scalar_tensor_tensor(a, bank[6][:, 0:n], hn_bias[:, f:f + 1], a, ALU.add, ALU.mult))
                dve.wait_ge(sem("gate_sums"), full + 4)
                dve.wait_ge(sem("gate_ops"), mine + 3)
                op(v.tensor_tensor(a, bank[7][:, 0:n], a, ALU.add))
                dve.wait_ge(sem("gate_ops"), mine + 4)
                op(v.scalar_tensor_tensor(a, dg, deg_w[:, 4 + f:5 + f], a, ALU.mult, ALU.add))
                dve.wait_ge(sem("gate_acts"), theirs + 3)
                op(v.tensor_tensor(xn, x_hi[:, f, c0:c0 + n].bitcast(F32), a, ALU.subtract))
                dve.wait_ge(sem("gate_ops"), mine + 6)
                op(v.tensor_tensor(xn, xn, x_lo[:, f, c0:c0 + n].bitcast(F32), ALU.add))
                dve.wait_ge(sem("gate_ops"), mine + 7)
                op(v.tensor_tensor(xn, xn, z, ALU.mult))
                dve.wait_ge(sem("gate_ops"), mine + 8)
                op(v.tensor_tensor(xn, xn, a, ALU.add))

            def state_lo(s, w):
                n, c0 = WIN_LEN[w], WIN_COL[w]
                dve.wait_ge(sem("state_hi"), NW * s + w + 1)
                v.tensor_tensor(x_lo[:, :, c0:c0 + n], x_new[:, :, 0:n], x_hi[:, :, c0:c0 + n].bitcast(F32), ALU.subtract)\
                 .then_inc(sem("state_lo"), 1)

            for u in range(FILL_B):
                relu_lo(u, u)
            with dve.Fori(0, STEPS) as s:
                for u in range(FILL_B, USES):
                    relu_lo(USES * s + u, u)
                msg_lo(s, 0)
                for w in range(1, NW):
                    gates(s, w - 1, 0)
                    msg_lo(s, w)
                    gates(s, w - 1, 1)
                    state_lo(s, w - 1)
                for u in range(FILL_A):
                    relu_lo(USES * s + USES + u, u)
                gates(s, NW - 1, 0)
                for u in range(FILL_A, FILL_B):
                    relu_lo(USES * s + USES + u, u)
                gates(s, NW - 1, 1)
                state_lo(s, NW - 1)

            dve.wait_ge(sem("state_lo"), NW * (STEPS + 1))
            dve.wait_ge(sem("relu_lo"), USES * STEPS + FILL_B)
            link(v.tensor_copy(ident_r[:], ident[:]))
            v.tensor_copy(ident_r[:], ident[:]).then_inc(sem("ident_r"), 1)
            dve.wait_ge(sem("x_again"), 32)
            for u in range(USES):
                m = min(2, NT - 2 * u)
                dve.wait_ge(sem("rows"), u + 1)
                xs = x1[:, 2 * u:2 * u + m, :].rearrange("p t d -> p (t d)")
                v.tensor_tensor(xs, xs, bank[u % 2][:, 0:m * D], ALU.add).then_inc(sem("x1_sum"), 1)
            dve.wait_ge(sem("x1_sum"), USES)
            for t in range(NT):
                last = v.bn_stats(st2[:, t, :], x1[:, t, :])
            link(last)
            for t in range(NT):
                last = v.bn_aggr(mv2[:, t, :], st2[:, t, :])
            link(last)
            v.tensor_scalar(rstd2[:], mv2[:, :, 1], 1e-5, None, ALU.add).then_inc(sem("var_ready"), 1)
            dve.wait_ge(sem("rstd_ready"), 2)
            dve.wait_ge(sem("x1_out"), 16)
            for t in range(NT):
                v.tensor_scalar(x1[:, t, :], x1[:, t, :], mv2[:, t, 0:1], rstd2[:, t:t + 1], ALU.subtract, ALU.mult)\
                 .then_inc(sem("x1_norm"), 1)
            for u in range(USES):
                m = min(2, NT - 2 * u) * P
                dve.wait_ge(sem("x2t_hi"), u + 1)
                v.tensor_tensor(x_lo[:, :, 2 * P * u:2 * P * u + m],
                                bank[2 + u % 2][:, 0:DT * m].rearrange("p (t n) -> p t n", t=DT),
                                x_hi[:, :, 2 * P * u:2 * P * u + m].bitcast(F32), ALU.subtract).then_inc(sem("x2t_lo"), 1)
            dve.wait_ge(sem("gate_in"), 64)
            dve.wait_ge(sem("x2t_lo"), USES)
            link(v.tensor_copy(wg_r[0][:], wg[:]))
            v.tensor_tensor(wg_r[1][:], wg[:], wg_r[0][:].bitcast(F32), ALU.subtract).then_inc(sem("wg_split"), 1)
            dve.wait_ge(sem("hid_bias_t"), 1)
            link(v.tensor_copy(hid_bias[:], bank[5][:, 0:BLOCKS]))
            dve.wait_ge(sem("logits"), 1)
            dve.wait_ge(sem("iotas"), 6)
            lg = bank[4][:, 0:NT * NX].rearrange("p (t e) -> p t e", e=NX)

            def over_tiles(row):
                return row[:].rearrange("p (a e) -> p a e", a=1).broadcast_to([P, NT, NX])

            def over_experts(k):
                return top[:, k, :].rearrange("p (t a) -> p t a", a=1).broadcast_to([P, NT, NX])

            link(v.tensor_tensor(logit[:], lg, bg_b[:, 0:1, :].broadcast_to([P, NT, NX]), ALU.add))
            link(v.tensor_tensor(logit[:], logit[:], bg_b[:, 1:2, :].broadcast_to([P, NT, NX]), ALU.add))
            for k, hot_k in enumerate((hot1, hot2)):
                link(v.tensor_reduce(top[:, k, :], logit[:], AX.X, ALU.max))
                link(v.tensor_tensor(cand[:], logit[:], over_experts(k), ALU.is_equal))
                link(v.tensor_scalar(cand[:], cand[:], float(-NX), float(NX), ALU.mult, ALU.add))
                link(v.tensor_tensor(cand[:], cand[:], eid[:], ALU.add))
                link(v.tensor_reduce(top[:, 4, :], cand[:], AX.X, ALU.min))
                link(v.tensor_tensor(hot_k[:], eid[:], over_experts(4), ALU.is_equal))
                if k == 0:
                    link(v.tensor_scalar(cand[:], hot_k[:], -3.0e38, None, ALU.mult))
                    link(v.tensor_tensor(logit[:], logit[:], cand[:], ALU.add))
            v.tensor_tensor(top[:, 2, :], top[:, 1, :], top[:, 0, :], ALU.subtract).then_inc(sem("top_diff"), 1)
            dve.wait_ge(sem("top_exp"), 1)
            link(v.tensor_scalar(top[:, 3, :], top[:, 2, :], 1.0, None, ALU.add))
            link(v.reciprocal(top[:, 4, :], top[:, 3, :]))
            link(v.tensor_tensor(top[:, 5, :], top[:, 2, :], top[:, 4, :], ALU.mult))
            link(v.tensor_tensor(hot1[:], hot1[:], over_experts(4), ALU.mult))
            link(v.tensor_tensor(hot2[:], hot2[:], over_experts(5), ALU.mult))
            v.tensor_tensor(hot1[:], hot1[:], hot2[:], ALU.add).then_inc(sem("combine"), 1)
            for c in range(CHUNKS):
                dve.wait_ge(sem("chunk_hi"), c + 1)
                hi, lo = chunk_dst(c)
                src_ = raw[c % 4][:] if c % 4 < DT else raw[c % 4][:].rearrange("p (t d) -> p t d", t=2)
                v.tensor_tensor(lo, src_, hi.bitcast(F32), ALU.subtract).then_inc(sem("chunk_lo"), 1)
                if c == 3:
                    dve.wait_ge(sem("comb_tr"), (NT + 3) // 4)
                    for g in range((NT + 3) // 4):
                        n = min(4, NT - 4 * g) * P
                        c0 = 0 if g < 6 else P
                        last = v.tensor_copy(comb_t[:, g * 512:g * 512 + n], bank[COMB_BANK[g]][0:NX, c0:c0 + n])
                    last.then_inc(sem("comb_sb"), 1)

            dve.wait_ge(sem("chunk_lo"), CHUNKS)
            dve.wait_ge(sem("comb_out"), 16)
            with dve.Fori(0, FN) as w:
                for i in range(BLOCKS):
                    n = BLOCKS * w + i
                    b, e = i % 2, i // HT
                    if i % HT == 0:
                        dve.wait_ge(sem(f"comb_in{e % 4}"), 32 * w + 16 * (e // 4 + 1))
                    dve.wait_ge(sem("h_relu"), n + 1)
                    v.tensor_tensor(act_h[b][:], act_h[b][:], comb_b[e % 4][:], ALU.mult).then_inc(sem("h_scaled"), 1)
                    dve.wait_ge(sem("h_hi"), n + 1)
                    v.tensor_tensor(h_lo[b][:], act_h[b][:], h_hi[b][:].bitcast(F32), ALU.subtract).then_inc(sem("h_lo"), 1)
                dve.wait_ge(sem("x1_in"), 16 * (w + 1))
                for j in range(PIECES // 2):
                    dve.wait_ge(sem("y_turned"), (PIECES // 2) * w + j + 1)
                    ys = y_rows[:, 2 * j:2 * j + 2, :].rearrange("p t d -> p (t d)")
                    v.tensor_tensor(ys, ys, bank[6 + j][0:FP, :], ALU.add).then_inc(sem("y_ready"), 1)

        @block.scalar
        def _(act):
            a = nc.scalar
            act.wait_ge(sem("w_tr"), 1)
            a.activation(w1t[0][:], bank[4][:].rearrange("p (t j) -> p t j", t=DT), ACT.Copy).then_inc(sem("w_hi"), 1)
            for j in range(4):
                t, c = j // 2, j % 2
                act.wait_ge(sem("w_tr"), 7 + j)
                a.activation(wht[0][:, t, c * 384:(c + 1) * 384], bank[j % 2][:, 0:384], ACT.Copy).then_inc(sem("w_hi"), 1)
            for j in range(4):
                t, c = j // 2, j % 2
                act.wait_ge(sem("wc_scaled"), 1 + j)
                a.activation(wct[0][:, t, c * 384:(c + 1) * 384], e_f[0][:].rearrange("p g e -> p (g e)")[:, 0:384], ACT.Copy).then_inc(sem("w_hi"), 1)
            for u in range(USES):
                m = min(2, NT - 2 * u) * P
                act.wait_ge(sem("xt"), u + 1)
                a.activation(x_hi[:, :, 2 * P * u:2 * P * u + m], bank[6 + u % 2][:, 0:DT * m].rearrange("p (t n) -> p t n", t=DT),
                             ACT.Copy).then_inc(sem("xt_hi"), 1)
            with act.Fori(0, NSL // 2) as i:
                for b in range(2):
                    act.wait_ge(sem("slice_full"), 2 * i + (b + 1))
                    act.wait_ge(sem("stage_free"), 2 * i + (b + 1))
                    a.activation(trash[b][:], bank[b][:, 0:NT * SW], ACT.Relu, bias=over_bias[:, 0:1],
                                 accum_out=over[:, bass.ds(2 * i + b, 1)])
                    a.activation(stage[b][:].rearrange("p q c -> p (q c)"), bank[b][:, 0:NT * SW], ACT.Copy,
                                 saturate=False).then_inc(sem("stage_full"), 1)

            act.wait_ge(sem("deg_done"), NW)

            def relu_hi(g, u):
                m = min(2, NT - 2 * u)
                act.wait_ge(sem("relu_sums"), g + 1)
                a.activation(r_hi[:, 2 * u:2 * u + m, :].rearrange("p t d -> p (t d)"), bank[2 + u % 2][:, 0:m * D], ACT.Relu)\
                 .then_inc(sem("relu_hi"), 1)

            def msg_hi(s, w):
                n = WIN_LEN[w]
                if w:
                    act.wait_ge(sem("gate_sums"), half(s, w, 0) * 4)
                for f in range(DT):
                    act.wait_ge(sem("msg_sums"), half(s, w, f) + 1)
                    a.activation(m_hi[:, f, 0:n], bank[2 * (w % 2) + f][:, 0:n], ACT.Copy).then_inc(sem("msg_hi"), 1)

            def gates(s, w, f):
                n = WIN_LEN[w]
                mine = half(s, w, f) * 3
                theirs = half(s, w, f) * GATE_OPS + LEAD
                act.wait_ge(sem("gate_ops"), theirs + 1)
                a.activation(gate_a[:, 0:n], gate_a[:, 0:n], ACT.Sigmoid, bias=gate_bias[:, f:f + 1]).then_inc(sem("gate_acts"), 1)
                act.wait_ge(sem("gate_ops"), theirs + 2)
                a.activation(gate_z[:, 0:n], gate_z[:, 0:n], ACT.Sigmoid, bias=gate_bias[:, 2 + f:3 + f]).then_inc(sem("gate_acts"), 1)
                act.wait_ge(sem("gate_ops"), theirs + 5)
                a.activation(gate_a[:, 0:n], gate_a[:, 0:n], ACT.Tanh, bias=gate_bias[:, 4 + f:5 + f]).then_inc(sem("gate_acts"), 1)

            def state_hi(s, w):
                n, c0 = WIN_LEN[w], WIN_COL[w]
                act.wait_ge(sem("gate_ops"), half(s, w, 2) * GATE_OPS + LEAD)
                a.activation(x_hi[:, :, c0:c0 + n], x_new[:, :, 0:n], ACT.Copy).then_inc(sem("state_hi"), 1)

            for u in range(FILL_B):
                relu_hi(u, u)
            with act.Fori(0, STEPS) as s:
                for u in range(FILL_B, USES):
                    relu_hi(USES * s + u, u)
                msg_hi(s, 0)
                for w in range(1, NW):
                    gates(s, w - 1, 0)
                    msg_hi(s, w)
                    gates(s, w - 1, 1)
                    state_hi(s, w - 1)
                for u in range(FILL_A):
                    relu_hi(USES * s + USES + u, u)
                gates(s, NW - 1, 0)
                for u in range(FILL_A, FILL_B):
                    relu_hi(USES * s + USES + u, u)
                gates(s, NW - 1, 1)
                state_hi(s, NW - 1)

            for u in range(USES):
                m = min(2, NT - 2 * u) * P
                act.wait_ge(sem("x2t"), u + 1)
                a.activation(x_hi[:, :, 2 * P * u:2 * P * u + m], bank[2 + u % 2][:, 0:DT * m].rearrange("p (t n) -> p t n", t=DT),
                             ACT.Copy).then_inc(sem("x2t_hi"), 1)
            act.wait_ge(sem("top_diff"), 1)
            a.activation(top[:, 2, :], top[:, 2, :], ACT.Exp).then_inc(sem("top_exp"), 1)
            for c in range(CHUNKS):
                act.wait_ge(sem(f"chunk_in{c % 4}"), 16 * (c // 4 + 1))
                hi, lo = chunk_dst(c)
                src_ = raw[c % 4][:] if c % 4 < DT else raw[c % 4][:].rearrange("p (t d) -> p t d", t=2)
                a.activation(hi, src_, ACT.Copy).then_inc(sem("chunk_hi"), 1)
            act.wait_ge(sem("chunk_lo"), CHUNKS)
            act.wait_ge(sem("comb_out"), 16)
            with act.Fori(0, FN) as w:
                for i in range(BLOCKS + 1):
                    n = BLOCKS * w + i
                    if i < BLOCKS:
                        act.wait_ge(sem("h_sums"), n + 1)
                        if i >= 2:
                            act.wait_ge(sem("h_lo"), BLOCKS * w + (i - 1))
                        a.activation(act_h[i % 2][:], bank[i % 4][:, 0:FW], ACT.Relu, bias=hid_bias[:, i:i + 1]).then_inc(sem("h_relu"), 1)
                    if i >= 1:
                        b = (i - 1) % 2
                        act.wait_ge(sem("h_scaled"), n)
                        if i >= 3:
                            act.wait_ge(sem("y_sums"), BLOCKS * w + (i - 2))
                        a.activation(h_hi[b][:], act_h[b][:], ACT.Copy).then_inc(sem("h_hi"), 1)
                act.wait_ge(sem("y_full"), w + 1)
                for f in range(DT):
                    last = a.activation(y_t[:, f, :], bank[4 + f][:, 0:FW], ACT.Copy)
                last.then_inc(sem("y_t"), 1)

        @block.tensor
        def _(pe):
            mm = nc.tensor.matmul
            pe.wait_ge(sem("ident_ready"), 1)
            pe.wait_ge(sem("keys"), 1)
            for g in range(CG):
                for i in range(2):
                    last = nc.tensor.transpose(bank[i][:, g * P:(g + 1) * P], e_f[i][:, g, :], ident[:])
            last.then_inc(sem("keys_t"), 1)
            pe.wait_ge(sem("diags"), 1)
            pe.wait_ge(sem("ones_ready"), 1)
            for m in range(2):
                for g in range(CG):
                    last = mm(bank[2 + m][:, g * P:(g + 1) * P], ones_f[:], diag[:, m, g, :], start=True, stop=True)
            last.then_inc(sem("lims_b"), 1)
            pe.wait_ge(sem("w1_scaled"), 1)
            for t in range(DT):
                for h in range(DT):
                    last = nc.tensor.transpose(bank[4][:, t * D + h * P:t * D + (h + 1) * P], w1n[:, h, t * P:(t + 1) * P], ident[:])
            last.then_inc(sem("w_tr"), 1)
            for t in range(DT):
                last = mm(bank[5][:, 0:D], ones_f[:], b1_diag[:, t, :], start=t == 0, stop=t == DT - 1)
            last.then_inc(sem("w_tr"), 1)
            for j in range(4):
                t, c = j // 2, j % 2
                if j >= 2:
                    pe.wait_ge(sem("wit_ready"), j - 1)
                for o in range(3):
                    last = nc.tensor.transpose(bank[6 + j % 2][:, o * P:(o + 1) * P], win[:, 3 * c + o, t * P:(t + 1) * P], ident[:])
                last.then_inc(sem("w_tr"), 1)
            pe.wait_ge(sem("edge_table"), 1)
            for j in range(4):
                t, c = j // 2, j % 2
                if j >= 2:
                    pe.wait_ge(sem("w_lo"), j)
                for o in range(3):
                    last = nc.tensor.transpose(bank[j % 2][:, o * P:(o + 1) * P], whn[:, 3 * c + o, t * P:(t + 1) * P], ident[:])
                last.then_inc(sem("w_tr"), 1)
            pe.wait_ge(sem("wit_ready"), 4)
            pe.wait_ge(sem("bound_col"), 1)
            for o in range(GT):
                for t in range(DT):
                    last = mm(bank[2][:, o:o + 1], wit[:, t, o * P:(o + 1) * P], b2_col[:, t:t + 1], start=t == 0, stop=t == DT - 1)
            last.then_inc(sem("w_tr"), 1)
            for j in range(4):
                t, c = j // 2, j % 2
                if j == 0:
                    pe.wait_ge(sem("w_lo"), 1)
                    pe.wait_ge(sem("b1_done"), 1)
                if j >= 2:
                    pe.wait_ge(sem("wc_scaled"), j - 1)
                for m in range(DT):
                    last = mm(bank[4 + j % 2][:, 0:384], w2n[:, m, t * P:(t + 1) * P], wit[:, m, c * 384:(c + 1) * 384],
                              start=m == 0, stop=m == DT - 1)
                last.then_inc(sem("w_tr"), 1)
            for u in range(USES):
                m = min(2, NT - 2 * u)
                pe.wait_ge(sem("x_norm"), 2 * u + m)
                if u >= 2:
                    pe.wait_ge(sem("xt_lo"), u - 1)
                for t in range(DT):
                    for k in range(m):
                        last = nc.tensor.transpose(bank[6 + u % 2][:, (t * m + k) * P:(t * m + k + 1) * P],
                                                   xa[:, 2 * u + k, t * P:(t + 1) * P], ident[:])
                last.then_inc(sem("xt"), 1)

            pe.wait_ge(sem("bound_in"), 16)
            pe.wait_ge(sem("w_lo"), 9)
            for name, n in [("stage_full", 2)] + [(f"hot_free{s}", 1) for s in range(FIRST + 1)]:
                mm(bank[2][:, 0:2], ones_h[:], ones_h[:, 0:2], start=True, stop=True).then_inc(sem(name), n)
            extra = pe.alloc_register("pe_extra")
            pe.reg_mov(extra, 0)
            with pe.Fori(0, NSL // 2) as i:
                for b in range(2):
                    sl = 2 * i + b
                    first = pe.value_load(bound_row[0:1, bass.ds(2 * sl, 1)], min_val=0, max_val=NCH)
                    end = pe.value_load(bound_row[0:1, bass.ds(2 * sl + 1, 1)], min_val=0, max_val=NCH)
                    pe.wait_ge(sem("stage_full"), sl + 1)
                    for s in range(FIRST):
                        pe.wait_ge(sem(f"hot_full{s}"), sl + 1)
                        ins = mm(bank[b][:, 0:NT * SW], hot_row[s][:], hot_key[s][:], start=s == 0, stop=True, skip_group_check=True)
                        ins.then_inc(sem(f"hot_free{s}"), 1)
                    with pe.If(end > first + FIRST):
                        with pe.Fori(first + FIRST, end) as c:
                            pe.wait_ge(sem(f"hot_full{FIRST}"), pe.snap(extra) + 1)
                            mm(bank[b][:, 0:NT * SW], hot_row[FIRST][:], hot_key[FIRST][:], start=False, stop=True, skip_group_check=True)\
                                .then_inc(sem(f"hot_free{FIRST}"), 1)
                            pe.reg_add(extra, extra, 1)
                    mm(bank[2][:, 0:2], ones_h[:], ones_h[:, 0:2], start=True, stop=True).then_inc(sem("slice_full"), 1)
            pe.wait_ge(sem("stage_free"), NSL + 2)
            pe.wait_ge(sem("state_lo"), NW)
            for w in range(NW):
                if w >= 4:
                    pe.wait_ge(sem("deg_done"), w - 3)
                for q in range(NT):
                    last = mm(bank[4 + w % 4][:, 0:WIN_LEN[w]], ones_h[:], adj[:, q, WIN_COL[w]:WIN_COL[w] + WIN_LEN[w]],
                              start=q == 0, stop=q == NT - 1)
                last.then_inc(sem("deg_sum"), 1)
            pe.wait_ge(sem("deg_done"), NW)

            def relu_sum(t, u):
                m = min(2, NT - 2 * u)
                if not isinstance(t, int) or u >= 2:
                    pe.wait_ge(sem("relu_lo"), USES * t + max(u - 1, 0))
                pe.wait_ge(sem("state_lo"), NW * t + USE_WIN[u] + 1)
                o = bank[2 + u % 2]
                for k in range(m):
                    last = mm(o[:, k * D:(k + 1) * D], ones_r[:], b1_rows[:], start=k == 0, stop=False, skip_group_check=True)
                for k in range(m):
                    n0 = (2 * u + k) * P
                    for t in range(DT):
                        for xs, ws in ((x_hi, w1t[0]), (x_hi, w1t[1]), (x_lo, w1t[0])):
                            last = mm(o[:, k * D:(k + 1) * D], xs[:, t, n0:n0 + P], ws[:, t, :], start=False,
                                      stop=True, skip_group_check=True)
                last.then_inc(sem("relu_sums"), 1)

            def messages(w, f, q0, q1):
                n, c0 = WIN_LEN[w], WIN_COL[w]
                for q in range(q0, q1):
                    for r in (r_hi, r_lo):
                        last = mm(bank[2 * (w % 2) + f][:, 0:n], r[:, q, f * P:(f + 1) * P], adj[:, q, c0:c0 + n],
                                  start=q == 0 and r is r_hi, stop=q == NT - 1 and r is r_lo)
                if q1 == NT:
                    last.then_inc(sem("msg_sums"), 1)

            def gates(s, w, f):
                n, c0 = WIN_LEN[w], WIN_COL[w]
                pe.wait_ge(sem("gate_ops"), half(s, w, f) * GATE_OPS + 1)
                if f == 0:
                    pe.wait_ge(sem("msg_lo"), half(s, w, 2))
                for k, (b, parts) in enumerate(((4, (("h", f), ("m", f))), (5, (("h", 2 + f), ("m", 2 + f))),
                                                (6, (("h", 4 + f),)), (7, (("m", 4 + f),)))):
                    todo = []
                    for what, o in parts:
                        for t in range(DT):
                            if what == "h":
                                hi, lo, wt = x_hi[:, t, c0:c0 + n], x_lo[:, t, c0:c0 + n], wht
                            else:
                                hi, lo, wt = m_hi[:, t, 0:n], m_lo[:, t, 0:n], wct
                            wh, wl = (wt[i][:, t, o * P:(o + 1) * P] for i in range(2))
                            todo += [(wh, hi), (wh, lo), (wl, hi)]
                    for i, (wgt, mov) in enumerate(todo):
                        last = mm(bank[b][:, 0:n], wgt, mov, start=i == 0, stop=i == len(todo) - 1)
                    last.then_inc(sem("gate_sums"), 1)

            late = 2 * EARLY
            for u in range(FILL_B):
                relu_sum(0, u)
            with pe.Fori(0, STEPS) as s:
                for u in range(FILL_B, EARLY):
                    relu_sum(s, u)
                pe.wait_ge(sem("relu_lo"), USES * s + EARLY)
                mm(bank[0][:, 0:2], ones_r[:], b1_rows[:, 0:2], start=True, stop=True)
                messages(0, 0, 0, late)
                messages(0, 1, 0, late)
                for u in range(EARLY, USES):
                    relu_sum(s, u)
                pe.wait_ge(sem("relu_lo"), USES * s + USES)
                mm(bank[3][:, 0:2], ones_r[:], b1_rows[:, 0:2], start=True, stop=True)
                messages(0, 0, late, NT)
                messages(0, 1, late, NT)
                for w in range(1, NW):
                    messages(w, 0, 0, NT)
                    gates(s, w - 1, 0)
                    messages(w, 1, 0, NT)
                    gates(s, w - 1, 1)
                for u in range(FILL_A):
                    relu_sum(s + 1, u)
                gates(s, NW - 1, 0)
                for u in range(FILL_A, FILL_B):
                    relu_sum(s + 1, u)
                gates(s, NW - 1, 1)

            pe.wait_ge(sem("state_lo"), NW * (STEPS + 1))
            pe.wait_ge(sem("ident_r"), 1)
            pe.wait_ge(sem("relu_lo"), USES * STEPS + FILL_B)
            for u in range(USES):
                m = min(2, NT - 2 * u)
                if u >= 2:
                    pe.wait_ge(sem("x1_sum"), u - 1)
                for k in range(m):
                    n0 = (2 * u + k) * P
                    for t in range(DT):
                        for xs in (x_hi, x_lo):
                            last = mm(bank[u % 2][:, k * D + t * P:k * D + (t + 1) * P], xs[:, t, n0:n0 + P], ident_r[:],
                                      start=k == 0 and t == 0 and xs is x_hi, stop=True, skip_group_check=True)
                last.then_inc(sem("rows"), 1)
            for u in range(USES):
                m = min(2, NT - 2 * u)
                pe.wait_ge(sem("x1_norm"), 2 * u + m)
                if u >= 2:
                    pe.wait_ge(sem("x2t_lo"), u - 1)
                for t in range(DT):
                    for k in range(m):
                        last = nc.tensor.transpose(bank[2 + u % 2][:, (t * m + k) * P:(t * m + k + 1) * P],
                                                   x1[:, 2 * u + k, t * P:(t + 1) * P], ident[:])
                last.then_inc(sem("x2t"), 1)
            pe.wait_ge(sem("x2t_lo"), USES)
            pe.wait_ge(sem("wg_split"), 1)
            nc.tensor.transpose(bank[5][:, 0:BLOCKS], hid_bias_rows[:], ident[0:BLOCKS, 0:BLOCKS]).then_inc(sem("hid_bias_t"), 1)
            first_mm = True
            for t in range(NT):
                for k in range(DT):
                    for xs in (x_hi, x_lo):
                        for ws in wg_r:
                            last = mm(bank[4][:, t * NX:(t + 1) * NX], xs[:, k, t * P:(t + 1) * P], ws[:, k, :],
                                      start=first_mm, stop=True, skip_group_check=True)
                            first_mm = False
            last.then_inc(sem("logits"), 1)
            pe.wait_ge(sem("combine"), 1)
            for g in range((NT + 3) // 4):
                o = bank[COMB_BANK[g]]
                for k in range(min(4, NT - 4 * g)):
                    c = k if g < 6 else 1
                    last = nc.tensor.transpose(o[0:NX, c * P:(c + 1) * P], hot1[:, 4 * g + k, :], ident[:])
                last.then_inc(sem("comb_tr"), 1)
            pe.wait_ge(sem("comb_sb"), 1)
            pe.wait_ge(sem("out_bias_in"), 16)
            with pe.Fori(0, FN) as w:
                c0 = pe.snap(w * FW)
                for i in range(BLOCKS + 2):
                    if i < BLOCKS:
                        e, h = i // HT, i % HT
                        if h == 0:
                            pe.wait_ge(sem("chunk_lo"), 4 * e + DT)
                        if i >= 4:
                            pe.wait_ge(sem("h_relu"), BLOCKS * w + (i - 3))
                        k = 0
                        for t in range(DT):
                            for xs, ws in ((x_hi, f1w[0]), (x_lo, f1w[0]), (x_hi, f1w[1])):
                                last = mm(bank[i % 4][:, 0:FW], ws[:, t, e, h * P:(h + 1) * P], xs[:, t, bass.ds(c0, FW)],
                                          start=k == 0, stop=k == 5)
                                k += 1
                        last.then_inc(sem("h_sums"), 1)
                    if i >= 2:
                        j = i - 2
                        e, h = j // HT, j % HT
                        if h == 0:
                            pe.wait_ge(sem("chunk_lo"), 4 * e + 4)
                        pe.wait_ge(sem("h_lo"), BLOCKS * w + j + 1)
                        for f in range(DT):
                            k = 0
                            for hs, ws in ((h_hi, f2w[0]), (h_lo, f2w[0]), (h_hi, f2w[1])):
                                last = mm(bank[4 + f][:, 0:FW], ws[:, h, e, f * P:(f + 1) * P], hs[j % 2][:],
                                          start=j == 0 and k == 0, stop=False)
                                k += 1
                        last.then_inc(sem("y_sums"), 1)
                pe.wait_ge(sem("comb_w_in"), 16 * (w + 1))
                for f in range(DT):
                    last = mm(bank[4 + f][:, 0:FW], out_bias[:, f * P:(f + 1) * P], comb_w[:], start=False, stop=True)
                last.then_inc(sem("y_full"), 1)
                pe.wait_ge(sem("y_t"), w + 1)
                for j in range(PIECES):
                    for f in range(DT):
                        last = nc.tensor.transpose(bank[6 + j // 2][0:FP, (j % 2) * D + f * P:(j % 2) * D + (f + 1) * P],
                                                   y_t[:, f, j * FP:(j + 1) * FP], ident[:])
                    if j % 2:
                        last.then_inc(sem("y_turned"), 1)


_INS = ["x", "src", "dst"] + ["L0_gnn_" + n for n in ("W1", "b1", "W2", "b2", "W_ih", "b_ih", "W_hh", "b_hh")] \
    + ["L0_ffn_" + n for n in ("Wg", "bg", "bias", "W1", "b1", "W2", "b2")]


def kernel(**inputs):
    import numpy as _np
    import concourse.bacc as _bacc
    from concourse.bass_utils import run_bass_kernel_spmd as _run

    nc = _bacc.Bacc("TRN2", target_bir_lowering=False, num_devices=1)
    arrays, args = {}, []
    for name in _INS:
        a = _np.ascontiguousarray(inputs[name])
        arrays[f"in_{name}"] = a
        args.append(nc.dram_tensor(f"in_{name}", a.shape, mybir.dt.from_np(a.dtype), kind="ExternalInput").ap())
    args.append(nc.dram_tensor("out_0", (N, D), F32, kind="ExternalOutput").ap())
    gnn_ffn(nc, *args)
    r = _run(nc, [arrays], core_ids=[0])
    return r.results[0]["out_0"]
```

```python
from contextlib import ExitStack

import concourse.bass as bass
from concourse import mybir

F32 = mybir.dt.float32
F32R = mybir.dt.float32r
F16 = mybir.dt.float16
F8 = mybir.dt.float8e4
I32 = mybir.dt.int32
U16 = mybir.dt.uint16
U32 = mybir.dt.uint32
ALU = mybir.AluOpType
ACT = mybir.ActivationFunctionType
AX = mybir.AxisListType

P = 128
N = 3125
D = 256
E = 53125
STEPS = 6
DT = D // P
NT = (N + P - 1) // P
NPAD = NT * P
TAIL = N - (NT - 1) * P
G3 = 3 * D
GT = G3 // P

WIN_TILES = (4, 4, 4, 4, 3, 3, 3)
NW = len(WIN_TILES)
WIN_T0 = [sum(WIN_TILES[:w]) for w in range(NW)]
WIN_COL = [t * P for t in WIN_T0]
WIN_LEN = [n * P for n in WIN_TILES]
WIN_LEN[-1] = N + N % 2 - WIN_COL[-1]

SW = 16
NSL = (N + SW - 1) // SW
GROUP = 4
NSL = (NSL + GROUP - 1) // GROUP * GROUP
TURNS = NSL // GROUP
ACOLS = NSL * SW
KEY = 512
NCH = (E + P - 1) // P
CG = (NCH + P - 1) // P
SLOTS = 4
TURN_SLOTS = GROUP * SLOTS
SL_T = (NSL + P - 1) // P
EXACT8 = 16

USES = (NT + 1) // 2
USE_WIN = [max(w for w in range(NW) if WIN_T0[w] <= min(2 * u + 1, NT - 1)) for u in range(USES)]
EARLY = max(u for u in range(USES) if USE_WIN[u] < NW - 1) + 1
FILL_A = sum(USE_WIN[u] < 3 for u in range(USES))
FILL_B = sum(USE_WIN[u] < 5 for u in range(USES))

GATE_OPS = 9
NX = 8
HID = 512
HT = HID // P
FW = 448
FN = (N + FW - 1) // FW
PIECES = 4
FP = FW // PIECES
FLAST = N - (FN - 1) * FW - (PIECES - 1) * FP
COMB_BANK = (0, 1, 2, 3, 6, 7, 5)
BLOCKS = NX * HT
CHUNKS = 2 * DT * NX
LEAD = 6


def gnn_ffn(nc, x, src, dst, W1, b1, W2, b2, W_ih, b_ih, W_hh, b_hh, Wg, bg, bias, F1, fb1, F2, fb2, out):
    stack = ExitStack()
    with stack:
        sems = {}

        def sem(name):
            if name not in sems:
                sems[name] = stack.enter_context(nc.semaphore(name))
            return sems[name]

        def allocator(scope):
            return lambda name, shape, dt: scope.enter_context(nc.sbuf_tensor(name, shape, dt))

        sb = allocator(stack)
        bank = [stack.enter_context(nc.psum_tensor(f"bank{i}", [P, 512], F32)) for i in range(8)]

        ident = sb("ident", [P, P], F32)
        x_hi = sb("x_hi", [P, DT, NPAD], F32R)
        x_lo = sb("x_lo", [P, DT, NPAD], F32R)

        slow_flag = sb("slow_flag", [1, 1], I32)

        gnn = ExitStack()
        gb = allocator(gnn)
        w1t = [gb(f"w1t_{p}", [P, DT, D], F32R) for p in ("hi", "lo")]
        wct = [gb(f"wct_{p}", [P, DT, G3], F32R) for p in ("hi", "lo")]
        wht = [gb(f"wht_{p}", [P, DT, G3], F32R) for p in ("hi", "lo")]
        b1_rows = gb("b1_rows", [P, D], F32R)
        ones_r = gb("ones_r", [P, P], F32R)
        gate_bias = gb("gate_bias", [P, GT], F32)
        hn_bias = gb("hn_bias", [P, DT], F32)
        deg_w = gb("deg_w", [P, GT], F32)
        degree = gb("degree", [P, ACOLS], U16)

        prep = ExitStack()
        pp = allocator(prep)
        xa = pp("xa", [P, NT, D], F32)
        w1n = pp("w1n", [P, DT, D], F32)
        w2n = pp("w2n", [P, DT, D], F32)
        win = pp("win", [P, GT, D], F32)
        whn = pp("whn", [P, GT, D], F32)
        wit = pp("wit", [P, DT, G3], F32)
        e_src = pp("e_src", [P, CG, P], I32)
        e_dst = pp("e_dst", [P, CG, P], I32)
        e_tmp = pp("e_tmp", [P, CG, P], I32)
        e_f = [pp(f"e_f{i}", [P, CG, P], F32) for i in range(3)]
        lim = pp("lim", [P, 2, CG], F32)
        diag = pp("diag", [P, 2, CG, P], F32)
        lim_b = pp("lim_b", [P, 2, CG * P], F32)
        chunk_id = pp("chunk_id", [P, CG * P], F32)
        mask = pp("mask", [P, CG * P], F32)
        prep.close()
        adj_scope = ExitStack()
        planes_scope = ExitStack()
        planes = allocator(planes_scope)("planes", [P, 2, NT, 512], F16)
        planes_scope.close()
        adj = allocator(adj_scope)("adj", [P, NT, ACOLS], F8)

        bs = ExitStack()
        bb = allocator(bs)
        key_t = bb("key_t", [P, NCH], F32)
        row_t = bb("row_t", [P, NCH], F32)
        picked = bb("picked", [P, CG, NSL * SLOTS], F32)
        slot_id = bb("slot_id", [P, SLOTS], F32)
        part_id = bb("part_id", [P, CG], F32)
        slot_key = bb("slot_key", [P, NSL, SLOTS], F32)
        slot_row = bb("slot_row", [P, NSL, SLOTS], F32)
        turn_key = bb("turn_key", [P, TURN_SLOTS], F32)
        turn_row = bb("turn_row", [P, TURN_SLOTS], F32)
        iota_key = bb("iota_key", [P, NT * SW], F16)
        iota_row = bb("iota_row", [P, P], F16)
        slice_off = bb("slice_off", [P, NSL], F32)
        hot_key = [bb(f"hot_key{s}", [P, NT * SW], F16) for s in range(2 * SLOTS)]
        hot_row = [bb(f"hot_row{s}", [P, P], F16) for s in range(2 * SLOTS)]
        stage = [bb(f"stage{i}", [P, NT, 2 * SW], F8) for i in range(2)]
        trash = [bb(f"trash{i}", [P, NT * SW], F16) for i in range(GROUP)]
        over = bb("over", [P, NSL], F32)
        bound_row = bb("bound_row", [1, 2 * 2 * P], I32)
        bound = bb("bound", [P, 2, 2], I32)
        slice_id = bb("slice_id", [P, 2], F32)
        bnd = bb("bnd", [P, 2, 2], F32)
        small = bb("small", [P, 16], F32)
        smalli = bb("smalli", [P, 16], I32)
        b1_col = bb("b1_col", [P, DT], F32)
        b2_col = bb("b2_col", [P, DT], F32)
        bih_col = bb("bih_col", [P, GT], F32)
        bhh_col = bb("bhh_col", [P, GT], F32)
        b1_diag = bb("b1_diag", [P, 2, D], F32)
        st = bb("st", [P, NT, 6], F32)
        mv = bb("mv", [P, NT, 2], F32)
        rstd = bb("rstd", [P, NT], F32)
        expo = bb("expo", [P, NT], F32)
        ones_h = bb("ones_h", [P, P], F16)
        ones_f = bb("ones_f", [P, P], F32)
        more = bb("more", [P, SL_T + 2], F32)
        minus_exact = bb("minus_exact", [P, 1], F32)
        bs.close()

        steps = ExitStack()
        ss = allocator(steps)
        r_hi = ss("r_hi", [P, NT, D], F16)
        r_lo = ss("r_lo", [P, NT, D], F16)
        m_hi = ss("m_hi", [P, DT, 512], F32R)
        m_lo = ss("m_lo", [P, DT, 512], F32R)
        gate_a = ss("gate_a", [P, 512], F32)
        gate_z = ss("gate_z", [P, 512], F32)
        x_new = ss("x_new", [P, DT, 512], F32)
        steps.close()
        adj_scope.close()
        gnn.close()

        ffn = ExitStack()
        fb = allocator(ffn)
        f1w = [fb(f"f1w_{p}", [P, DT, NX, HID], F32R) for p in ("hi", "lo")]
        f2w = [fb(f"f2w_{p}", [P, HT, NX, D], F32R) for p in ("hi", "lo")]
        ident_r = fb("ident_r", [P, P], F32R)
        hid_bias = fb("hid_bias", [P, BLOCKS], F32)
        out_bias = fb("out_bias", [NX, D], F32)
        norm2 = ExitStack()
        nb = allocator(norm2)
        x1 = nb("x1", [P, NT, D], F32)
        st2 = nb("st2", [P, NT, 6], F32)
        mv2 = nb("mv2", [P, NT, 2], F32)
        rstd2 = nb("rstd2", [P, NT], F32)
        expo2 = nb("expo2", [P, NT], F32)
        norm2.close()
        gate = ExitStack()
        tb = allocator(gate)
        wg = tb("wg", [P, DT, NX], F32)
        wg_r = [tb(f"wg_{p}", [P, DT, NX], F32R) for p in ("hi", "lo")]
        bg_b = tb("bg_b", [P, 2, NX], F32)
        eid = tb("eid", [P, NT, NX], F32)
        logit = tb("logit", [P, NT, NX], F32)
        cand = tb("cand", [P, NT, NX], F32)
        hot1 = tb("hot1", [P, NT, NX], F32)
        hot2 = tb("hot2", [P, NT, NX], F32)
        top = tb("top", [P, 6, NT], F32)
        comb_t = tb("comb_t", [NX, NPAD], F32)
        hid_bias_rows = tb("hid_bias_rows", [BLOCKS, P], F32)
        raw = [tb(f"raw{i}", [P, HID], F32) for i in range(4)]
        gate.close()
        hb_ = ExitStack()
        hb = allocator(hb_)
        act_h = [hb(f"act_h{i}", [P, FW], F32) for i in range(2)]
        h_hi = [hb(f"h_hi{i}", [P, FW], F32R) for i in range(2)]
        h_lo = [hb(f"h_lo{i}", [P, FW], F32R) for i in range(2)]
        comb_b = [hb(f"comb_b{i}", [P, FW], F32) for i in range(4)]
        comb_w = hb("comb_w", [NX, FW], F32)
        y_t = hb("y_t", [P, DT, FW], F32)
        y_rows = hb("y_rows", [FP, PIECES, D], F32)
        hb_.close()
        ffn.close()

        x1_dram = nc.dram_tensor("x1_scratch", (NPAD, D), F32, kind="Internal").ap()
        comb_dram = nc.dram_tensor("comb_scratch", (NX, NPAD), F32, kind="Internal").ap()
        plane_dram = [nc.dram_tensor(f"plane_scratch{i}", (P, NT, ACOLS), F16, kind="Internal").ap() for i in range(2)]
        bound_dram = nc.dram_tensor("bound_scratch", (2 * P, 2), I32, kind="Internal").ap()
        inputs = sem("inputs")
        block = stack.enter_context(nc.Block())

        exact_sum = picked[:, 0, 0:NT * SW]
        exact_part = [trash[i] for i in range(2)]
        EXACT_STORED = 32 * NSL + 1

        def if_slow(engine):
            engine.wait_ge(sem("slow_flag"), 1)
            slow = engine.value_load(slow_flag[0:1, 0:1], min_val=0, max_val=1)
            return slow

        def half(s, w, f):
            return s * (2 * NW) + 2 * w + f

        @block.sync
        def _(sp):
            sp.wait_ge(sem("edges_clear"), 2)
            full = (NCH - 1) // P * P
            rest = E // P - full
            for buf, inp in ((e_src, src), (e_dst, dst)):
                sp.dma_start(buf[:, 0:full // P, :], inp[0:full * P].rearrange("(g p e) -> p g e", p=P, e=P)).then_inc(sem("edges"), 16)
                sp.dma_start(buf[0:rest, full // P, :], inp[full * P:(full + rest) * P].rearrange("(p e) -> p e", e=P)).then_inc(sem("edges"), 16)
            last = E - (full + rest) * P
            sp.dma_start(e_src[rest:rest + 1, full // P, P - last:P], src[E - last:E].rearrange("(a e) -> a e", a=1)).then_inc(sem("edges"), 16)
            sp.dma_start(e_dst[rest:rest + 1, full // P, :], dst[E - P:E].rearrange("(a e) -> a e", a=1)).then_inc(sem("edges"), 16)
            sp.dma_start(w1n[:], W1.rearrange("(t p) i -> p t i", p=P)).then_inc(inputs, 16)
            sp.dma_start(w2n[:], W2.rearrange("(t p) i -> p t i", p=P)).then_inc(inputs, 16)
            sp.dma_start(win[:], W_ih.rearrange("(t p) i -> p t i", p=P)).then_inc(inputs, 16)
            sp.dma_start(whn[:], W_hh.rearrange("(t p) i -> p t i", p=P)).then_inc(inputs, 16)
            for buf, inp in ((b1_col, b1), (b2_col, b2), (bih_col, b_ih), (bhh_col, b_hh)):
                sp.dma_start(buf[:], inp.rearrange("(t p) -> p t", p=P), allow_slow_non_contiguous=True).then_inc(inputs, 16)
            sp.wait_ge(sem("xa_clear"), 1)
            sp.dma_start(xa[:, 0:NT - 1, :], x[0:(NT - 1) * P, :].rearrange("(t p) d -> p t d", p=P)).then_inc(sem("x_in"), 16)
            sp.dma_start(xa[0:TAIL, NT - 1, :], x[(NT - 1) * P:N, :]).then_inc(sem("x_in"), 16)
            sp.wait_ge(sem("bound_col"), 1)
            sp.dma_start(bound_dram.rearrange("(t p) b -> p t b", p=P), bound[:]).then_inc(sem("bound_out"), 16)
            sp.wait_ge(sem("bound_out"), 16)
            sp.dma_start(bound_row[:], bound_dram.rearrange("(a p) b -> a (p b)", a=1)).then_inc(sem("bound_in"), 16)
            slow = if_slow(sp)
            with sp.If(slow > 0):
                with sp.Fori(0, NSL) as sl:
                    c0 = sp.snap(sl * SW)
                    sp.wait_ge(sem("exact_split"), sl + 1)
                    for i in range(2):
                        sp.dma_start(plane_dram[i][:, :, bass.ds(c0, SW)], exact_part[i][:].rearrange("p (q c) -> p q c", c=SW))\
                          .then_inc(sem("exact_stored"), 16)
                sp.wait_ge(sem("exact_stored"), EXACT_STORED)

                def load_planes(w):
                    n, c0 = WIN_LEN[w], WIN_COL[w]
                    for i in range(2):
                        sp.dma_start(planes[:, i, :, 0:n], plane_dram[i][:, :, c0:c0 + n]).then_inc(sem("planes_in"), 16)

                for w in range(NW):
                    load_planes(w)
                    sp.wait_ge(sem("exact_deg_sum"), w + 1)
                load_planes(0)
                with sp.Fori(0, STEPS - 1) as s:
                    for w in range(NW):
                        sp.wait_ge(sem("msg_sums"), half(s, w, 2))
                        load_planes((w + 1) % NW)
                for w in range(NW - 1):
                    sp.wait_ge(sem("msg_sums"), half(STEPS - 1, w, 2))
                    load_planes(w + 1)
            sp.wait_ge(sem("x1_clear"), 1)
            sp.dma_start(x1[:, 0:NT - 1, :], x[0:(NT - 1) * P, :].rearrange("(t p) d -> p t d", p=P)).then_inc(sem("x_again"), 16)
            sp.dma_start(x1[0:TAIL, NT - 1, :], x[(NT - 1) * P:N, :]).then_inc(sem("x_again"), 16)
            sp.dma_start(out_bias[:], fb2[:]).then_inc(sem("out_bias_in"), 16)
            sp.wait_ge(sem("x1_sum"), USES)
            sp.dma_start(x1_dram.rearrange("(t p) d -> p t d", p=P), x1[:]).then_inc(sem("x1_out"), 16)
            sp.wait_ge(sem("x2t"), USES)
            sp.dma_start(wg[:], Wg.rearrange("(t p) e -> p t e", p=P)).then_inc(sem("gate_in"), 16)
            sp.dma_start(bg_b[:, 0, :], bg.rearrange("(a e) -> a e", a=1).broadcast_to([P, NX])).then_inc(sem("gate_in"), 16)
            sp.dma_start(bg_b[:, 1, :], bias.rearrange("(a e) -> a e", a=1).broadcast_to([P, NX])).then_inc(sem("gate_in"), 16)
            sp.dma_start(hid_bias_rows[:], fb1.rearrange("e (t p) -> (e t) p", p=P)).then_inc(sem("gate_in"), 16)
            for c in range(CHUNKS):
                e, k = c // 4, c % 4
                if c >= 4:
                    sp.wait_ge(sem("chunk_lo"), c - 3)
                if c == CHUNKS // 2:
                    sp.wait_ge(sem("comb_sb"), 1)
                    sp.dma_start(comb_dram[:], comb_t[:]).then_inc(sem("comb_out"), 16)
                if k < DT:
                    sp.dma_start(raw[c % 4][:], F1[e, k * P:(k + 1) * P, :]).then_inc(sem(f"chunk_in{c % 4}"), 16)
                else:
                    h0 = (k - DT) * 2 * P
                    sp.dma_start(raw[c % 4][:].rearrange("p (t d) -> p t d", t=2),
                                 F2[e, h0:h0 + 2 * P, :].rearrange("(t p) d -> p t d", p=P)).then_inc(sem(f"chunk_in{c % 4}"), 16)
            sp.wait_ge(sem("chunk_lo"), CHUNKS)
            sp.wait_ge(sem("comb_out"), 16)

            def load_comb(e, c0):
                sp.dma_start(comb_b[e % 4][:], comb_dram[e:e + 1, bass.ds(c0, FW)].broadcast_to([P, FW]))\
                  .then_inc(sem(f"comb_in{e % 4}"), 16)

            for e in range(4):
                load_comb(e, 0)

            def load_rows(w):
                sp.dma_start(comb_w[:], comb_dram[:, bass.ds(w * FW, FW)]).then_inc(sem("comb_w_in"), 16)
                sp.dma_start(y_rows[:], x1_dram[bass.ds(w * FW, FW), :].rearrange("(j p) d -> p j d", p=FP)).then_inc(sem("x1_in"), 16)

            def feed(w, experts):
                for e in experts:
                    sp.wait_ge(sem("h_scaled"), BLOCKS * w + HT * (e + 1))
                    n = e + 4
                    load_comb(n % NX, (w + n // NX) * FW)
                sp.wait_ge(sem("y_ready"), (PIECES // 2) * (w + 1))

            load_rows(0)
            with sp.Fori(0, FN - 1) as w:
                feed(w, range(NX))
                sp.dma_start(out[bass.ds(w * FW, FW), :].rearrange("(j p) d -> p j d", p=FP), y_rows[:]).then_inc(sem("y_stored"), 16)
                sp.wait_ge(sem("y_stored"), 16 * (w + 1))
                load_rows(w + 1)
            feed(FN - 1, range(NX - 4))
            r0 = (FN - 1) * FW
            r1 = r0 + (PIECES - 1) * FP
            sp.dma_start(out[r0:r1, :].rearrange("(j p) d -> p j d", p=FP), y_rows[:, 0:PIECES - 1, :]).then_inc(sem("y_stored"), 16)
            sp.dma_start(out[r1:N, :], y_rows[0:FLAST, PIECES - 1, :]).then_inc(sem("y_stored"), 16)
            sp.wait_ge(sem("y_stored"), 16 * (FN + 1))

        INPUTS = 16 * 8

        @block.gpsimd
        def _(pool):
            pool.memset(ones_f[:], 1.0).then_inc(sem("ones_ready"), 1)
            pool.memset(e_src[:], -1).then_inc(sem("edges_clear"), 1)
            pool.memset(e_dst[:], 0).then_inc(sem("edges_clear"), 1)
            pool.memset(xa[:, NT - 1, :], 0.0).then_inc(sem("xa_clear"), 1)
            pool.memset(ident[:], 0.0).then_inc(sem("p0"), 1)
            pool.wait_ge(sem("p0"), 1)
            pool.affine_select(out=ident[:], in_=ident[:], compare_op=ALU.not_equal, fill=1.0, base=0,
                               pattern=[[-1, P]], channel_multiplier=1).then_inc(sem("ident_ready"), 1)
            pool.iota(chunk_id[:], [[1, CG * P]], base=0, channel_multiplier=0, allow_small_or_imprecise_dtypes=True).then_inc(sem("iotas"), 1)
            pool.iota(slice_id[:], [[P, 2]], base=0, channel_multiplier=1, allow_small_or_imprecise_dtypes=True).then_inc(sem("iotas"), 1)
            pool.iota(iota_key[:], [[1, NT * SW]], base=0, channel_multiplier=0, allow_small_or_imprecise_dtypes=True).then_inc(sem("iotas"), 1)
            pool.iota(iota_row[:], [[1, P]], base=0, channel_multiplier=0, allow_small_or_imprecise_dtypes=True).then_inc(sem("iotas"), 1)
            pool.iota(slice_off[:], [[KEY, NSL]], base=0, channel_multiplier=0, allow_small_or_imprecise_dtypes=True).then_inc(sem("iotas"), 1)
            pool.iota(slot_id[:], [[1, SLOTS]], base=0, channel_multiplier=0, allow_small_or_imprecise_dtypes=True).then_inc(sem("iotas"), 1)
            pool.iota(part_id[:], [[P, CG]], base=0, channel_multiplier=1, allow_small_or_imprecise_dtypes=True).then_inc(sem("iotas"), 1)
            pool.memset(minus_exact[:], -float(EXACT8)).then_inc(sem("stage_free"), 2)
            pool.memset(expo[:], -0.5).then_inc(sem("p0"), 1)
            pool.wait_ge(sem("p0"), 2)
            pool.wait_ge(sem("var_ready"), 1)
            pool.tensor_tensor(rstd[:], rstd[:], expo[:], ALU.pow).then_inc(sem("rstd_ready"), 1)
            with pool.Fori(0, TURNS) as i:
                for b in range(GROUP):
                    if b % 2:
                        pool.wait_ge(sem("stage_full"), GROUP * i + (b + 5))
                        pool.tensor_copy(adj[:].bitcast(U32)[:, :, bass.ds(i * (GROUP * SW // 4) + (b - 1) * SW // 4, 2 * SW // 4)],
                                         stage[b // 2][:].bitcast(U32)).then_inc(sem("stage_free"), 1)
            slow = if_slow(pool)
            with pool.If(slow > 0):
                with pool.Fori(0, NSL) as sl:
                    pool.wait_ge(sem("exact_hi"), sl + 2)
                    pool.tensor_tensor(exact_part[1][:], exact_sum, exact_part[0][:], ALU.subtract).then_inc(sem("exact_split"), 1)
            pool.wait_ge(sem("state_lo"), NW * (STEPS + 1))
            pool.memset(x1[:, NT - 1, :], 0.0).then_inc(sem("x1_clear"), 1)
            pool.memset(expo2[:], -0.5).then_inc(sem("p0"), 1)
            pool.wait_ge(sem("p0"), 3)
            pool.wait_ge(sem("var_ready"), 2)
            pool.tensor_tensor(rstd2[:], rstd2[:], expo2[:], ALU.pow).then_inc(sem("rstd_ready"), 1)
            pool.wait_ge(sem("x2t"), USES)
            pool.iota(eid[:], [[0, NT], [1, NX]], base=0, channel_multiplier=0, allow_small_or_imprecise_dtypes=True).then_inc(sem("iotas"), 1)

        def chunk_dst(c):
            e, k = c // 4, c % 4
            if k < DT:
                return [w[:, k, e, :] for w in f1w]
            return [w[:, 2 * (k - DT):2 * (k - DT) + 2, e, :] for w in f2w]

        @block.vector
        def _(dve):
            chain = [0]

            def link(ins):
                chain[0] += 1
                ins.then_inc(sem("dve_prep"), 1)
                dve.wait_ge(sem("dve_prep"), chain[0])

            v = nc.vector
            dve.wait_ge(sem("edges"), 16 * 6)
            link(v.tensor_scalar(e_tmp[:], e_dst[:], -SW, (KEY // SW).bit_length() - 1, ALU.bitwise_and, ALU.arith_shift_left))
            link(v.scalar_tensor_tensor(e_tmp[:], e_dst[:], SW - 1, e_tmp[:], ALU.bitwise_and, ALU.bitwise_or))
            link(v.tensor_copy(e_f[2][:], e_dst[:]))
            link(v.tensor_scalar(e_dst[:], e_src[:], 127, None, ALU.bitwise_and))
            link(v.tensor_copy(e_f[1][:], e_dst[:]))
            link(v.tensor_scalar(e_src[:], e_src[:], -P, (P // SW).bit_length() - 1, ALU.bitwise_and, ALU.arith_shift_right))
            link(v.tensor_tensor(e_tmp[:], e_tmp[:], e_src[:], ALU.bitwise_or))
            v.tensor_copy(e_f[0][:], e_tmp[:]).then_inc(sem("keys"), 1)
            v.tensor_reduce(lim[:, 0, :], e_f[2][:], AX.X, ALU.min).then_inc(sem("lims"), 1)
            v.tensor_reduce(lim[:, 1, :], e_f[2][:], AX.X, ALU.max).then_inc(sem("lims"), 1)
            dve.wait_ge(sem("lims"), 2)
            dve.wait_ge(sem("ident_ready"), 1)
            for m in range(2):
                for g in range(CG):
                    last = v.tensor_scalar(diag[:, m, g, :], ident[:], lim[:, m, g:g + 1], None, ALU.mult)
            last.then_inc(sem("diags"), 1)
            dve.wait_ge(sem("keys_t"), 1)
            v.tensor_copy(key_t[:, 0:NCH], bank[0][:, 0:NCH])
            v.tensor_copy(row_t[:, 0:NCH], bank[1][:, 0:NCH]).then_inc(sem("edge_table"), 1)
            dve.wait_ge(sem("lims_b"), 1)
            v.tensor_copy(lim_b[:, 0, :], bank[2][:])
            link(v.tensor_copy(lim_b[:, 1, :], bank[3][:]))
            dve.wait_ge(sem("iotas"), 7)
            for t in range(2):
                link(v.tensor_scalar(small[:, 0:1], slice_id[:, t:t + 1], float(SW), float(SW - 1), ALU.mult, ALU.add))
                link(v.tensor_scalar(small[:, 1:2], slice_id[:, t:t + 1], float(SW), None, ALU.mult))
                link(v.tensor_scalar(mask[:, 0:NCH], lim_b[:, 0, 0:NCH], small[:, 0:1], None, ALU.is_le))
                link(v.scalar_tensor_tensor(mask[:, 0:NCH], lim_b[:, 1, 0:NCH], small[:, 1:2], mask[:, 0:NCH], ALU.is_ge, ALU.mult))
                link(v.scalar_tensor_tensor(e_f[2][:].rearrange("p g e -> p (g e)")[:, 0:NCH], chunk_id[:, 0:NCH], float(-NCH), mask[:, 0:NCH], ALU.add, ALU.mult))
                link(v.tensor_reduce(small[:, 2:3], e_f[2][:].rearrange("p g e -> p (g e)")[:, 0:NCH], AX.X, ALU.min))
                link(v.scalar_tensor_tensor(e_f[2][:].rearrange("p g e -> p (g e)")[:, 0:NCH], chunk_id[:, 0:NCH], 1.0, mask[:, 0:NCH], ALU.add, ALU.mult))
                link(v.tensor_reduce(bnd[:, t, 1:2], e_f[2][:].rearrange("p g e -> p (g e)")[:, 0:NCH], AX.X, ALU.max))
                link(v.tensor_scalar(bnd[:, t, 0:1], small[:, 2:3], float(NCH), None, ALU.add))
            v.tensor_copy(bound[:], bnd[:]).then_inc(sem("bound_col"), 1)
            for t in range(SL_T):
                link(v.scalar_tensor_tensor(more[:, t:t + 1], bnd[:, t, 1:2], float(-SLOTS), bnd[:, t, 0:1], ALU.add, ALU.subtract))
            for t in range(SL_T):
                last = v.tensor_scalar(diag[:, 0, t, :], ident[:], bnd[:, t, 0:1], None, ALU.mult)
            last.then_inc(sem("first_diag"), 1)
            dve.wait_ge(sem("first_b"), 1)
            link(v.tensor_tensor(slot_key[:], bank[3][:, 0:NSL].rearrange("p (n a) -> p n a", a=1).broadcast_to([P, NSL, SLOTS]),
                                 slot_id[:].rearrange("p (a s) -> p a s", a=1).broadcast_to([P, NSL, SLOTS]), ALU.add))
            for g in range(CG):
                last = v.tensor_scalar(picked[:, g, :], slot_key[:].rearrange("p n s -> p (n s)"), part_id[:, g:g + 1], None, ALU.is_equal)
            last.then_inc(sem("picked"), 1)

            dve.wait_ge(sem("x_in"), 32)
            for t in range(NT):
                last = v.bn_stats(st[:, t, :], xa[:, t, :])
            link(last)
            for t in range(NT):
                last = v.bn_aggr(mv[:, t, :], st[:, t, :])
            link(last)
            v.tensor_scalar(rstd[:], mv[:, :, 1], 1e-5, None, ALU.add).then_inc(sem("var_ready"), 1)

            dve.wait_ge(inputs, INPUTS)
            for t in range(DT):
                link(v.tensor_reduce(small[:, t:t + 1], w1n[:, t, :], AX.X, ALU.add, apply_absolute_value=True))
            link(v.tensor_reduce(small[:, 2:4], b1_col[:].rearrange("p (t a) -> p t a", a=1), AX.X, ALU.add, apply_absolute_value=True))
            link(v.scalar_tensor_tensor(small[:, 4:6], small[:, 0:2], 16.0, small[:, 2:4], ALU.mult, ALU.add))
            link(v.tensor_scalar(smalli[:, 0:2], small[:, 4:6].bitcast(I32), 0xFF << 23, None, ALU.bitwise_and))
            link(v.tensor_scalar(smalli[:, 0:2], smalli[:, 0:2], float(20 << 23), None, ALU.max))
            link(v.tensor_scalar(smalli[:, 2:4], smalli[:, 0:2], -1.0, float(268 << 23), ALU.mult, ALU.add))
            link(v.tensor_scalar(smalli[:, 4:6], smalli[:, 0:2], float(-(14 << 23)), None, ALU.add))
            sc = smalli[:].bitcast(F32)
            for t in range(DT):
                link(v.tensor_scalar(w1n[:, t, :], w1n[:, t, :], sc[:, 2 + t:3 + t], None, ALU.mult))
                link(v.tensor_scalar(small[:, 6 + t:7 + t], b1_col[:, t:t + 1], sc[:, 2 + t:3 + t], None, ALU.mult))
            for t in range(DT):
                for h in range(DT):
                    if h == t:
                        link(v.tensor_scalar(b1_diag[:, t, h * P:(h + 1) * P], ident[:], small[:, 6 + t:7 + t], None, ALU.mult))
                    else:
                        link(v.memset(b1_diag[:, t, h * P:(h + 1) * P], 0.0))
            link(v.memset(ones_h[:], 1.0))
            link(v.tensor_copy(ones_r[:], ones_h[:]))
            v.memset(b1_rows[:].bitcast(F32), 0.0).then_inc(sem("w1_scaled"), 1)
            v.tensor_tensor(gate_bias[:, 0:4], bih_col[:, 0:4], bhh_col[:, 0:4], ALU.add)
            v.tensor_copy(gate_bias[:, 4:6], bih_col[:, 4:6])
            v.tensor_copy(hn_bias[:], bhh_col[:, 4:6])

            dve.wait_ge(sem("rstd_ready"), 1)
            for t in range(NT):
                v.tensor_scalar(xa[:, t, :], xa[:, t, :], mv[:, t, 0:1], rstd[:, t:t + 1], ALU.subtract, ALU.mult)\
                 .then_inc(sem("x_norm"), 1)

            dve.wait_ge(sem("w_hi"), 1)
            v.tensor_tensor(w1t[1][:], bank[4][:].rearrange("p (t j) -> p t j", t=DT), w1t[0][:].bitcast(F32), ALU.subtract).then_inc(sem("w_lo"), 1)
            dve.wait_ge(sem("w_tr"), 2)
            v.tensor_copy(b1_rows[0:1, :], bank[5][0:1, 0:D])
            link(v.tensor_copy(b1_rows[32:33, :], bank[5][32:33, 0:D]))
            v.tensor_tensor(b1_rows[32:33, :], bank[5][32:33, 0:D], b1_rows[32:33, :].bitcast(F32), ALU.subtract).then_inc(sem("b1_done"), 1)
            for j in range(4):
                t, c = j // 2, j % 2
                dve.wait_ge(sem("w_tr"), 3 + j)
                v.tensor_copy(wit[:, t, c * 384:(c + 1) * 384], bank[6 + j % 2][:, 0:384]).then_inc(sem("wit_ready"), 1)
            for j in range(4):
                t, c = j // 2, j % 2
                dve.wait_ge(sem("w_hi"), 2 + j)
                v.tensor_tensor(wht[1][:, t, c * 384:(c + 1) * 384], bank[j % 2][:, 0:384],
                                wht[0][:, t, c * 384:(c + 1) * 384].bitcast(F32), ALU.subtract).then_inc(sem("w_lo"), 1)
            dve.wait_ge(sem("w_tr"), 11)
            v.tensor_copy(deg_w[:], bank[2][:, 0:GT])
            for j in range(4):
                t, c = j // 2, j % 2
                dve.wait_ge(sem("w_tr"), 12 + j)
                if j:
                    dve.wait_ge(sem("w_lo"), 5 + j)
                ins = v.tensor_scalar(e_f[2][:].rearrange("p g e -> p (g e)")[:, 0:384], bank[4 + j % 2][:, 0:384], sc[:, 4 + t:5 + t], None, ALU.mult)
                ins.then_inc(sem("wc_scaled"), 1)
                dve.wait_ge(sem("w_hi"), 6 + j)
                v.tensor_tensor(wct[1][:, t, c * 384:(c + 1) * 384], e_f[2][:].rearrange("p g e -> p (g e)")[:, 0:384],
                                wct[0][:, t, c * 384:(c + 1) * 384].bitcast(F32), ALU.subtract).then_inc(sem("w_lo"), 1)
            dve.wait_ge(sem("slot_sums"), 1)
            half_n = NSL // 2
            for h in range(2):
                v.tensor_tensor(slot_key[:, h * half_n:(h + 1) * half_n, :], bank[2 + h][:, 0:half_n * SLOTS].rearrange("p (n s) -> p n s", s=SLOTS),
                                slice_off[:, h * half_n:(h + 1) * half_n].rearrange("p (n a) -> p n a", a=1).broadcast_to([P, half_n, SLOTS]), ALU.subtract)
            for h in range(2):
                last = v.tensor_copy(slot_row[:, h * half_n:(h + 1) * half_n, :], bank[h][:, 0:half_n * SLOTS].rearrange("p (n s) -> p n s", s=SLOTS))
            last.then_inc(sem("slot_tables"), 1)
            for u in range(USES):
                m = min(2, NT - 2 * u) * P
                dve.wait_ge(sem("xt_hi"), u + 1)
                ins = v.tensor_tensor(x_lo[:, :, 2 * P * u:2 * P * u + m],
                                      bank[6 + u % 2][:, 0:DT * m].rearrange("p (t n) -> p t n", t=DT),
                                      x_hi[:, :, 2 * P * u:2 * P * u + m].bitcast(F32), ALU.subtract)
                ins.then_inc(*((sem("xt_lo"), 1) if u < USES - 1 else (sem("state_lo"), NW)))

            dve.wait_ge(sem("slot_tables"), 1)
            with dve.Fori(0, TURNS) as i:
                dve.wait_ge(sem("hots_full"), GROUP * i + GROUP)
                v.tensor_copy(turn_row[:], slot_row[:].rearrange("p a b -> p (a b)")[:, bass.ds(i * TURN_SLOTS, TURN_SLOTS)])
                v.tensor_copy(turn_key[:], slot_key[:].rearrange("p a b -> p (a b)")[:, bass.ds(i * TURN_SLOTS, TURN_SLOTS)]).then_inc(sem("turn_key"), 1)
                dve.wait_ge(sem("turn_key"), i + 1)
                for b in range(GROUP):
                    dve.wait_ge(sem("hot_free"), GROUP * i + (b + 1))
                    for s in range(SLOTS):
                        k = (b % 2) * SLOTS + s
                        v.tensor_scalar(hot_row[k][:], iota_row[:], turn_row[:, b * SLOTS + s:b * SLOTS + s + 1], None, ALU.is_equal)
                        last = v.tensor_scalar(hot_key[k][:], iota_key[:], turn_key[:, b * SLOTS + s:b * SLOTS + s + 1], None, ALU.is_equal)
                    last.then_inc(sem("hots_full"), 1)

            dve.wait_ge(sem("stage_full"), NSL + GROUP)
            link(v.tensor_reduce(more[:, SL_T:SL_T + 1], over[:], AX.X, ALU.max))
            link(v.tensor_reduce(more[:, SL_T + 1:SL_T + 2], more[:, 0:SL_T + 1], AX.X, ALU.max))
            v.tensor_scalar(more[:, SL_T + 1:SL_T + 2], more[:, SL_T + 1:SL_T + 2], 0.0, None, ALU.max).then_inc(sem("more"), 1)
            dve.wait_ge(sem("bound_in"), 16)
            for w in range(NW):
                dve.wait_ge(sem("deg_sum"), w + 1)
                v.tensor_copy(degree[:, WIN_COL[w]:WIN_COL[w] + WIN_LEN[w]], bank[4 + w % 4][:, 0:WIN_LEN[w]]).then_inc(sem("deg_done"), 1)

            dve.wait_ge(sem("slow_sum"), 1)
            v.tensor_scalar(slow_flag[:], bank[3][0:1, 0:1], 1.0, None, ALU.min).then_inc(sem("slow_flag"), 1)
            slow = if_slow(dve)
            with dve.If(slow > 0):
                v.memset(hot_key[1][:], 0.0).then_inc(sem("zero_key"), 1)
                taken = dve.alloc_register("dve_taken")
                dve.reg_mov(taken, 0)
                with dve.Fori(0, NSL) as sl:
                    first = dve.value_load(bound_row[0:1, bass.ds(2 * sl, 1)], min_val=0, max_val=NCH)
                    end = dve.value_load(bound_row[0:1, bass.ds(2 * sl + 1, 1)], min_val=0, max_val=NCH)
                    with dve.Fori(first, end) as c:
                        dve.wait_ge(sem("chunk_used"), dve.snap(taken) + 1)
                        v.tensor_scalar(hot_row[0][:], iota_row[:], row_t[:, bass.ds(c, 1)], None, ALU.is_equal)
                        v.tensor_scalar(hot_key[0][:], iota_key[:], slice_off[:, bass.ds(sl, 1)], key_t[:, bass.ds(c, 1)],
                                        ALU.add, ALU.is_equal).then_inc(sem("chunk_hot"), 1)
                        dve.reg_add(taken, taken, 1)
                for w in range(NW):
                    dve.wait_ge(sem("exact_deg_sum"), w + 1)
                    v.tensor_copy(degree[:, WIN_COL[w]:WIN_COL[w] + WIN_LEN[w]], bank[4 + w % 4][:, 0:WIN_LEN[w]]).then_inc(sem("exact_deg_done"), 1)
                dve.wait_ge(sem("exact_deg_done"), NW)
                dve.wait_ge(sem("exact_stored"), EXACT_STORED)
            v.memset(x_new[:, 0, 0:2], 0.0).then_inc(sem("gate_ops"), LEAD)
            dve.wait_ge(sem("deg_done"), NW)
            dve.wait_ge(sem("gate_ops"), LEAD)

            def relu_lo(g, u):
                m = min(2, NT - 2 * u)
                dve.wait_ge(sem("relu_hi"), g + 1)
                v.scalar_tensor_tensor(r_lo[:, 2 * u:2 * u + m, :].rearrange("p t d -> p (t d)"), bank[2 + u % 2][:, 0:m * D], 0.0,
                                       r_hi[:, 2 * u:2 * u + m, :].rearrange("p t d -> p (t d)"), ALU.max, ALU.subtract)\
                 .then_inc(sem("relu_lo"), 1)

            def msg_lo(s, w):
                for f in range(DT):
                    n = WIN_LEN[w]
                    dve.wait_ge(sem("msg_hi"), half(s, w, f) + 1)
                    v.tensor_tensor(m_lo[:, f, 0:n], bank[2 * (w % 2) + f][:, 0:n], m_hi[:, f, 0:n].bitcast(F32), ALU.subtract)\
                     .then_inc(sem("msg_lo"), 1)

            def gates(s, w, f):
                n, c0 = WIN_LEN[w], WIN_COL[w]
                h = dve.snap(half(s, w, f)) if not isinstance(s, int) else half(s, w, f)
                mine = h * GATE_OPS + LEAD
                mine = dve.snap(mine) if not isinstance(s, int) else mine
                theirs = h * 3
                full = h * 4
                dg = degree[:, c0:c0 + n]
                a, z, xn = gate_a[:, 0:n], gate_z[:, 0:n], x_new[:, f, 0:n]

                def op(ins):
                    ins.then_inc(sem("gate_ops"), 1)

                dve.wait_ge(sem("gate_ops"), mine)
                dve.wait_ge(sem("gate_sums"), full + 1)
                op(v.scalar_tensor_tensor(a, dg, deg_w[:, f:f + 1], bank[4][:, 0:n], ALU.mult, ALU.add))
                dve.wait_ge(sem("gate_sums"), full + 2)
                op(v.scalar_tensor_tensor(z, dg, deg_w[:, 2 + f:3 + f], bank[5][:, 0:n], ALU.mult, ALU.add))
                dve.wait_ge(sem("gate_sums"), full + 3)
                dve.wait_ge(sem("gate_acts"), theirs + 1)
                op(v.scalar_tensor_tensor(a, bank[6][:, 0:n], hn_bias[:, f:f + 1], a, ALU.add, ALU.mult))
                dve.wait_ge(sem("gate_sums"), full + 4)
                dve.wait_ge(sem("gate_ops"), mine + 3)
                op(v.tensor_tensor(a, bank[7][:, 0:n], a, ALU.add))
                dve.wait_ge(sem("gate_ops"), mine + 4)
                op(v.scalar_tensor_tensor(a, dg, deg_w[:, 4 + f:5 + f], a, ALU.mult, ALU.add))
                dve.wait_ge(sem("gate_acts"), theirs + 3)
                op(v.tensor_tensor(xn, x_hi[:, f, c0:c0 + n].bitcast(F32), a, ALU.subtract))
                dve.wait_ge(sem("gate_ops"), mine + 6)
                op(v.tensor_tensor(xn, xn, x_lo[:, f, c0:c0 + n].bitcast(F32), ALU.add))
                dve.wait_ge(sem("gate_ops"), mine + 7)
                op(v.tensor_tensor(xn, xn, z, ALU.mult))
                dve.wait_ge(sem("gate_ops"), mine + 8)
                op(v.tensor_tensor(xn, xn, a, ALU.add))

            def state_lo(s, w):
                n, c0 = WIN_LEN[w], WIN_COL[w]
                dve.wait_ge(sem("state_hi"), NW * s + w + 1)
                v.tensor_tensor(x_lo[:, :, c0:c0 + n], x_new[:, :, 0:n], x_hi[:, :, c0:c0 + n].bitcast(F32), ALU.subtract)\
                 .then_inc(sem("state_lo"), 1)

            for u in range(FILL_B):
                relu_lo(u, u)
            with dve.Fori(0, STEPS) as s:
                for u in range(FILL_B, USES):
                    relu_lo(USES * s + u, u)
                msg_lo(s, 0)
                for w in range(1, NW):
                    gates(s, w - 1, 0)
                    msg_lo(s, w)
                    gates(s, w - 1, 1)
                    state_lo(s, w - 1)
                for u in range(FILL_A):
                    relu_lo(USES * s + USES + u, u)
                gates(s, NW - 1, 0)
                for u in range(FILL_A, FILL_B):
                    relu_lo(USES * s + USES + u, u)
                gates(s, NW - 1, 1)
                state_lo(s, NW - 1)

            dve.wait_ge(sem("state_lo"), NW * (STEPS + 1))
            dve.wait_ge(sem("relu_lo"), USES * STEPS + FILL_B)
            link(v.tensor_copy(ident_r[:], ident[:]))
            v.tensor_copy(ident_r[:], ident[:]).then_inc(sem("ident_r"), 1)
            dve.wait_ge(sem("x_again"), 32)
            for u in range(USES):
                m = min(2, NT - 2 * u)
                dve.wait_ge(sem("rows"), u + 1)
                xs = x1[:, 2 * u:2 * u + m, :].rearrange("p t d -> p (t d)")
                v.tensor_tensor(xs, xs, bank[u % 2][:, 0:m * D], ALU.add).then_inc(sem("x1_sum"), 1)
            dve.wait_ge(sem("x1_sum"), USES)
            for t in range(NT):
                last = v.bn_stats(st2[:, t, :], x1[:, t, :])
            link(last)
            for t in range(NT):
                last = v.bn_aggr(mv2[:, t, :], st2[:, t, :])
            link(last)
            v.tensor_scalar(rstd2[:], mv2[:, :, 1], 1e-5, None, ALU.add).then_inc(sem("var_ready"), 1)
            dve.wait_ge(sem("rstd_ready"), 2)
            dve.wait_ge(sem("x1_out"), 16)
            for t in range(NT):
                v.tensor_scalar(x1[:, t, :], x1[:, t, :], mv2[:, t, 0:1], rstd2[:, t:t + 1], ALU.subtract, ALU.mult)\
                 .then_inc(sem("x1_norm"), 1)
            for u in range(USES):
                m = min(2, NT - 2 * u) * P
                dve.wait_ge(sem("x2t_hi"), u + 1)
                v.tensor_tensor(x_lo[:, :, 2 * P * u:2 * P * u + m],
                                bank[2 + u % 2][:, 0:DT * m].rearrange("p (t n) -> p t n", t=DT),
                                x_hi[:, :, 2 * P * u:2 * P * u + m].bitcast(F32), ALU.subtract).then_inc(sem("x2t_lo"), 1)
            dve.wait_ge(sem("gate_in"), 64)
            dve.wait_ge(sem("x2t_lo"), USES)
            link(v.tensor_copy(wg_r[0][:], wg[:]))
            v.tensor_tensor(wg_r[1][:], wg[:], wg_r[0][:].bitcast(F32), ALU.subtract).then_inc(sem("wg_split"), 1)
            dve.wait_ge(sem("hid_bias_t"), 1)
            link(v.tensor_copy(hid_bias[:], bank[5][:, 0:BLOCKS]))
            dve.wait_ge(sem("logits"), 1)
            dve.wait_ge(sem("iotas"), 8)
            lg = bank[4][:, 0:NT * NX].rearrange("p (t e) -> p t e", e=NX)

            def over_tiles(row):
                return row[:].rearrange("p (a e) -> p a e", a=1).broadcast_to([P, NT, NX])

            def over_experts(k):
                return top[:, k, :].rearrange("p (t a) -> p t a", a=1).broadcast_to([P, NT, NX])

            link(v.tensor_tensor(logit[:], lg, bg_b[:, 0:1, :].broadcast_to([P, NT, NX]), ALU.add))
            link(v.tensor_tensor(logit[:], logit[:], bg_b[:, 1:2, :].broadcast_to([P, NT, NX]), ALU.add))
            for k, hot_k in enumerate((hot1, hot2)):
                link(v.tensor_reduce(top[:, k, :], logit[:], AX.X, ALU.max))
                link(v.tensor_tensor(cand[:], logit[:], over_experts(k), ALU.is_equal))
                link(v.tensor_scalar(cand[:], cand[:], float(-NX), float(NX), ALU.mult, ALU.add))
                link(v.tensor_tensor(cand[:], cand[:], eid[:], ALU.add))
                link(v.tensor_reduce(top[:, 4, :], cand[:], AX.X, ALU.min))
                link(v.tensor_tensor(hot_k[:], eid[:], over_experts(4), ALU.is_equal))
                if k == 0:
                    link(v.tensor_scalar(cand[:], hot_k[:], -3.0e38, None, ALU.mult))
                    link(v.tensor_tensor(logit[:], logit[:], cand[:], ALU.add))
            v.tensor_tensor(top[:, 2, :], top[:, 1, :], top[:, 0, :], ALU.subtract).then_inc(sem("top_diff"), 1)
            dve.wait_ge(sem("top_exp"), 1)
            link(v.tensor_scalar(top[:, 3, :], top[:, 2, :], 1.0, None, ALU.add))
            link(v.reciprocal(top[:, 4, :], top[:, 3, :]))
            link(v.tensor_tensor(top[:, 5, :], top[:, 2, :], top[:, 4, :], ALU.mult))
            link(v.tensor_tensor(hot1[:], hot1[:], over_experts(4), ALU.mult))
            link(v.tensor_tensor(hot2[:], hot2[:], over_experts(5), ALU.mult))
            v.tensor_tensor(hot1[:], hot1[:], hot2[:], ALU.add).then_inc(sem("combine"), 1)
            for c in range(CHUNKS):
                dve.wait_ge(sem("chunk_hi"), c + 1)
                hi, lo = chunk_dst(c)
                src_ = raw[c % 4][:] if c % 4 < DT else raw[c % 4][:].rearrange("p (t d) -> p t d", t=2)
                v.tensor_tensor(lo, src_, hi.bitcast(F32), ALU.subtract).then_inc(sem("chunk_lo"), 1)
                if c == 3:
                    dve.wait_ge(sem("comb_tr"), (NT + 3) // 4)
                    for g in range((NT + 3) // 4):
                        n = min(4, NT - 4 * g) * P
                        c0 = 0 if g < 6 else P
                        last = v.tensor_copy(comb_t[:, g * 512:g * 512 + n], bank[COMB_BANK[g]][0:NX, c0:c0 + n])
                    last.then_inc(sem("comb_sb"), 1)

            dve.wait_ge(sem("chunk_lo"), CHUNKS)
            dve.wait_ge(sem("comb_out"), 16)
            with dve.Fori(0, FN) as w:
                for i in range(BLOCKS):
                    n = BLOCKS * w + i
                    b, e = i % 2, i // HT
                    if i % HT == 0:
                        dve.wait_ge(sem(f"comb_in{e % 4}"), 32 * w + 16 * (e // 4 + 1))
                    dve.wait_ge(sem("h_relu"), n + 1)
                    v.tensor_tensor(act_h[b][:], act_h[b][:], comb_b[e % 4][:], ALU.mult).then_inc(sem("h_scaled"), 1)
                    dve.wait_ge(sem("h_hi"), n + 1)
                    v.tensor_tensor(h_lo[b][:], act_h[b][:], h_hi[b][:].bitcast(F32), ALU.subtract).then_inc(sem("h_lo"), 1)
                dve.wait_ge(sem("x1_in"), 16 * (w + 1))
                for j in range(PIECES // 2):
                    dve.wait_ge(sem("y_turned"), (PIECES // 2) * w + j + 1)
                    ys = y_rows[:, 2 * j:2 * j + 2, :].rearrange("p t d -> p (t d)")
                    v.tensor_tensor(ys, ys, bank[6 + j][0:FP, :], ALU.add).then_inc(sem("y_ready"), 1)

        @block.scalar
        def _(act):
            a = nc.scalar
            act.wait_ge(sem("w_tr"), 1)
            a.activation(w1t[0][:], bank[4][:].rearrange("p (t j) -> p t j", t=DT), ACT.Copy).then_inc(sem("w_hi"), 1)
            for j in range(4):
                t, c = j // 2, j % 2
                act.wait_ge(sem("w_tr"), 7 + j)
                a.activation(wht[0][:, t, c * 384:(c + 1) * 384], bank[j % 2][:, 0:384], ACT.Copy).then_inc(sem("w_hi"), 1)
            for j in range(4):
                t, c = j // 2, j % 2
                act.wait_ge(sem("wc_scaled"), 1 + j)
                a.activation(wct[0][:, t, c * 384:(c + 1) * 384], e_f[2][:].rearrange("p g e -> p (g e)")[:, 0:384], ACT.Copy).then_inc(sem("w_hi"), 1)
            for u in range(USES):
                m = min(2, NT - 2 * u) * P
                act.wait_ge(sem("xt"), u + 1)
                a.activation(x_hi[:, :, 2 * P * u:2 * P * u + m], bank[6 + u % 2][:, 0:DT * m].rearrange("p (t n) -> p t n", t=DT),
                             ACT.Copy).then_inc(sem("xt_hi"), 1)
            with act.Fori(0, TURNS) as i:
                for b in range(GROUP):
                    act.wait_ge(sem("slice_full"), GROUP * i + (b + 1))
                    if b % 2 == 0:
                        act.wait_ge(sem("stage_free"), 2 * i + (b // 2 + 1))
                    a.activation(trash[b][:], bank[b][:, 0:NT * SW], ACT.Relu, bias=minus_exact[:, 0:1],
                                 accum_out=over[:, bass.ds(GROUP * i + b, 1)])
                    a.activation(stage[b // 2][:, :, (b % 2) * SW:(b % 2 + 1) * SW], bank[b][:, 0:NT * SW].rearrange("p (q c) -> p q c", c=SW),
                                 ACT.Copy, saturate=False).then_inc(sem("stage_full"), 1)

            slow = if_slow(act)
            with act.If(slow > 0):
                with act.Fori(0, NSL) as sl:
                    act.wait_ge(sem("exact_full"), sl + 1)
                    act.wait_ge(sem("exact_stored"), 32 * sl + 1)
                    a.activation(exact_sum, bank[0][:, 0:NT * SW], ACT.Copy)
                    a.activation(exact_part[0][:], bank[0][:, 0:NT * SW], ACT.Copy).then_inc(sem("exact_hi"), 1)
                act.wait_ge(sem("exact_deg_sum"), NW)
                act.wait_ge(sem("exact_stored"), EXACT_STORED)
            act.wait_ge(sem("deg_done"), NW)

            def relu_hi(g, u):
                m = min(2, NT - 2 * u)
                act.wait_ge(sem("relu_sums"), g + 1)
                a.activation(r_hi[:, 2 * u:2 * u + m, :].rearrange("p t d -> p (t d)"), bank[2 + u % 2][:, 0:m * D], ACT.Relu)\
                 .then_inc(sem("relu_hi"), 1)

            def msg_hi(s, w):
                n = WIN_LEN[w]
                if w:
                    act.wait_ge(sem("gate_sums"), half(s, w, 0) * 4)
                for f in range(DT):
                    act.wait_ge(sem("msg_sums"), half(s, w, f) + 1)
                    a.activation(m_hi[:, f, 0:n], bank[2 * (w % 2) + f][:, 0:n], ACT.Copy).then_inc(sem("msg_hi"), 1)

            def gates(s, w, f):
                n = WIN_LEN[w]
                mine = half(s, w, f) * 3
                theirs = half(s, w, f) * GATE_OPS + LEAD
                act.wait_ge(sem("gate_ops"), theirs + 1)
                a.activation(gate_a[:, 0:n], gate_a[:, 0:n], ACT.Sigmoid, bias=gate_bias[:, f:f + 1]).then_inc(sem("gate_acts"), 1)
                act.wait_ge(sem("gate_ops"), theirs + 2)
                a.activation(gate_z[:, 0:n], gate_z[:, 0:n], ACT.Sigmoid, bias=gate_bias[:, 2 + f:3 + f]).then_inc(sem("gate_acts"), 1)
                act.wait_ge(sem("gate_ops"), theirs + 5)
                a.activation(gate_a[:, 0:n], gate_a[:, 0:n], ACT.Tanh, bias=gate_bias[:, 4 + f:5 + f]).then_inc(sem("gate_acts"), 1)

            def state_hi(s, w):
                n, c0 = WIN_LEN[w], WIN_COL[w]
                act.wait_ge(sem("gate_ops"), half(s, w, 2) * GATE_OPS + LEAD)
                a.activation(x_hi[:, :, c0:c0 + n], x_new[:, :, 0:n], ACT.Copy).then_inc(sem("state_hi"), 1)

            for u in range(FILL_B):
                relu_hi(u, u)
            with act.Fori(0, STEPS) as s:
                for u in range(FILL_B, USES):
                    relu_hi(USES * s + u, u)
                msg_hi(s, 0)
                for w in range(1, NW):
                    gates(s, w - 1, 0)
                    msg_hi(s, w)
                    gates(s, w - 1, 1)
                    state_hi(s, w - 1)
                for u in range(FILL_A):
                    relu_hi(USES * s + USES + u, u)
                gates(s, NW - 1, 0)
                for u in range(FILL_A, FILL_B):
                    relu_hi(USES * s + USES + u, u)
                gates(s, NW - 1, 1)
                state_hi(s, NW - 1)

            for u in range(USES):
                m = min(2, NT - 2 * u) * P
                act.wait_ge(sem("x2t"), u + 1)
                a.activation(x_hi[:, :, 2 * P * u:2 * P * u + m], bank[2 + u % 2][:, 0:DT * m].rearrange("p (t n) -> p t n", t=DT),
                             ACT.Copy).then_inc(sem("x2t_hi"), 1)
            act.wait_ge(sem("top_diff"), 1)
            a.activation(top[:, 2, :], top[:, 2, :], ACT.Exp).then_inc(sem("top_exp"), 1)
            for c in range(CHUNKS):
                act.wait_ge(sem(f"chunk_in{c % 4}"), 16 * (c // 4 + 1))
                hi, lo = chunk_dst(c)
                src_ = raw[c % 4][:] if c % 4 < DT else raw[c % 4][:].rearrange("p (t d) -> p t d", t=2)
                a.activation(hi, src_, ACT.Copy).then_inc(sem("chunk_hi"), 1)
            act.wait_ge(sem("chunk_lo"), CHUNKS)
            act.wait_ge(sem("comb_out"), 16)
            with act.Fori(0, FN) as w:
                for i in range(BLOCKS + 1):
                    n = BLOCKS * w + i
                    if i < BLOCKS:
                        act.wait_ge(sem("h_sums"), n + 1)
                        if i >= 2:
                            act.wait_ge(sem("h_lo"), BLOCKS * w + (i - 1))
                        a.activation(act_h[i % 2][:], bank[i % 4][:, 0:FW], ACT.Relu, bias=hid_bias[:, i:i + 1]).then_inc(sem("h_relu"), 1)
                    if i >= 1:
                        b = (i - 1) % 2
                        act.wait_ge(sem("h_scaled"), n)
                        if i >= 3:
                            act.wait_ge(sem("y_sums"), BLOCKS * w + (i - 2))
                        a.activation(h_hi[b][:], act_h[b][:], ACT.Copy).then_inc(sem("h_hi"), 1)
                act.wait_ge(sem("y_full"), w + 1)
                for f in range(DT):
                    last = a.activation(y_t[:, f, :], bank[4 + f][:, 0:FW], ACT.Copy)
                last.then_inc(sem("y_t"), 1)

        @block.tensor
        def _(pe):
            mm = nc.tensor.matmul
            pe.wait_ge(sem("ident_ready"), 1)
            pe.wait_ge(sem("keys"), 1)
            for g in range(CG):
                for i in range(2):
                    last = nc.tensor.transpose(bank[i][:, g * P:(g + 1) * P], e_f[i][:, g, :], ident[:])
            last.then_inc(sem("keys_t"), 1)
            pe.wait_ge(sem("diags"), 1)
            pe.wait_ge(sem("ones_ready"), 1)
            for m in range(2):
                for g in range(CG):
                    last = mm(bank[2 + m][:, g * P:(g + 1) * P], ones_f[:], diag[:, m, g, :], start=True, stop=True)
            last.then_inc(sem("lims_b"), 1)
            pe.wait_ge(sem("first_diag"), 1)
            for t in range(SL_T):
                last = mm(bank[3][:, t * P:(t + 1) * P], ones_f[:], diag[:, 0, t, :], start=True, stop=True)
            last.then_inc(sem("first_b"), 1)
            pe.wait_ge(sem("w1_scaled"), 1)
            for t in range(DT):
                for h in range(DT):
                    last = nc.tensor.transpose(bank[4][:, t * D + h * P:t * D + (h + 1) * P], w1n[:, h, t * P:(t + 1) * P], ident[:])
            last.then_inc(sem("w_tr"), 1)
            for t in range(DT):
                last = mm(bank[5][:, 0:D], ones_f[:], b1_diag[:, t, :], start=t == 0, stop=t == DT - 1)
            last.then_inc(sem("w_tr"), 1)
            for j in range(4):
                t, c = j // 2, j % 2
                if j >= 2:
                    pe.wait_ge(sem("wit_ready"), j - 1)
                for o in range(3):
                    last = nc.tensor.transpose(bank[6 + j % 2][:, o * P:(o + 1) * P], win[:, 3 * c + o, t * P:(t + 1) * P], ident[:])
                last.then_inc(sem("w_tr"), 1)
            pe.wait_ge(sem("edge_table"), 1)
            for j in range(4):
                t, c = j // 2, j % 2
                if j >= 2:
                    pe.wait_ge(sem("w_lo"), j)
                for o in range(3):
                    last = nc.tensor.transpose(bank[j % 2][:, o * P:(o + 1) * P], whn[:, 3 * c + o, t * P:(t + 1) * P], ident[:])
                last.then_inc(sem("w_tr"), 1)
            pe.wait_ge(sem("wit_ready"), 4)
            pe.wait_ge(sem("bound_col"), 1)
            for o in range(GT):
                for t in range(DT):
                    last = mm(bank[2][:, o:o + 1], wit[:, t, o * P:(o + 1) * P], b2_col[:, t:t + 1], start=t == 0, stop=t == DT - 1)
            last.then_inc(sem("w_tr"), 1)
            for j in range(4):
                t, c = j // 2, j % 2
                if j == 0:
                    pe.wait_ge(sem("w_lo"), 1)
                    pe.wait_ge(sem("b1_done"), 1)
                if j >= 2:
                    pe.wait_ge(sem("wc_scaled"), j - 1)
                for m in range(DT):
                    last = mm(bank[4 + j % 2][:, 0:384], w2n[:, m, t * P:(t + 1) * P], wit[:, m, c * 384:(c + 1) * 384],
                              start=m == 0, stop=m == DT - 1)
                last.then_inc(sem("w_tr"), 1)
            pe.wait_ge(sem("picked"), 1)
            pe.wait_ge(sem("w_lo"), 6)
            half_n = NSL // 2 * SLOTS
            for i in range(2):
                for h in range(2):
                    for g in range(CG):
                        last = mm(bank[(2 - 2 * i) + h][:, 0:half_n], e_f[i][:, g, :], picked[:, g, h * half_n:(h + 1) * half_n],
                                  start=g == 0, stop=g == CG - 1)
            last.then_inc(sem("slot_sums"), 1)
            for u in range(USES):
                m = min(2, NT - 2 * u)
                pe.wait_ge(sem("x_norm"), 2 * u + m)
                if u >= 2:
                    pe.wait_ge(sem("xt_lo"), u - 1)
                for t in range(DT):
                    for k in range(m):
                        last = nc.tensor.transpose(bank[6 + u % 2][:, (t * m + k) * P:(t * m + k + 1) * P],
                                                   xa[:, 2 * u + k, t * P:(t + 1) * P], ident[:])
                last.then_inc(sem("xt"), 1)

            pe.wait_ge(sem("w_lo"), 9)
            pe.wait_ge(sem("slot_tables"), 1)
            for name, n in (("stage_full", 4), ("hot_free", 2), ("hots_full", GROUP)):
                mm(bank[5][:, 0:2], ones_h[:], ones_h[:, 0:2], start=True, stop=True).then_inc(sem(name), n)
            with pe.Fori(0, TURNS) as i:
                for b in range(GROUP):
                    pe.wait_ge(sem("stage_full"), GROUP * i + (b + 1))
                    pe.wait_ge(sem("hots_full"), GROUP * i + (b + GROUP + 1))
                    for s in range(SLOTS):
                        k = (b % 2) * SLOTS + s
                        ins = mm(bank[b][:, 0:NT * SW], hot_row[k][:], hot_key[k][:], start=s == 0, stop=s == SLOTS - 1)
                    ins.then_inc(sem("slice_full"), 1)
                    mm(bank[5][:, 0:2], ones_h[:], ones_h[:, 0:2], start=True, stop=True).then_inc(sem("hot_free"), 1)
            pe.wait_ge(sem("stage_free"), 2 * TURNS + 2)
            pe.wait_ge(sem("state_lo"), NW)
            for w in range(NW):
                if w >= 4:
                    pe.wait_ge(sem("deg_done"), w - 3)
                for q in range(NT):
                    last = mm(bank[4 + w % 4][:, 0:WIN_LEN[w]], ones_h[:], adj[:, q, WIN_COL[w]:WIN_COL[w] + WIN_LEN[w]],
                              start=q == 0, stop=q == NT - 1)
                last.then_inc(sem("deg_sum"), 1)
            pe.wait_ge(sem("more"), 1)
            mm(bank[3][0:1, 0:1], more[:, SL_T + 1:SL_T + 2], ones_f[:, 0:1], start=True, stop=True).then_inc(sem("slow_sum"), 1)
            pe.wait_ge(sem("deg_done"), NW)
            slow = if_slow(pe)
            with pe.If(slow > 0):
                for name in ("exact_stored", "exact_hi", "chunk_used"):
                    mm(bank[5][:, 0:2], ones_h[:], ones_h[:, 0:2], start=True, stop=True).then_inc(sem(name), 1)
                taken = pe.alloc_register("pe_taken")
                pe.reg_mov(taken, 0)
                pe.wait_ge(sem("zero_key"), 1)
                with pe.Fori(0, NSL) as sl:
                    first = pe.value_load(bound_row[0:1, bass.ds(2 * sl, 1)], min_val=0, max_val=NCH)
                    end = pe.value_load(bound_row[0:1, bass.ds(2 * sl + 1, 1)], min_val=0, max_val=NCH)
                    pe.wait_ge(sem("exact_hi"), sl + 1)
                    mm(bank[0][:, 0:NT * SW], ones_h[:], hot_key[1][:], start=True, stop=True, skip_group_check=True)
                    with pe.Fori(first, end) as c:
                        pe.wait_ge(sem("chunk_hot"), pe.snap(taken) + 1)
                        mm(bank[0][:, 0:NT * SW], hot_row[0][:], hot_key[0][:], start=False, stop=True, skip_group_check=True)\
                            .then_inc(sem("chunk_used"), 1)
                        pe.reg_add(taken, taken, 1)
                    mm(bank[5][:, 0:2], ones_h[:], ones_h[:, 0:2], start=True, stop=True).then_inc(sem("exact_full"), 1)
                for w in range(NW):
                    pe.wait_ge(sem("planes_in"), 32 * (w + 1))
                    if w >= 4:
                        pe.wait_ge(sem("exact_deg_done"), w - 3)
                    for q in range(NT):
                        for i in range(2):
                            last = mm(bank[4 + w % 4][:, 0:WIN_LEN[w]], ones_h[:], planes[:, i, q, 0:WIN_LEN[w]],
                                      start=q == 0 and i == 0, stop=q == NT - 1 and i == 1)
                    last.then_inc(sem("exact_deg_sum"), 1)
                pe.wait_ge(sem("exact_deg_done"), NW)

            def relu_sum(t, u):
                m = min(2, NT - 2 * u)
                if not isinstance(t, int) or u >= 2:
                    pe.wait_ge(sem("relu_lo"), USES * t + max(u - 1, 0))
                pe.wait_ge(sem("state_lo"), NW * t + USE_WIN[u] + 1)
                o = bank[2 + u % 2]
                for k in range(m):
                    last = mm(o[:, k * D:(k + 1) * D], ones_r[:], b1_rows[:], start=k == 0, stop=False, skip_group_check=True)
                for k in range(m):
                    n0 = (2 * u + k) * P
                    for t in range(DT):
                        for xs, ws in ((x_hi, w1t[0]), (x_hi, w1t[1]), (x_lo, w1t[0])):
                            last = mm(o[:, k * D:(k + 1) * D], xs[:, t, n0:n0 + P], ws[:, t, :], start=False,
                                      stop=True, skip_group_check=True)
                last.then_inc(sem("relu_sums"), 1)

            def messages(s, w, f, q0, q1, exact):
                n, c0 = WIN_LEN[w], WIN_COL[w]
                if exact:
                    pe.wait_ge(sem("planes_in"), (s + 1) * (32 * NW) + 32 * (w + 1))
                for q in range(q0, q1):
                    counts = [planes[:, i, q, 0:n] for i in range(2)] if exact else [adj[:, q, c0:c0 + n]]
                    todo = [(r, c) for c in counts for r in (r_hi, r_lo)]
                    for i, (r, c) in enumerate(todo):
                        last = mm(bank[2 * (w % 2) + f][:, 0:n], r[:, q, f * P:(f + 1) * P], c,
                                  start=q == 0 and i == 0, stop=q == NT - 1 and i == len(todo) - 1)
                if q1 == NT:
                    last.then_inc(sem("msg_sums"), 1)

            def gates(s, w, f):
                n, c0 = WIN_LEN[w], WIN_COL[w]
                pe.wait_ge(sem("gate_ops"), half(s, w, f) * GATE_OPS + 1)
                if f == 0:
                    pe.wait_ge(sem("msg_lo"), half(s, w, 2))
                for k, (b, parts) in enumerate(((4, (("h", f), ("m", f))), (5, (("h", 2 + f), ("m", 2 + f))),
                                                (6, (("h", 4 + f),)), (7, (("m", 4 + f),)))):
                    todo = []
                    for what, o in parts:
                        for t in range(DT):
                            if what == "h":
                                hi, lo, wt = x_hi[:, t, c0:c0 + n], x_lo[:, t, c0:c0 + n], wht
                            else:
                                hi, lo, wt = m_hi[:, t, 0:n], m_lo[:, t, 0:n], wct
                            wh, wl = (wt[i][:, t, o * P:(o + 1) * P] for i in range(2))
                            todo += [(wh, hi), (wh, lo), (wl, hi)]
                    for i, (wgt, mov) in enumerate(todo):
                        last = mm(bank[b][:, 0:n], wgt, mov, start=i == 0, stop=i == len(todo) - 1)
                    last.then_inc(sem("gate_sums"), 1)

            late = 2 * EARLY
            for u in range(FILL_B):
                relu_sum(0, u)

            def all_steps(exact):
                with pe.Fori(0, STEPS) as s:
                    for u in range(FILL_B, EARLY):
                        relu_sum(s, u)
                    pe.wait_ge(sem("relu_lo"), USES * s + EARLY)
                    mm(bank[0][:, 0:2], ones_r[:], b1_rows[:, 0:2], start=True, stop=True)
                    messages(s, 0, 0, 0, late, exact)
                    messages(s, 0, 1, 0, late, exact)
                    for u in range(EARLY, USES):
                        relu_sum(s, u)
                    pe.wait_ge(sem("relu_lo"), USES * s + USES)
                    mm(bank[3][:, 0:2], ones_r[:], b1_rows[:, 0:2], start=True, stop=True)
                    messages(s, 0, 0, late, NT, exact)
                    messages(s, 0, 1, late, NT, exact)
                    for w in range(1, NW):
                        messages(s, w, 0, 0, NT, exact)
                        gates(s, w - 1, 0)
                        messages(s, w, 1, 0, NT, exact)
                        gates(s, w - 1, 1)
                    for u in range(FILL_A):
                        relu_sum(s + 1, u)
                    gates(s, NW - 1, 0)
                    for u in range(FILL_A, FILL_B):
                        relu_sum(s + 1, u)
                    gates(s, NW - 1, 1)

            with pe.If(slow > 0):
                all_steps(True)
            with pe.If(slow < 1):
                all_steps(False)

            pe.wait_ge(sem("state_lo"), NW * (STEPS + 1))
            pe.wait_ge(sem("ident_r"), 1)
            pe.wait_ge(sem("relu_lo"), USES * STEPS + FILL_B)
            for u in range(USES):
                m = min(2, NT - 2 * u)
                if u >= 2:
                    pe.wait_ge(sem("x1_sum"), u - 1)
                for k in range(m):
                    n0 = (2 * u + k) * P
                    for t in range(DT):
                        for xs in (x_hi, x_lo):
                            last = mm(bank[u % 2][:, k * D + t * P:k * D + (t + 1) * P], xs[:, t, n0:n0 + P], ident_r[:],
                                      start=k == 0 and t == 0 and xs is x_hi, stop=True, skip_group_check=True)
                last.then_inc(sem("rows"), 1)
            for u in range(USES):
                m = min(2, NT - 2 * u)
                pe.wait_ge(sem("x1_norm"), 2 * u + m)
                if u >= 2:
                    pe.wait_ge(sem("x2t_lo"), u - 1)
                for t in range(DT):
                    for k in range(m):
                        last = nc.tensor.transpose(bank[2 + u % 2][:, (t * m + k) * P:(t * m + k + 1) * P],
                                                   x1[:, 2 * u + k, t * P:(t + 1) * P], ident[:])
                last.then_inc(sem("x2t"), 1)
            pe.wait_ge(sem("x2t_lo"), USES)
            pe.wait_ge(sem("wg_split"), 1)
            nc.tensor.transpose(bank[5][:, 0:BLOCKS], hid_bias_rows[:], ident[0:BLOCKS, 0:BLOCKS]).then_inc(sem("hid_bias_t"), 1)
            first_mm = True
            for t in range(NT):
                for k in range(DT):
                    for xs in (x_hi, x_lo):
                        for ws in wg_r:
                            last = mm(bank[4][:, t * NX:(t + 1) * NX], xs[:, k, t * P:(t + 1) * P], ws[:, k, :],
                                      start=first_mm, stop=True, skip_group_check=True)
                            first_mm = False
            last.then_inc(sem("logits"), 1)
            pe.wait_ge(sem("combine"), 1)
            for g in range((NT + 3) // 4):
                o = bank[COMB_BANK[g]]
                for k in range(min(4, NT - 4 * g)):
                    c = k if g < 6 else 1
                    last = nc.tensor.transpose(o[0:NX, c * P:(c + 1) * P], hot1[:, 4 * g + k, :], ident[:])
                last.then_inc(sem("comb_tr"), 1)
            pe.wait_ge(sem("comb_sb"), 1)
            pe.wait_ge(sem("out_bias_in"), 16)
            with pe.Fori(0, FN) as w:
                c0 = pe.snap(w * FW)
                for i in range(BLOCKS + 2):
                    if i < BLOCKS:
                        e, h = i // HT, i % HT
                        if h == 0:
                            pe.wait_ge(sem("chunk_lo"), 4 * e + DT)
                        if i >= 4:
                            pe.wait_ge(sem("h_relu"), BLOCKS * w + (i - 3))
                        k = 0
                        for t in range(DT):
                            for xs, ws in ((x_hi, f1w[0]), (x_lo, f1w[0]), (x_hi, f1w[1])):
                                last = mm(bank[i % 4][:, 0:FW], ws[:, t, e, h * P:(h + 1) * P], xs[:, t, bass.ds(c0, FW)],
                                          start=k == 0, stop=k == 5)
                                k += 1
                        last.then_inc(sem("h_sums"), 1)
                    if i >= 2:
                        j = i - 2
                        e, h = j // HT, j % HT
                        if h == 0:
                            pe.wait_ge(sem("chunk_lo"), 4 * e + 4)
                        pe.wait_ge(sem("h_lo"), BLOCKS * w + j + 1)
                        for f in range(DT):
                            k = 0
                            for hs, ws in ((h_hi, f2w[0]), (h_lo, f2w[0]), (h_hi, f2w[1])):
                                last = mm(bank[4 + f][:, 0:FW], ws[:, h, e, f * P:(f + 1) * P], hs[j % 2][:],
                                          start=j == 0 and k == 0, stop=False)
                                k += 1
                        last.then_inc(sem("y_sums"), 1)
                pe.wait_ge(sem("comb_w_in"), 16 * (w + 1))
                for f in range(DT):
                    last = mm(bank[4 + f][:, 0:FW], out_bias[:, f * P:(f + 1) * P], comb_w[:], start=False, stop=True)
                last.then_inc(sem("y_full"), 1)
                pe.wait_ge(sem("y_t"), w + 1)
                for j in range(PIECES):
                    for f in range(DT):
                        last = nc.tensor.transpose(bank[6 + j // 2][0:FP, (j % 2) * D + f * P:(j % 2) * D + (f + 1) * P],
                                                   y_t[:, f, j * FP:(j + 1) * FP], ident[:])
                    if j % 2:
                        last.then_inc(sem("y_turned"), 1)


_INS = ["x", "src", "dst"] + ["L0_gnn_" + n for n in ("W1", "b1", "W2", "b2", "W_ih", "b_ih", "W_hh", "b_hh")] \
    + ["L0_ffn_" + n for n in ("Wg", "bg", "bias", "W1", "b1", "W2", "b2")]


def kernel(**inputs):
    import numpy as _np
    import concourse.bacc as _bacc
    from concourse.bass_utils import run_bass_kernel_spmd as _run

    nc = _bacc.Bacc("TRN2", target_bir_lowering=False, num_devices=1)
    arrays, args = {}, []
    for name in _INS:
        a = _np.ascontiguousarray(inputs[name])
        arrays[f"in_{name}"] = a
        args.append(nc.dram_tensor(f"in_{name}", a.shape, mybir.dt.from_np(a.dtype), kind="ExternalInput").ap())
    args.append(nc.dram_tensor("out_0", (N, D), F32, kind="ExternalOutput").ap())
    gnn_ffn(nc, *args)
    r = _run(nc, [arrays], core_ids=[0])
    return r.results[0]["out_0"]
```

```python
from contextlib import ExitStack

import concourse.bass as bass
from concourse import mybir

F32 = mybir.dt.float32
F32R = mybir.dt.float32r
F16 = mybir.dt.float16
F8 = mybir.dt.float8e4
I32 = mybir.dt.int32
U16 = mybir.dt.uint16
U32 = mybir.dt.uint32
ALU = mybir.AluOpType
ACT = mybir.ActivationFunctionType
AX = mybir.AxisListType

P = 128
N = 3125
D = 256
E = 53125
STEPS = 6
DT = D // P
NT = (N + P - 1) // P
NPAD = NT * P
TAIL = N - (NT - 1) * P
G3 = 3 * D
GT = G3 // P

WIN_TILES = (4, 4, 4, 4, 3, 3, 3)
NW = len(WIN_TILES)
WIN_T0 = [sum(WIN_TILES[:w]) for w in range(NW)]
WIN_COL = [t * P for t in WIN_T0]
WIN_LEN = [n * P for n in WIN_TILES]
WIN_LEN[-1] = N + N % 2 - WIN_COL[-1]

SW = 16
NSL = (N + SW - 1) // SW
GROUP = 28
RING = 4
NSL = (NSL + GROUP - 1) // GROUP * GROUP
TURNS = NSL // GROUP
ACOLS = NSL * SW
KEY = 512
NCH = (E + P - 1) // P
BE = P // 2
NB = (E + BE - 1) // BE
CG = (NB + P - 1) // P
CB = (CG + 1) // 2 * P
SLOTS = 3
TURN_SLOTS = GROUP * SLOTS
SL_T = (NSL + P - 1) // P
EXACT8 = 16

USES = (NT + 1) // 2
USE_WIN = [max(w for w in range(NW) if WIN_T0[w] <= min(2 * u + 1, NT - 1)) for u in range(USES)]
EARLY = max(u for u in range(USES) if USE_WIN[u] < NW - 1) + 1
FILL_A = sum(USE_WIN[u] < 3 for u in range(USES))
FILL_B = EARLY
RELU_BANK = [(2, 3, 0, 1)[u % 4] if u < EARLY else 2 + (u - EARLY + 1) % 2 for u in range(USES)]

GATE_OPS = 9
NX = 8
HID = 512
HT = HID // P
TILE = 512
TT = TILE // P
MAX_TILES = (2 * N + NX * (TILE - 1)) // TILE
SLOT_ROWS = (MAX_TILES + 1) * TILE
OUT_TILES = 5
X1_GAP = 64
LG = (NT + 3) // 4
BLOCKS = NX * HT
CHUNKS = 2 * DT * NX
LEAD = GATE_OPS


def gnn_ffn(nc, x, src, dst, W1, b1, W2, b2, W_ih, b_ih, W_hh, b_hh, Wg, bg, bias, F1, fb1, F2, fb2, out):
    stack = ExitStack()
    with stack:
        sems = {}

        def sem(name):
            if name not in sems:
                sems[name] = stack.enter_context(nc.semaphore(name))
            return sems[name]

        def allocator(scope):
            return lambda name, shape, dt: scope.enter_context(nc.sbuf_tensor(name, shape, dt))

        sb = allocator(stack)
        bank = [stack.enter_context(nc.psum_tensor(f"bank{i}", [P, 512], F32)) for i in range(8)]

        ident = sb("ident", [P, P], F32)

        tile_scope = ExitStack()
        ab = allocator(tile_scope)
        raw_scope = ExitStack()
        raw = [allocator(raw_scope)(f"raw{i}", [P, HID], F32) for i in range(4)]
        raw_scope.close()
        h_hi = ab("h_hi", [P, HT, TILE], F32R)
        h_lo = ab("h_lo", [P, HT, TILE], F32R)
        act_h = [ab(f"act_h{i}", [P, TILE], F32) for i in range(2)]
        slot_x = ab("slot_x", [P, TT, D], F32)
        slot_y = ab("slot_y", [P, TT, D], F32)
        xt_hi = ab("xt_hi", [P, DT, TILE], F32R)
        xt_lo = ab("xt_lo", [P, DT, TILE], F32R)
        out_bias = ab("out_bias", [P, NX, D], F32)
        eid = ab("eid", [P, NT, NX], F32)
        logit = ab("logit", [P, NT, NX], F32)
        cand = ab("cand", [P, NT, NX], F32)
        hot1 = ab("hot1", [P, NT, NX], F32)
        hot2 = ab("hot2", [P, NT, NX], F32)
        chosen = ab("chosen", [P, NT, NX], F16)
        tile_scope.close()

        edge_scope = ExitStack()
        eb = allocator(edge_scope)
        e_tmp = eb("e_tmp", [P, CG, P], I32)
        diag = eb("diag", [P, 2, CG, P], F32)
        lim_b = eb("lim_b", [P, 2, CG * P], F32)
        block_id = eb("block_id", [P, CG * P], F32)
        mask = eb("mask", [P, CG * P], F32)
        picked = eb("picked", [P, CG, NSL * SLOTS], F32)
        edge_scope.close()

        x_hi = sb("x_hi", [P, DT, NPAD], F32R)
        x_lo = sb("x_lo", [P, DT, NPAD], F32R)

        slow_flag = sb("slow_flag", [1, 1], I32)

        gnn = ExitStack()
        gb = allocator(gnn)
        w1t = [gb(f"w1t_{p}", [P, DT, D], F32R) for p in ("hi", "lo")]
        wct = [gb(f"wct_{p}", [P, DT, G3], F32R) for p in ("hi", "lo")]
        wht = [gb(f"wht_{p}", [P, DT, G3], F32R) for p in ("hi", "lo")]
        b1_rows = gb("b1_rows", [P, D], F32R)
        ones_r = gb("ones_r", [P, P], F32R)
        gate_bias = gb("gate_bias", [P, GT], F32)
        hn_bias = gb("hn_bias", [P, DT], F32)
        deg_w = gb("deg_w", [P, GT], F32)
        degree = gb("degree", [P, ACOLS], U16)

        prep = ExitStack()
        pp = allocator(prep)
        xa = pp("xa", [P, NT, D], F32)
        w1n = pp("w1n", [P, DT, D], F32)
        w2n = pp("w2n", [P, DT, D], F32)
        win = pp("win", [P, GT, D], F32)
        whn = pp("whn", [P, GT, D], F32)
        wit = pp("wit", [P, DT, G3], F32)
        e_src = pp("e_src", [P, CG, P], I32)
        e_dst = pp("e_dst", [P, CG, P], I32)
        e_f = [pp(f"e_f{i}", [P, CG, P], F32) for i in range(3)]
        lim = pp("lim", [P, 2, CG], F32)
        prep.close()
        adj_scope = ExitStack()
        planes_scope = ExitStack()
        planes = allocator(planes_scope)("planes", [P, 2, NT, 512], F16)
        planes_scope.close()
        adj = allocator(adj_scope)("adj", [P, NT, ACOLS], F8)

        bs = ExitStack()
        bb = allocator(bs)
        key_t = bb("key_t", [P, CB], F32)
        row_t = bb("row_t", [P, CB], F32)
        exact_sum = bb("exact_sum", [P, NT * SW], F32)
        slot_id = bb("slot_id", [P, SLOTS], F32)
        part_id = bb("part_id", [P, CG], F32)
        slot_key = bb("slot_key", [P, NSL, SLOTS], F32)
        slot_row = bb("slot_row", [P, NSL, SLOTS], F32)
        turn_key = bb("turn_key", [P, TURN_SLOTS], F32)
        turn_row = bb("turn_row", [P, TURN_SLOTS], F32)
        iota_key = bb("iota_key", [P, NT * SW], F16)
        iota_row = bb("iota_row", [P, P], F16)
        slice_off = bb("slice_off", [P, NSL], F32)
        hot_key = [bb(f"hot_key{s}", [P, NT * SW], F16) for s in range(2 * SLOTS)]
        hot_row = [bb(f"hot_row{s}", [P, P], F16) for s in range(2 * SLOTS)]
        stage = [bb(f"stage{i}", [P, NT, 2 * SW], F8) for i in range(2)]
        trash = [bb(f"trash{i}", [P, NT * SW], F16) for i in range(RING)]
        over = bb("over", [P, NSL], F32)
        zero_rows = bb("zero_rows", [P, D], F32)
        bound_row = bb("bound_row", [1, 2 * 2 * P], I32)
        bound = bb("bound", [P, 2, 2], I32)
        slice_id = bb("slice_id", [P, 2], F32)
        bnd = bb("bnd", [P, 2, 2], F32)
        small = bb("small", [P, 16], F32)
        smalli = bb("smalli", [P, 16], I32)
        b1_col = bb("b1_col", [P, DT], F32)
        b2_col = bb("b2_col", [P, DT], F32)
        bih_col = bb("bih_col", [P, GT], F32)
        bhh_col = bb("bhh_col", [P, GT], F32)
        b1_diag = bb("b1_diag", [P, 2, D], F32)
        st = bb("st", [P, NT, 6], F32)
        mv = bb("mv", [P, NT, 2], F32)
        rstd = bb("rstd", [P, NT], F32)
        expo = bb("expo", [P, NT], F32)
        ones_h = bb("ones_h", [P, P], F16)
        ones_f = bb("ones_f", [P, P], F32)
        more = bb("more", [P, SL_T + 2], F32)
        minus_exact = bb("minus_exact", [P, 1], F32)
        bs.close()

        steps = ExitStack()
        ss = allocator(steps)
        r_hi = ss("r_hi", [P, NT, D], F16)
        r_lo = ss("r_lo", [P, NT, D], F16)
        m_hi = ss("m_hi", [P, DT, 512], F32R)
        m_lo = ss("m_lo", [P, DT, 512], F32R)
        gate_a = ss("gate_a", [P, 512], F32)
        gate_z = ss("gate_z", [P, 512], F32)
        x_new = ss("x_new", [P, DT, 512], F32)
        steps.close()
        adj_scope.close()
        gnn.close()

        ffn = ExitStack()
        fb = allocator(ffn)
        f1w_hi = fb("f1w_hi", [P, DT, NX, HID], F32R)
        hid_bias = fb("hid_bias", [P, BLOCKS], F32)
        top = fb("top", [P, 6, NT], F32)
        slot_of = fb("slot_of", [P, 2, NT], U32)
        tiles_of = fb("tiles_of", [P, NX + 1], I32)
        wg = fb("wg", [P, DT, NX], F32)
        bg_b = fb("bg_b", [P, 2, NX], F32)
        hid_bias_rows = fb("hid_bias_rows", [BLOCKS, P], F32)
        wg_r = [fb(f"wg_{p}", [P, DT, NX], F32R) for p in ("hi", "lo")]
        ident_r = fb("ident_r", [P, P], F32R)
        st2 = fb("st2", [P, NT, 6], F32)
        mv2 = fb("mv2", [P, NT, 2], F32)
        rstd2 = fb("rstd2", [P, NT], F32)
        expo2 = fb("expo2", [P, NT], F32)
        all_ones = fb("all_ones", [P, P], F16)
        before = fb("before", [P, P], F16)
        valid = fb("valid", [P, 2], F32)
        room = fb("room", [P, 2, NX], F32)
        roomi = fb("roomi", [P, NX], I32)
        fb("below_adj", [P, X1_GAP], F32)
        x1 = fb("x1", [P, NT, D], F32)
        final = ExitStack()
        y_pair = allocator(final)("y_pair", [P, NT, 2, D], F32)
        final.close()
        logit_scope = ExitStack()
        logit_t = allocator(logit_scope)("logit_t", [NX, NPAD], F32)
        logit_scope.close()
        f1w = [f1w_hi, fb("f1w_lo", [P, DT, NX, HID], F32R)]
        f2w = [fb(f"f2w_{p}", [P, HT, NX, D], F32R) for p in ("hi", "lo")]
        ffn.close()

        x1_dram = nc.dram_tensor("x1_scratch", (NPAD, D), F32, kind="Internal").ap()
        slot_in = nc.dram_tensor("slot_in", (SLOT_ROWS, D), F32, kind="Internal").ap()
        slot_out = nc.dram_tensor("slot_out", (SLOT_ROWS, D), F32, kind="Internal").ap()
        plane_dram = [nc.dram_tensor(f"plane_scratch{i}", (P, NT, ACOLS), F16, kind="Internal").ap() for i in range(2)]
        bound_dram = nc.dram_tensor("bound_scratch", (2 * P, 2), I32, kind="Internal").ap()
        inputs = sem("inputs")
        block = stack.enter_context(nc.Block())

        exact_part = [trash[i] for i in range(2)]
        EXACT_STORED = 32 * NSL + 1

        def read_slow_flag(engine):
            engine.wait_ge(sem("slow_flag"), 1)
            return engine.value_load(slow_flag[0:1, 0:1], min_val=0, max_val=1)

        def half(s, w, f):
            return s * (2 * NW) + 2 * w + f

        @block.sync
        def _(sp):
            sp.wait_ge(sem("edges_clear"), 2)
            whole = NB - 2
            full = whole // P * P
            rest = whole - full
            for buf, inp in ((e_src, src), (e_dst, dst)):
                for h in range(2):
                    e0 = h * BE
                    sp.dma_start(buf[:, 0:full // P, e0:e0 + BE], inp[e0:e0 + full * BE].rearrange("(g p e) -> p g e", p=P, e=BE)).then_inc(sem("edges"), 16)
                    e1 = full * BE + e0
                    sp.dma_start(buf[0:rest, full // P, e0:e0 + BE], inp[e1:e1 + rest * BE].rearrange("(p e) -> p e", e=BE)).then_inc(sem("edges"), 16)
                sp.dma_start(buf[rest:rest + 1, full // P, 0:E - whole * BE], inp[whole * BE:E].rearrange("(a e) -> a e", a=1)).then_inc(sem("edges"), 16)
            last = E - (NB - 1) * BE
            sp.dma_start(e_src[rest + 1:rest + 2, full // P, BE - last:BE], src[E - last:E].rearrange("(a e) -> a e", a=1)).then_inc(sem("edges"), 16)
            sp.dma_start(e_dst[rest + 1:rest + 2, full // P, 0:BE], dst[E - BE:E].rearrange("(a e) -> a e", a=1)).then_inc(sem("edges"), 16)
            sp.dma_start(w1n[:], W1.rearrange("(t p) i -> p t i", p=P)).then_inc(inputs, 16)
            sp.dma_start(w2n[:], W2.rearrange("(t p) i -> p t i", p=P)).then_inc(inputs, 16)
            sp.dma_start(win[:], W_ih.rearrange("(t p) i -> p t i", p=P)).then_inc(inputs, 16)
            sp.dma_start(whn[:], W_hh.rearrange("(t p) i -> p t i", p=P)).then_inc(inputs, 16)
            for buf, inp in ((b1_col, b1), (b2_col, b2), (bih_col, b_ih), (bhh_col, b_hh)):
                sp.dma_start(buf[:], inp.rearrange("(t p) -> p t", p=P), allow_slow_non_contiguous=True).then_inc(inputs, 16)
            sp.wait_ge(sem("xa_clear"), 1)
            sp.dma_start(xa[:, 0:NT - 1, :], x[0:(NT - 1) * P, :].rearrange("(t p) d -> p t d", p=P)).then_inc(sem("x_in"), 16)
            sp.dma_start(xa[0:TAIL, NT - 1, :], x[(NT - 1) * P:N, :]).then_inc(sem("x_in"), 16)
            sp.wait_ge(sem("zero_rows"), 1)
            for buf in (slot_in, slot_out):
                sp.dma_start(buf.rearrange("(t p) d -> p t d", p=P),
                             zero_rows[:].rearrange("p (a d) -> p a d", a=1).broadcast_to([P, SLOT_ROWS // P, D])).then_inc(sem("slots_zero"), 16)
            sp.wait_ge(sem("bound_col"), 1)
            sp.dma_start(bound_dram.rearrange("(t p) b -> p t b", p=P), bound[:]).then_inc(sem("bound_out"), 16)
            sp.wait_ge(sem("bound_out"), 16)
            sp.dma_start(bound_row[:], bound_dram.rearrange("(a p) b -> a (p b)", a=1)).then_inc(sem("bound_in"), 16)
            slow = read_slow_flag(sp)
            with sp.If(slow > 0):
                with sp.Fori(0, NSL) as sl:
                    c0 = sp.snap(sl * SW)
                    sp.wait_ge(sem("exact_split"), sl + 1)
                    for i in range(2):
                        sp.dma_start(plane_dram[i][:, :, bass.ds(c0, SW)], exact_part[i][:].rearrange("p (q c) -> p q c", c=SW))\
                          .then_inc(sem("exact_stored"), 16)
                sp.wait_ge(sem("exact_stored"), EXACT_STORED)

                def load_planes(w):
                    n, c0 = WIN_LEN[w], WIN_COL[w]
                    for i in range(2):
                        sp.dma_start(planes[:, i, :, 0:n], plane_dram[i][:, :, c0:c0 + n]).then_inc(sem("planes_in"), 16)

                for w in range(NW):
                    load_planes(w)
                    sp.wait_ge(sem("exact_deg_sum"), w + 1)
                load_planes(0)
                with sp.Fori(0, STEPS - 1) as s:
                    for w in range(NW):
                        sp.wait_ge(sem("msg_sums"), half(s, w, 2))
                        load_planes((w + 1) % NW)
                for w in range(NW - 1):
                    sp.wait_ge(sem("msg_sums"), half(STEPS - 1, w, 2))
                    load_planes(w + 1)
            sp.wait_ge(sem("x1_clear"), 1)
            sp.dma_start(x1[:, 0:NT - 1, :], x[0:(NT - 1) * P, :].rearrange("(t p) d -> p t d", p=P)).then_inc(sem("x_again"), 16)
            sp.dma_start(x1[0:TAIL, NT - 1, :], x[(NT - 1) * P:N, :]).then_inc(sem("x_again"), 16)
            sp.wait_ge(sem("state_lo"), NW * (STEPS + 1))
            sp.dma_start(wg[:], Wg.rearrange("(t p) e -> p t e", p=P)).then_inc(sem("gate_in"), 16)
            sp.dma_start(bg_b[:, 0, :], bg.rearrange("(a e) -> a e", a=1).broadcast_to([P, NX])).then_inc(sem("gate_in"), 16)
            sp.dma_start(bg_b[:, 1, :], bias.rearrange("(a e) -> a e", a=1).broadcast_to([P, NX])).then_inc(sem("gate_in"), 16)
            sp.dma_start(hid_bias_rows[:], fb1.rearrange("e (t p) -> (e t) p", p=P)).then_inc(sem("gate_in"), 16)
            sp.wait_ge(sem("x1_sum"), USES)
            sp.dma_start(x1_dram.rearrange("(t p) d -> p t d", p=P), x1[:]).then_inc(sem("x1_out"), 16)
            sp.wait_ge(sem("logits"), 1)
            for e in range(NX):
                sp.dma_start(out_bias[:, e, :], fb2[e:e + 1, :].broadcast_to([P, D])).then_inc(sem("out_bias_in"), 16)
            for c in range(CHUNKS):
                e, k = c // 4, c % 4
                if c >= 4:
                    sp.wait_ge(sem("chunk_lo"), c - 3)
                if k < DT:
                    sp.dma_start(raw[c % 4][:], F1[e, k * P:(k + 1) * P, :]).then_inc(sem(f"chunk_in{c % 4}"), 16)
                else:
                    h0 = (k - DT) * 2 * P
                    sp.dma_start(raw[c % 4][:].rearrange("p (t d) -> p t d", t=2),
                                 F2[e, h0:h0 + 2 * P, :].rearrange("(t p) d -> p t d", p=P)).then_inc(sem(f"chunk_in{c % 4}"), 16)
            sp.wait_ge(sem("scattered"), 16 * 2 * NT)

            def load_tile(r0):
                sp.dma_start(slot_x[:], slot_in[bass.ds(r0, TILE), :].rearrange("(j p) d -> p j d", p=P)).then_inc(sem("tile_in"), 16)

            load_tile(0)
            sp.dma_start(x1[:], x1_dram.rearrange("(t p) d -> p t d", p=P)).then_inc(sem("x1_in"), 16)
            tiles = sp.value_load(tiles_of[0:1, NX:NX + 1], min_val=0, max_val=MAX_TILES)
            with sp.Fori(0, tiles) as t:
                r0 = sp.snap(t * TILE)
                r1 = sp.snap(t * TILE + TILE)
                sp.wait_ge(sem("tile_turned"), t + 1)
                load_tile(r1)
                sp.wait_ge(sem("y_ready"), 2 * t + 4)
                sp.dma_start(slot_out[bass.ds(r0, TILE), :].rearrange("(j p) d -> p j d", p=P), slot_y[:]).then_inc(sem("y_stored"), 16)
            for g in range(NT // OUT_TILES):
                t0, t1 = g * OUT_TILES, (g + 1) * OUT_TILES
                sp.wait_ge(sem("summed"), t1)
                if t1 < NT:
                    sp.dma_start(out[t0 * P:t1 * P, :].rearrange("(t p) d -> p t d", p=P), x1[:, t0:t1, :]).then_inc(sem("stored"), 16)
                else:
                    sp.dma_start(out[t0 * P:(t1 - 1) * P, :].rearrange("(t p) d -> p t d", p=P), x1[:, t0:t1 - 1, :]).then_inc(sem("stored"), 16)
                    sp.dma_start(out[(t1 - 1) * P:N, :], x1[0:TAIL, t1 - 1, :]).then_inc(sem("stored"), 16)
            sp.wait_ge(sem("stored"), 16 * (NT // OUT_TILES + 1))

        INPUTS = 16 * 8

        @block.gpsimd
        def _(pool):
            pool.memset(ones_f[:], 1.0).then_inc(sem("ones_ready"), 1)
            pool.memset(e_src[:], -1).then_inc(sem("edges_clear"), 1)
            pool.memset(e_dst[:], 0).then_inc(sem("edges_clear"), 1)
            pool.memset(zero_rows[:], 0.0).then_inc(sem("zero_rows"), 1)
            pool.memset(xa[:, NT - 1, :], 0.0).then_inc(sem("xa_clear"), 1)
            pool.memset(ident[:], 0.0).then_inc(sem("p0"), 1)
            pool.wait_ge(sem("p0"), 1)
            pool.affine_select(out=ident[:], in_=ident[:], compare_op=ALU.not_equal, fill=1.0, base=0,
                               pattern=[[-1, P]], channel_multiplier=1).then_inc(sem("ident_ready"), 1)
            pool.iota(block_id[:], [[1, CG * P]], base=0, channel_multiplier=0, allow_small_or_imprecise_dtypes=True).then_inc(sem("iotas"), 1)
            pool.iota(slice_id[:], [[P, 2]], base=0, channel_multiplier=1, allow_small_or_imprecise_dtypes=True).then_inc(sem("iotas"), 1)
            pool.iota(iota_key[:], [[1, NT * SW]], base=0, channel_multiplier=0, allow_small_or_imprecise_dtypes=True).then_inc(sem("iotas"), 1)
            pool.iota(iota_row[:], [[1, P]], base=0, channel_multiplier=0, allow_small_or_imprecise_dtypes=True).then_inc(sem("iotas"), 1)
            pool.iota(slice_off[:], [[KEY, NSL]], base=0, channel_multiplier=0, allow_small_or_imprecise_dtypes=True).then_inc(sem("iotas"), 1)
            pool.iota(slot_id[:], [[2, SLOTS]], base=0, channel_multiplier=0, allow_small_or_imprecise_dtypes=True).then_inc(sem("iotas"), 1)
            pool.iota(part_id[:], [[P, CG]], base=0, channel_multiplier=1, allow_small_or_imprecise_dtypes=True).then_inc(sem("iotas"), 1)
            pool.memset(minus_exact[:], -float(EXACT8)).then_inc(sem("stage_free"), 2)
            pool.memset(expo[:], -0.5).then_inc(sem("p0"), 1)
            pool.wait_ge(sem("p0"), 2)
            pool.wait_ge(sem("var_ready"), 1)
            pool.tensor_tensor(rstd[:], rstd[:], expo[:], ALU.pow).then_inc(sem("rstd_ready"), 1)
            with pool.Fori(0, TURNS) as i:
                for b in range(GROUP):
                    if b % 2:
                        pool.wait_ge(sem("stage_full"), GROUP * i + (b + 1 + RING))
                        pool.tensor_copy(adj[:].bitcast(U32)[:, :, bass.ds(i * (GROUP * SW // 4) + (b - 1) * SW // 4, 2 * SW // 4)],
                                         stage[b // 2 % 2][:].bitcast(U32)).then_inc(sem("stage_free"), 1)
            slow = read_slow_flag(pool)
            with pool.If(slow > 0):
                with pool.Fori(0, NSL) as sl:
                    pool.wait_ge(sem("exact_hi"), sl + 2)
                    pool.tensor_tensor(exact_part[1][:], exact_sum[:], exact_part[0][:], ALU.subtract).then_inc(sem("exact_split"), 1)
            pool.wait_ge(sem("msg_sums"), DT * NW * STEPS)
            pool.memset(x1[:, NT - 1, :], 0.0).then_inc(sem("x1_clear"), 1)
            pool.wait_ge(sem("state_lo"), NW * (STEPS + 1))
            pool.memset(expo2[:], -0.5).then_inc(sem("p0"), 1)
            pool.wait_ge(sem("p0"), 3)
            pool.wait_ge(sem("var_ready"), 2)
            pool.tensor_tensor(rstd2[:], rstd2[:], expo2[:], ALU.pow).then_inc(sem("rstd_ready"), 1)
            pool.wait_ge(sem("logits"), 1)
            pool.iota(eid[:], [[0, NT], [1, NX]], base=0, channel_multiplier=0, allow_small_or_imprecise_dtypes=True).then_inc(sem("iotas"), 1)
            pool.memset(before[:], 1.0)
            pool.memset(all_ones[:], 1.0)
            pool.memset(valid[:], 1.0).then_inc(sem("p0"), 1)
            pool.wait_ge(sem("p0"), 4)
            pool.affine_select(out=before[:], in_=before[:], compare_op=ALU.is_gt, fill=0.0, base=0,
                               pattern=[[1, P]], channel_multiplier=-1).then_inc(sem("iotas"), 1)
            pool.affine_select(out=valid[:], in_=valid[:], compare_op=ALU.is_gt, fill=0.0, base=TAIL,
                               pattern=[[0, 2]], channel_multiplier=-1).then_inc(sem("iotas"), 1)
            pool.wait_ge(sem("slots_zero"), 32)
            pool.wait_ge(sem("slot_of"), 1)
            for t in range(NT):
                n = TAIL if t == NT - 1 else P
                for k in range(2):
                    pool.indirect_dma_start(slot_in[:], bass.IndirectOffsetOnAxis(ap=slot_of[0:n, k, t:t + 1], axis=0),
                                            x1[0:n, t, :], None).then_inc(sem("scattered"), 16)
            tiles = pool.value_load(tiles_of[0:1, NX:NX + 1], min_val=0, max_val=MAX_TILES)
            pool.wait_ge(sem("y_stored"), tiles * 16 + 1)
            pool.tensor_tensor(valid[:, 1:2], valid[:, 0:1], valid[:, 0:1], ALU.mult).then_inc(sem("experts_done"), 1)
            pool.wait_ge(sem("experts_done"), 1)
            for t in range(NT):
                n = TAIL if t == NT - 1 else P
                for k in range(2):
                    pool.indirect_dma_start(y_pair[0:n, t, k, :], None, slot_out[:],
                                            bass.IndirectOffsetOnAxis(ap=slot_of[0:n, k, t:t + 1], axis=0)).then_inc(sem(f"gathered{t // 2}"), 16)

        def chunk_dst(c):
            e, k = c // 4, c % 4
            if k < DT:
                return [w[:, k, e, :] for w in f1w]
            return [w[:, 2 * (k - DT):2 * (k - DT) + 2, e, :] for w in f2w]

        @block.vector
        def _(dve):
            chain = [0]

            def link(ins):
                chain[0] += 1
                ins.then_inc(sem("dve_prep"), 1)
                dve.wait_ge(sem("dve_prep"), chain[0])

            v = nc.vector
            dve.wait_ge(sem("edges"), 16 * 12)
            link(v.tensor_scalar(e_tmp[:], e_dst[:], -SW, (KEY // SW).bit_length() - 1, ALU.bitwise_and, ALU.arith_shift_left))
            link(v.scalar_tensor_tensor(e_tmp[:], e_dst[:], SW - 1, e_tmp[:], ALU.bitwise_and, ALU.bitwise_or))
            link(v.tensor_copy(e_f[2][:], e_dst[:]))
            link(v.tensor_scalar(e_dst[:], e_src[:], 127, None, ALU.bitwise_and))
            link(v.tensor_copy(e_f[1][:], e_dst[:]))
            link(v.tensor_scalar(e_src[:], e_src[:], -P, (P // SW).bit_length() - 1, ALU.bitwise_and, ALU.arith_shift_right))
            link(v.tensor_tensor(e_tmp[:], e_tmp[:], e_src[:], ALU.bitwise_or))
            v.tensor_copy(e_f[0][:], e_tmp[:]).then_inc(sem("keys"), 1)
            v.tensor_reduce(lim[:, 0, :], e_f[2][:, :, 0:BE], AX.X, ALU.min).then_inc(sem("lims"), 1)
            v.tensor_reduce(lim[:, 1, :], e_f[2][:, :, 0:BE], AX.X, ALU.max).then_inc(sem("lims"), 1)
            dve.wait_ge(sem("lims"), 2)
            dve.wait_ge(sem("ident_ready"), 1)
            for m in range(2):
                for g in range(CG):
                    last = v.tensor_scalar(diag[:, m, g, :], ident[:], lim[:, m, g:g + 1], None, ALU.mult)
            last.then_inc(sem("diags"), 1)
            dve.wait_ge(sem("keys_t"), 1)
            for i, table in ((0, key_t), (1, row_t)):
                for h in range(2):
                    last = v.tensor_copy(table[:, h * 2 * P:(h + 1) * 2 * P], bank[2 * i + h][:].rearrange("p (c two) -> p c two", two=2)[:, :, 0])
            last.then_inc(sem("edge_table"), 1)
            dve.wait_ge(sem("lims_b"), 1)
            for m in range(2):
                for h in range(2):
                    n = min(4, CG - 4 * h) * P
                    last = v.tensor_copy(lim_b[:, m, h * 512:h * 512 + n], bank[4 + 2 * m + h][:, 0:n])
            link(last)
            dve.wait_ge(sem("iotas"), 7)
            for t in range(2):
                link(v.tensor_scalar(small[:, 0:1], slice_id[:, t:t + 1], float(SW), float(SW - 1), ALU.mult, ALU.add))
                link(v.tensor_scalar(small[:, 1:2], slice_id[:, t:t + 1], float(SW), None, ALU.mult))
                link(v.tensor_scalar(mask[:, 0:NB], lim_b[:, 0, 0:NB], small[:, 0:1], None, ALU.is_le))
                link(v.scalar_tensor_tensor(mask[:, 0:NB], lim_b[:, 1, 0:NB], small[:, 1:2], mask[:, 0:NB], ALU.is_ge, ALU.mult))
                link(v.scalar_tensor_tensor(e_f[2][:].rearrange("p g e -> p (g e)")[:, 0:NB], block_id[:, 0:NB], float(-NB), mask[:, 0:NB], ALU.add, ALU.mult))
                link(v.tensor_reduce(small[:, 2:3], e_f[2][:].rearrange("p g e -> p (g e)")[:, 0:NB], AX.X, ALU.min))
                link(v.scalar_tensor_tensor(e_f[2][:].rearrange("p g e -> p (g e)")[:, 0:NB], block_id[:, 0:NB], 1.0, mask[:, 0:NB], ALU.add, ALU.mult))
                link(v.tensor_reduce(bnd[:, t, 1:2], e_f[2][:].rearrange("p g e -> p (g e)")[:, 0:NB], AX.X, ALU.max))
                link(v.tensor_scalar(bnd[:, t, 0:1], small[:, 2:3], float(NB), None, ALU.add))
            link(v.tensor_copy(bound[:], bnd[:]))
            link(v.tensor_scalar(bound[:, :, 1], bound[:, :, 1], 1, None, ALU.add))
            v.tensor_scalar(bound[:], bound[:], 1, None, ALU.arith_shift_right).then_inc(sem("bound_col"), 1)
            for t in range(SL_T):
                link(v.scalar_tensor_tensor(more[:, t:t + 1], bnd[:, t, 1:2], float(-2 * SLOTS), bnd[:, t, 0:1], ALU.add, ALU.subtract))
            for t in range(SL_T):
                last = v.tensor_scalar(diag[:, 0, t, :], ident[:], bnd[:, t, 0:1], None, ALU.mult)
            last.then_inc(sem("first_diag"), 1)
            dve.wait_ge(sem("first_b"), 1)
            link(v.tensor_tensor(slot_key[:], bank[3][:, 0:NSL].rearrange("p (n a) -> p n a", a=1).broadcast_to([P, NSL, SLOTS]),
                                 slot_id[:].rearrange("p (a s) -> p a s", a=1).broadcast_to([P, NSL, SLOTS]), ALU.add))
            for g in range(CG):
                last = v.tensor_scalar(picked[:, g, :], slot_key[:].rearrange("p n s -> p (n s)"), part_id[:, g:g + 1], None, ALU.is_equal)
            last.then_inc(sem("picked"), 1)

            dve.wait_ge(sem("x_in"), 32)
            for t in range(NT):
                last = v.bn_stats(st[:, t, :], xa[:, t, :])
            link(last)
            for t in range(NT):
                last = v.bn_aggr(mv[:, t, :], st[:, t, :])
            link(last)
            v.tensor_scalar(rstd[:], mv[:, :, 1], 1e-5, None, ALU.add).then_inc(sem("var_ready"), 1)

            dve.wait_ge(inputs, INPUTS)
            for t in range(DT):
                link(v.tensor_reduce(small[:, t:t + 1], w1n[:, t, :], AX.X, ALU.add, apply_absolute_value=True))
            link(v.tensor_reduce(small[:, 2:4], b1_col[:].rearrange("p (t a) -> p t a", a=1), AX.X, ALU.add, apply_absolute_value=True))
            link(v.scalar_tensor_tensor(small[:, 4:6], small[:, 0:2], 16.0, small[:, 2:4], ALU.mult, ALU.add))
            link(v.tensor_scalar(smalli[:, 0:2], small[:, 4:6].bitcast(I32), 0xFF << 23, None, ALU.bitwise_and))
            link(v.tensor_scalar(smalli[:, 0:2], smalli[:, 0:2], float(20 << 23), None, ALU.max))
            link(v.tensor_scalar(smalli[:, 2:4], smalli[:, 0:2], -1.0, float(268 << 23), ALU.mult, ALU.add))
            link(v.tensor_scalar(smalli[:, 4:6], smalli[:, 0:2], float(-(14 << 23)), None, ALU.add))
            sc = smalli[:].bitcast(F32)
            for t in range(DT):
                link(v.tensor_scalar(w1n[:, t, :], w1n[:, t, :], sc[:, 2 + t:3 + t], None, ALU.mult))
                link(v.tensor_scalar(small[:, 6 + t:7 + t], b1_col[:, t:t + 1], sc[:, 2 + t:3 + t], None, ALU.mult))
            for t in range(DT):
                for h in range(DT):
                    if h == t:
                        link(v.tensor_scalar(b1_diag[:, t, h * P:(h + 1) * P], ident[:], small[:, 6 + t:7 + t], None, ALU.mult))
                    else:
                        link(v.memset(b1_diag[:, t, h * P:(h + 1) * P], 0.0))
            link(v.memset(ones_h[:], 1.0))
            link(v.tensor_copy(ones_r[:], ones_h[:]))
            v.memset(b1_rows[:].bitcast(F32), 0.0).then_inc(sem("w1_scaled"), 1)
            v.tensor_tensor(gate_bias[:, 0:4], bih_col[:, 0:4], bhh_col[:, 0:4], ALU.add)
            v.tensor_copy(gate_bias[:, 4:6], bih_col[:, 4:6])
            v.tensor_copy(hn_bias[:], bhh_col[:, 4:6])

            dve.wait_ge(sem("rstd_ready"), 1)
            for t in range(NT):
                v.tensor_scalar(xa[:, t, :], xa[:, t, :], mv[:, t, 0:1], rstd[:, t:t + 1], ALU.subtract, ALU.mult)\
                 .then_inc(sem("x_norm"), 1)

            dve.wait_ge(sem("w_hi"), 1)
            v.tensor_tensor(w1t[1][:], bank[4][:].rearrange("p (t j) -> p t j", t=DT), w1t[0][:].bitcast(F32), ALU.subtract).then_inc(sem("w_lo"), 1)
            dve.wait_ge(sem("w_tr"), 2)
            v.tensor_copy(b1_rows[0:1, :], bank[5][0:1, 0:D])
            link(v.tensor_copy(b1_rows[32:33, :], bank[5][32:33, 0:D]))
            v.tensor_tensor(b1_rows[32:33, :], bank[5][32:33, 0:D], b1_rows[32:33, :].bitcast(F32), ALU.subtract).then_inc(sem("b1_done"), 1)
            for j in range(4):
                t, c = j // 2, j % 2
                dve.wait_ge(sem("w_tr"), 3 + j)
                v.tensor_copy(wit[:, t, c * 384:(c + 1) * 384], bank[6 + j % 2][:, 0:384]).then_inc(sem("wit_ready"), 1)
            for j in range(4):
                t, c = j // 2, j % 2
                dve.wait_ge(sem("w_hi"), 2 + j)
                v.tensor_tensor(wht[1][:, t, c * 384:(c + 1) * 384], bank[j % 2][:, 0:384],
                                wht[0][:, t, c * 384:(c + 1) * 384].bitcast(F32), ALU.subtract).then_inc(sem("w_lo"), 1)
            dve.wait_ge(sem("w_tr"), 11)
            v.tensor_copy(deg_w[:], bank[2][:, 0:GT])
            for j in range(4):
                t, c = j // 2, j % 2
                dve.wait_ge(sem("w_tr"), 12 + j)
                if j:
                    dve.wait_ge(sem("w_lo"), 5 + j)
                ins = v.tensor_scalar(e_f[2][:].rearrange("p g e -> p (g e)")[:, 0:384], bank[4 + j % 2][:, 0:384], sc[:, 4 + t:5 + t], None, ALU.mult)
                ins.then_inc(sem("wc_scaled"), 1)
                dve.wait_ge(sem("w_hi"), 6 + j)
                v.tensor_tensor(wct[1][:, t, c * 384:(c + 1) * 384], e_f[2][:].rearrange("p g e -> p (g e)")[:, 0:384],
                                wct[0][:, t, c * 384:(c + 1) * 384].bitcast(F32), ALU.subtract).then_inc(sem("w_lo"), 1)
            dve.wait_ge(sem("slot_sums"), 1)
            half_n = NSL // 2
            for h in range(2):
                v.tensor_tensor(slot_key[:, h * half_n:(h + 1) * half_n, :], bank[2 + h][:, 0:half_n * SLOTS].rearrange("p (n s) -> p n s", s=SLOTS),
                                slice_off[:, h * half_n:(h + 1) * half_n].rearrange("p (n a) -> p n a", a=1).broadcast_to([P, half_n, SLOTS]), ALU.subtract)
            for h in range(2):
                last = v.tensor_copy(slot_row[:, h * half_n:(h + 1) * half_n, :], bank[h][:, 0:half_n * SLOTS].rearrange("p (n s) -> p n s", s=SLOTS))
            last.then_inc(sem("slot_tables"), 1)
            for u in range(USES):
                m = min(2, NT - 2 * u) * P
                dve.wait_ge(sem("xt_hi"), u + 1)
                ins = v.tensor_tensor(x_lo[:, :, 2 * P * u:2 * P * u + m],
                                      bank[6 + u % 2][:, 0:DT * m].rearrange("p (t n) -> p t n", t=DT),
                                      x_hi[:, :, 2 * P * u:2 * P * u + m].bitcast(F32), ALU.subtract)
                ins.then_inc(*((sem("xt_lo"), 1) if u < USES - 1 else (sem("state_lo"), NW)))

            dve.wait_ge(sem("slot_tables"), 1)
            with dve.Fori(0, TURNS) as i:
                dve.wait_ge(sem("hots_full"), GROUP * i + GROUP)
                v.tensor_copy(turn_row[:], slot_row[:].rearrange("p a b -> p (a b)")[:, bass.ds(i * TURN_SLOTS, TURN_SLOTS)])
                v.tensor_copy(turn_key[:], slot_key[:].rearrange("p a b -> p (a b)")[:, bass.ds(i * TURN_SLOTS, TURN_SLOTS)]).then_inc(sem("turn_key"), 1)
                dve.wait_ge(sem("turn_key"), i + 1)
                for b in range(GROUP):
                    dve.wait_ge(sem("hot_free"), GROUP * i + (b + 1))
                    for s in range(SLOTS):
                        k = (b % 2) * SLOTS + s
                        v.tensor_scalar(hot_row[k][:], iota_row[:], turn_row[:, b * SLOTS + s:b * SLOTS + s + 1], None, ALU.is_equal)
                        last = v.tensor_scalar(hot_key[k][:], iota_key[:], turn_key[:, b * SLOTS + s:b * SLOTS + s + 1], None, ALU.is_equal)
                    last.then_inc(sem("hots_full"), 1)

            dve.wait_ge(sem("stage_full"), NSL + RING)
            link(v.tensor_reduce(more[:, SL_T:SL_T + 1], over[:], AX.X, ALU.max))
            link(v.tensor_reduce(more[:, SL_T + 1:SL_T + 2], more[:, 0:SL_T + 1], AX.X, ALU.max))
            v.tensor_scalar(more[:, SL_T + 1:SL_T + 2], more[:, SL_T + 1:SL_T + 2], 0.0, None, ALU.max).then_inc(sem("more"), 1)
            dve.wait_ge(sem("bound_in"), 16)
            dve.wait_ge(sem("slow_sum"), 1)
            v.tensor_scalar(slow_flag[:], bank[3][0:1, 0:1], 1.0, None, ALU.min).then_inc(sem("slow_flag"), 1)
            slow = read_slow_flag(dve)
            with dve.If(slow > 0):
                v.memset(hot_key[1][:], 0.0).then_inc(sem("zero_key"), 1)
                taken = dve.alloc_register("dve_taken")
                dve.reg_mov(taken, 0)
                with dve.Fori(0, NSL) as sl:
                    first = dve.value_load(bound_row[0:1, bass.ds(2 * sl, 1)], min_val=0, max_val=NCH)
                    end = dve.value_load(bound_row[0:1, bass.ds(2 * sl + 1, 1)], min_val=0, max_val=NCH)
                    with dve.If(end > first):
                        with dve.Fori(first, end) as c:
                            dve.wait_ge(sem("chunk_used"), dve.snap(taken) + 1)
                            v.tensor_scalar(hot_row[0][:], iota_row[:], row_t[:, bass.ds(c, 1)], None, ALU.is_equal)
                            v.tensor_scalar(hot_key[0][:], iota_key[:], slice_off[:, bass.ds(sl, 1)], key_t[:, bass.ds(c, 1)],
                                            ALU.add, ALU.is_equal).then_inc(sem("chunk_hot"), 1)
                            dve.reg_add(taken, taken, 1)
                for w in range(NW):
                    dve.wait_ge(sem("exact_deg_sum"), w + 1)
                    v.tensor_copy(degree[:, WIN_COL[w]:WIN_COL[w] + WIN_LEN[w]], bank[4 + w % 4][:, 0:WIN_LEN[w]]).then_inc(sem("exact_deg_done"), 1)
                dve.wait_ge(sem("exact_deg_done"), NW)
                dve.wait_ge(sem("exact_stored"), EXACT_STORED)
            v.memset(x_new[:, 0, 0:2], 0.0).then_inc(sem("gate_ops"), LEAD)
            dve.wait_ge(sem("stage_free"), NSL // 2 + 2)
            dve.wait_ge(sem("deg_done"), NSL // 2 + 2)
            dve.wait_ge(sem("gate_ops"), LEAD)

            def relu_lo(g, u):
                m = min(2, NT - 2 * u)
                dve.wait_ge(sem("relu_hi"), g + 1)
                v.scalar_tensor_tensor(r_lo[:, 2 * u:2 * u + m, :].rearrange("p t d -> p (t d)"), bank[RELU_BANK[u]][:, 0:m * D], 0.0,
                                       r_hi[:, 2 * u:2 * u + m, :].rearrange("p t d -> p (t d)"), ALU.max, ALU.subtract)\
                 .then_inc(sem("relu_lo"), 1)

            def msg_lo(s, w):
                for f in range(DT):
                    n = WIN_LEN[w]
                    dve.wait_ge(sem("msg_hi"), half(s, w, f) + 1)
                    v.tensor_tensor(m_lo[:, f, 0:n], bank[2 * (w % 2) + f][:, 0:n], m_hi[:, f, 0:n].bitcast(F32), ALU.subtract)\
                     .then_inc(sem("msg_lo"), 1)

            def gates(s, w, f):
                n, c0 = WIN_LEN[w], WIN_COL[w]
                h = dve.snap(half(s, w, f)) if not isinstance(s, int) else half(s, w, f)
                mine = h * GATE_OPS + LEAD
                mine = dve.snap(mine) if not isinstance(s, int) else mine
                theirs = h * 3
                full = h * 4
                dg = degree[:, c0:c0 + n]
                a, z, xn = gate_a[:, 0:n], gate_z[:, 0:n], x_new[:, f, 0:n]

                def op(ins):
                    ins.then_inc(sem("gate_ops"), 1)

                dve.wait_ge(sem("gate_ops"), mine)
                dve.wait_ge(sem("gate_sums"), full + 1)
                op(v.scalar_tensor_tensor(a, dg, deg_w[:, f:f + 1], bank[4][:, 0:n], ALU.mult, ALU.add))
                dve.wait_ge(sem("gate_sums"), full + 2)
                op(v.scalar_tensor_tensor(z, dg, deg_w[:, 2 + f:3 + f], bank[5][:, 0:n], ALU.mult, ALU.add))
                dve.wait_ge(sem("gate_sums"), full + 3)
                dve.wait_ge(sem("gate_acts"), theirs + 1)
                op(v.scalar_tensor_tensor(a, bank[6][:, 0:n], hn_bias[:, f:f + 1], a, ALU.add, ALU.mult))
                dve.wait_ge(sem("gate_sums"), full + 4)
                dve.wait_ge(sem("gate_ops"), mine + 3)
                op(v.tensor_tensor(a, bank[7][:, 0:n], a, ALU.add))
                dve.wait_ge(sem("gate_ops"), mine + 4)
                op(v.scalar_tensor_tensor(a, dg, deg_w[:, 4 + f:5 + f], a, ALU.mult, ALU.add))
                dve.wait_ge(sem("gate_acts"), theirs + 3)
                op(v.tensor_tensor(xn, x_hi[:, f, c0:c0 + n].bitcast(F32), a, ALU.subtract))
                dve.wait_ge(sem("gate_ops"), mine + 6)
                op(v.tensor_tensor(xn, xn, x_lo[:, f, c0:c0 + n].bitcast(F32), ALU.add))
                dve.wait_ge(sem("gate_ops"), mine + 7)
                op(v.tensor_tensor(xn, xn, z, ALU.mult))
                dve.wait_ge(sem("gate_ops"), mine + 8)
                op(v.tensor_tensor(xn, xn, a, ALU.add))

            def state_lo(s, w):
                n, c0 = WIN_LEN[w], WIN_COL[w]
                dve.wait_ge(sem("state_hi"), NW * s + w + 1)
                v.tensor_tensor(x_lo[:, :, c0:c0 + n], x_new[:, :, 0:n], x_hi[:, :, c0:c0 + n].bitcast(F32), ALU.subtract)\
                 .then_inc(sem("state_lo"), 1)

            for u in range(FILL_B):
                relu_lo(u, u)
            with dve.Fori(0, STEPS) as s:
                for u in range(FILL_B, USES):
                    relu_lo(USES * s + u, u)
                msg_lo(s, 0)
                for w in range(1, NW):
                    gates(s, w - 1, 0)
                    if w < NW - 1:
                        msg_lo(s, w)
                    gates(s, w - 1, 1)
                    state_lo(s, w - 1)
                msg_lo(s, NW - 1)
                for u in range(FILL_A):
                    relu_lo(USES * s + USES + u, u)
                gates(s, NW - 1, 0)
                for u in range(FILL_A, FILL_B):
                    relu_lo(USES * s + USES + u, u)
                gates(s, NW - 1, 1)
                state_lo(s, NW - 1)

            dve.wait_ge(sem("state_lo"), NW * (STEPS + 1))
            dve.wait_ge(sem("relu_lo"), USES * STEPS + FILL_B)
            v.tensor_copy(ident_r[:], ident[:]).then_inc(sem("ident_r"), 1)
            dve.wait_ge(sem("x_again"), 32)
            for u in range(USES):
                m = min(2, NT - 2 * u)
                dve.wait_ge(sem("rows"), u + 1)
                xs = x1[:, 2 * u:2 * u + m, :].rearrange("p t d -> p (t d)")
                v.tensor_tensor(xs, xs, bank[u % 2][:, 0:m * D], ALU.add).then_inc(sem("x1_sum"), 1)
                if u:
                    dve.wait_ge(sem("x1_sum"), u)
                    for t in (2 * u - 2, 2 * u - 1):
                        v.bn_stats(st2[:, t, :], x1[:, t, :])
            dve.wait_ge(sem("x1_sum"), USES)
            link(v.bn_stats(st2[:, NT - 1, :], x1[:, NT - 1, :]))
            for t in range(NT):
                last = v.bn_aggr(mv2[:, t, :], st2[:, t, :])
            link(last)
            v.tensor_scalar(rstd2[:], mv2[:, :, 1], 1e-5, None, ALU.add).then_inc(sem("var_ready"), 1)
            dve.wait_ge(sem("gate_in"), 64)
            link(v.tensor_copy(wg_r[0][:], wg[:]))
            v.tensor_tensor(wg_r[1][:], wg[:], wg_r[0][:].bitcast(F32), ALU.subtract).then_inc(sem("wg_split"), 1)
            dve.wait_ge(sem("hid_bias_t"), 1)
            v.tensor_copy(hid_bias[:], bank[5][:, 0:BLOCKS]).then_inc(sem("hid_bias_sb"), 1)
            dve.wait_ge(sem("rstd_ready"), 2)
            dve.wait_ge(sem("x1_out"), 16)
            for t in range(NT):
                v.tensor_scalar(x1[:, t, :], x1[:, t, :], mv2[:, t, 0:1], rstd2[:, t:t + 1], ALU.subtract, ALU.mult)\
                 .then_inc(sem("x1_norm"), 1)
            for u in range(USES):
                m = min(2, NT - 2 * u) * P
                dve.wait_ge(sem("x2t_hi"), u + 1)
                v.tensor_tensor(x_lo[:, :, 2 * P * u:2 * P * u + m],
                                bank[2 + u % 2][:, 0:DT * m].rearrange("p (t n) -> p t n", t=DT),
                                x_hi[:, :, 2 * P * u:2 * P * u + m].bitcast(F32), ALU.subtract).then_inc(sem("x2t_lo"), 1)
            dve.wait_ge(sem("logits"), 1)
            dve.wait_ge(sem("iotas"), 10)
            lg = bank[4][:, 0:NT * NX].rearrange("p (t e) -> p t e", e=NX)

            def over_tiles(row):
                return row[:].rearrange("p (a e) -> p a e", a=1).broadcast_to([P, NT, NX])

            def over_experts(k):
                return top[:, k, :].rearrange("p (t a) -> p t a", a=1).broadcast_to([P, NT, NX])

            link(v.tensor_tensor(logit[:], lg, bg_b[:, 0:1, :].broadcast_to([P, NT, NX]), ALU.add))
            link(v.tensor_tensor(logit[:], logit[:], bg_b[:, 1:2, :].broadcast_to([P, NT, NX]), ALU.add))
            for k, hot_k in enumerate((hot1, hot2)):
                link(v.tensor_reduce(top[:, k, :], logit[:], AX.X, ALU.max))
                link(v.tensor_tensor(cand[:], logit[:], over_experts(k), ALU.is_equal))
                link(v.tensor_scalar(cand[:], cand[:], float(-NX), float(NX), ALU.mult, ALU.add))
                link(v.tensor_tensor(cand[:], cand[:], eid[:], ALU.add))
                link(v.tensor_reduce(top[:, 4, :], cand[:], AX.X, ALU.min))
                link(v.tensor_tensor(hot_k[:], eid[:], over_experts(4), ALU.is_equal))
                if k == 0:
                    link(v.tensor_scalar(cand[:], hot_k[:], -3.0e38, None, ALU.mult))
                    link(v.tensor_tensor(logit[:], logit[:], cand[:], ALU.add))
            v.tensor_tensor(top[:, 2, :], top[:, 1, :], top[:, 0, :], ALU.subtract).then_inc(sem("top_diff"), 1)
            link(v.tensor_scalar(hot1[:, NT - 1, :], hot1[:, NT - 1, :], valid[:, 0:1], None, ALU.mult))
            link(v.tensor_scalar(hot2[:, NT - 1, :], hot2[:, NT - 1, :], valid[:, 0:1], None, ALU.mult))
            v.tensor_tensor(chosen[:], hot1[:], hot2[:], ALU.add).then_inc(sem("chosen"), 1)
            dve.wait_ge(sem("top_exp"), 1)
            link(v.tensor_scalar(top[:, 3, :], top[:, 2, :], 1.0, None, ALU.add))
            link(v.reciprocal(top[:, 4, :], top[:, 3, :]))
            link(v.tensor_tensor(top[:, 5, :], top[:, 2, :], top[:, 4, :], ALU.mult))
            dve.wait_ge(sem("earlier"), 1)
            per = bank[6][:, 0:2 * NT * NX].rearrange("p (i t e) -> p i t e", i=2, e=NX)
            link(v.memset(cand[:, 0, :], 0.0))
            for t in range(1, NT):
                link(v.tensor_tensor(cand[:, t, :], cand[:, t - 1, :], per[:, 1, t - 1, :], ALU.add))
            link(v.tensor_tensor(room[:, 0, :], cand[:, NT - 1, :], per[:, 1, NT - 1, :], ALU.add))
            link(v.tensor_scalar(room[:, 0, :], room[:, 0, :], float(TILE - 1), None, ALU.add))
            link(v.tensor_copy(roomi[:], room[:, 0, :]))
            link(v.tensor_scalar(tiles_of[:, 0:NX], roomi[:], TILE.bit_length() - 1, None, ALU.arith_shift_right))
            link(v.tensor_copy(room[:, 0, :], tiles_of[:, 0:NX]))
            link(v.tensor_reduce(room[:, 1, NX - 1:NX], room[:, 0, :], AX.X, ALU.add))
            v.tensor_copy(tiles_of[:, NX:NX + 1], room[:, 1, NX - 1:NX]).then_inc(sem("tiles_of"), 1)
            link(v.memset(room[:, 1, 0:1], 0.0))
            for e in range(1, NX):
                link(v.scalar_tensor_tensor(room[:, 1, e:e + 1], room[:, 0, e - 1:e], float(TILE), room[:, 1, e - 1:e], ALU.mult, ALU.add))
            link(v.tensor_tensor(cand[:], cand[:], per[:, 0], ALU.add))
            link(v.tensor_tensor(cand[:], cand[:], room[:, 1:2, :].broadcast_to([P, NT, NX]), ALU.add))
            for k, hot_k in enumerate((hot1, hot2)):
                link(v.tensor_tensor(logit[:], hot_k[:], cand[:], ALU.mult))
                link(v.tensor_reduce(top[:, k, :], logit[:], AX.X, ALU.add))
            v.tensor_copy(slot_of[:], top[:, 0:2, :]).then_inc(sem("slot_of"), 1)
            for c in range(CHUNKS):
                dve.wait_ge(sem("chunk_hi"), c + 1)
                hi, lo = chunk_dst(c)
                src_ = raw[c % 4][:] if c % 4 < DT else raw[c % 4][:].rearrange("p (t d) -> p t d", t=2)
                v.tensor_tensor(lo, src_, hi.bitcast(F32), ALU.subtract).then_inc(sem("chunk_lo"), 1)

            def split_tile(turn):
                dve.wait_ge(sem("xt_hi2"), turn)
                for f in range(DT):
                    v.tensor_tensor(xt_lo[:, f, :], bank[4 + f][:], xt_hi[:, f, :].bitcast(F32), ALU.subtract).then_inc(sem("xt_split"), 1)

            dve.wait_ge(sem("chunk_lo"), CHUNKS)
            dve.wait_ge(sem("out_bias_in"), 16 * NX)
            split_tile(1)
            done = dve.alloc_register("dve_tiles")
            dve.reg_mov(done, 0)
            for e in range(NX):
                tiles = dve.value_load(tiles_of[0:1, e:e + 1], min_val=0, max_val=MAX_TILES)
                with dve.If(tiles > 0):
                    with dve.Fori(0, tiles):
                        n = dve.snap(done)
                        for h in range(HT):
                            i = e * HT + h
                            dve.wait_ge(sem("h_hi"), HT * n + (h + 1))
                            v.tensor_scalar(act_h[h % 2][:], bank[h][:], hid_bias[:, i:i + 1], 0.0, ALU.add, ALU.max).then_inc(sem("h_relu"), 1)
                            dve.wait_ge(sem("h_relu"), HT * n + (h + 1))
                            v.tensor_tensor(h_lo[:, h, :], act_h[h % 2][:], h_hi[:, h, :].bitcast(F32), ALU.subtract).then_inc(sem("h_lo"), 1)
                        split_tile(n + 2)
                        dve.wait_ge(sem("y_stored"), 16 * n + 1)
                        for j in range(2):
                            dve.wait_ge(sem("y_sums"), 2 * n + (j + 3))
                            v.tensor_tensor(slot_y[:, 2 * j:2 * j + 2, :], bank[6 + j][:].rearrange("p (t d) -> p t d", t=2),
                                            out_bias[:, e:e + 1, :].broadcast_to([P, 2, D]), ALU.add).then_inc(sem("y_ready"), 1)
                        dve.reg_add(done, done, 1)
            dve.wait_ge(sem("x1_in"), 16)
            for t in range(NT):
                m = TAIL if t == NT - 1 else P
                if t % 2 == 0:
                    dve.wait_ge(sem(f"gathered{t // 2}"), 32 * min(2, NT - t))
                v.scalar_tensor_tensor(x1[0:m, t, :], y_pair[0:m, t, 0, :], top[0:m, 4, t:t + 1], x1[0:m, t, :], ALU.mult, ALU.add).then_inc(sem("first_summed"), 1)
                dve.wait_ge(sem("first_summed"), t + 1)
                v.scalar_tensor_tensor(x1[0:m, t, :], y_pair[0:m, t, 1, :], top[0:m, 5, t:t + 1], x1[0:m, t, :], ALU.mult, ALU.add).then_inc(sem("summed"), 1)

        @block.scalar
        def _(act):
            a = nc.scalar
            act.wait_ge(sem("w_tr"), 1)
            a.activation(w1t[0][:], bank[4][:].rearrange("p (t j) -> p t j", t=DT), ACT.Copy).then_inc(sem("w_hi"), 1)
            for j in range(4):
                t, c = j // 2, j % 2
                act.wait_ge(sem("w_tr"), 7 + j)
                a.activation(wht[0][:, t, c * 384:(c + 1) * 384], bank[j % 2][:, 0:384], ACT.Copy).then_inc(sem("w_hi"), 1)
            for j in range(4):
                t, c = j // 2, j % 2
                act.wait_ge(sem("wc_scaled"), 1 + j)
                a.activation(wct[0][:, t, c * 384:(c + 1) * 384], e_f[2][:].rearrange("p g e -> p (g e)")[:, 0:384], ACT.Copy).then_inc(sem("w_hi"), 1)
            for u in range(USES):
                m = min(2, NT - 2 * u) * P
                act.wait_ge(sem("xt"), u + 1)
                a.activation(x_hi[:, :, 2 * P * u:2 * P * u + m], bank[6 + u % 2][:, 0:DT * m].rearrange("p (t n) -> p t n", t=DT),
                             ACT.Copy).then_inc(sem("xt_hi"), 1)
            def degree_copy(i, p):
                act.wait_ge(sem("deg_sum"), GROUP // 2 * i + (p + 1))
                a.activation(degree[:, bass.ds(i * (GROUP * SW) + p * 2 * SW, 2 * SW)], bank[6 + p % 2][:, 0:2 * SW], ACT.Copy).then_inc(sem("deg_done"), 1)

            with act.Fori(0, TURNS) as i:
                for b in range(GROUP):
                    act.wait_ge(sem("slice_full"), GROUP * i + (b + 1))
                    if b % 2 == 0:
                        act.wait_ge(sem("stage_free"), GROUP // 2 * i + (b // 2 + 1))
                    a.activation(trash[b % RING][:], bank[b % RING][:, 0:NT * SW], ACT.Relu, bias=minus_exact[:, 0:1],
                                 accum_out=over[:, bass.ds(GROUP * i + b, 1)])
                    a.activation(stage[b // 2 % 2][:, :, (b % 2) * SW:(b % 2 + 1) * SW], bank[b % RING][:, 0:NT * SW].rearrange("p (q c) -> p q c", c=SW),
                                 ACT.Copy, saturate=False).then_inc(sem("stage_full"), 1)
                    if b % 2 and b > 1:
                        degree_copy(i, b // 2 - 1)
                degree_copy(i, GROUP // 2 - 1)

            slow = read_slow_flag(act)
            with act.If(slow > 0):
                with act.Fori(0, NSL) as sl:
                    act.wait_ge(sem("exact_full"), sl + 1)
                    act.wait_ge(sem("exact_stored"), 32 * sl + 1)
                    a.activation(exact_sum[:], bank[0][:, 0:NT * SW], ACT.Copy)
                    a.activation(exact_part[0][:], bank[0][:, 0:NT * SW], ACT.Copy).then_inc(sem("exact_hi"), 1)
                act.wait_ge(sem("exact_deg_sum"), NW)
                act.wait_ge(sem("exact_stored"), EXACT_STORED)
            act.wait_ge(sem("stage_free"), NSL // 2 + 2)

            def relu_hi(g, u):
                m = min(2, NT - 2 * u)
                act.wait_ge(sem("relu_sums"), g + 1)
                a.activation(r_hi[:, 2 * u:2 * u + m, :].rearrange("p t d -> p (t d)"), bank[RELU_BANK[u]][:, 0:m * D], ACT.Relu)\
                 .then_inc(sem("relu_hi"), 1)

            def msg_hi(s, w):
                n = WIN_LEN[w]
                if w:
                    act.wait_ge(sem("gate_sums"), half(s, w, 0) * 4)
                for f in range(DT):
                    act.wait_ge(sem("msg_sums"), half(s, w, f) + 1)
                    a.activation(m_hi[:, f, 0:n], bank[2 * (w % 2) + f][:, 0:n], ACT.Copy).then_inc(sem("msg_hi"), 1)

            def gates(s, w, f):
                n = WIN_LEN[w]
                mine = half(s, w, f) * 3
                theirs = half(s, w, f) * GATE_OPS + LEAD
                act.wait_ge(sem("gate_ops"), theirs + 1)
                a.activation(gate_a[:, 0:n], gate_a[:, 0:n], ACT.Sigmoid, bias=gate_bias[:, f:f + 1]).then_inc(sem("gate_acts"), 1)
                act.wait_ge(sem("gate_ops"), theirs + 2)
                a.activation(gate_z[:, 0:n], gate_z[:, 0:n], ACT.Sigmoid, bias=gate_bias[:, 2 + f:3 + f]).then_inc(sem("gate_acts"), 1)
                act.wait_ge(sem("gate_ops"), theirs + 5)
                a.activation(gate_a[:, 0:n], gate_a[:, 0:n], ACT.Tanh, bias=gate_bias[:, 4 + f:5 + f]).then_inc(sem("gate_acts"), 1)

            def state_hi(s, w):
                n, c0 = WIN_LEN[w], WIN_COL[w]
                act.wait_ge(sem("gate_ops"), half(s, w, 2) * GATE_OPS + LEAD)
                a.activation(x_hi[:, :, c0:c0 + n], x_new[:, :, 0:n], ACT.Copy).then_inc(sem("state_hi"), 1)

            for u in range(FILL_B):
                relu_hi(u, u)
            with act.Fori(0, STEPS) as s:
                for u in range(FILL_B, USES):
                    relu_hi(USES * s + u, u)
                msg_hi(s, 0)
                for w in range(1, NW):
                    gates(s, w - 1, 0)
                    if w < NW - 1:
                        msg_hi(s, w)
                    gates(s, w - 1, 1)
                    state_hi(s, w - 1)
                msg_hi(s, NW - 1)
                for u in range(FILL_A):
                    relu_hi(USES * s + USES + u, u)
                gates(s, NW - 1, 0)
                for u in range(FILL_A, FILL_B):
                    relu_hi(USES * s + USES + u, u)
                gates(s, NW - 1, 1)
                state_hi(s, NW - 1)

            def logit_rows(g):
                n = min(4, NT - 4 * g) * P
                act.wait_ge(sem("logits_t"), g + 1)
                a.activation(logit_t[:, g * 4 * P:g * 4 * P + n], bank[6 + g % 2][0:NX, 0:n], ACT.Copy).then_inc(sem("logit_rows"), 1)

            for u in range(USES):
                m = min(2, NT - 2 * u) * P
                act.wait_ge(sem("x2t"), u + 1)
                a.activation(x_hi[:, :, 2 * P * u:2 * P * u + m], bank[2 + u % 2][:, 0:DT * m].rearrange("p (t n) -> p t n", t=DT),
                             ACT.Copy).then_inc(sem("x2t_hi"), 1)
                if u % 2 and u > 1:
                    logit_rows(u // 2 - 1)
            for g in range(LG - 2, LG):
                logit_rows(g)
            act.wait_ge(sem("top_diff"), 1)
            a.activation(top[:, 2, :], top[:, 2, :], ACT.Exp).then_inc(sem("top_exp"), 1)
            for c in range(CHUNKS):
                act.wait_ge(sem(f"chunk_in{c % 4}"), 16 * (c // 4 + 1))
                hi, lo = chunk_dst(c)
                src_ = raw[c % 4][:] if c % 4 < DT else raw[c % 4][:].rearrange("p (t d) -> p t d", t=2)
                a.activation(hi, src_, ACT.Copy).then_inc(sem("chunk_hi"), 1)
            act.wait_ge(sem("chunk_lo"), CHUNKS)

            def tile_hi(turn):
                act.wait_ge(sem("tile_turned"), turn)
                for f in range(DT):
                    last = a.activation(xt_hi[:, f, :], bank[4 + f][:], ACT.Copy)
                last.then_inc(sem("xt_hi2"), 1)

            tile_hi(1)
            act.wait_ge(sem("tiles_of"), 1)
            done = act.alloc_register("act_tiles")
            act.reg_mov(done, 0)
            for e in range(NX):
                tiles = act.value_load(tiles_of[0:1, e:e + 1], min_val=0, max_val=MAX_TILES)
                with act.If(tiles > 0):
                    with act.Fori(0, tiles):
                        n = act.snap(done)
                        act.wait_ge(sem("y_sums"), 2 * n + 2)
                        for h in range(HT):
                            i = e * HT + h
                            act.wait_ge(sem("h_sums"), HT * n + (h + 1))
                            a.activation(h_hi[:, h, :], bank[h][:], ACT.Relu, bias=hid_bias[:, i:i + 1]).then_inc(sem("h_hi"), 1)
                        tile_hi(n + 2)
                        act.reg_add(done, done, 1)

        @block.tensor
        def _(pe):
            mm = nc.tensor.matmul
            pe.wait_ge(sem("ident_ready"), 1)
            pe.wait_ge(sem("keys"), 1)
            for i in range(2):
                for g in range(2 * CB // P):
                    src_ = min(g, CG - 1)
                    last = nc.tensor.transpose(bank[2 * i + g // 4][:, g % 4 * P:(g % 4 + 1) * P], e_f[i][:, src_, :], ident[:])
            last.then_inc(sem("keys_t"), 1)
            pe.wait_ge(sem("diags"), 1)
            pe.wait_ge(sem("ones_ready"), 1)
            for m in range(2):
                for g in range(CG):
                    last = mm(bank[4 + 2 * m + g // 4][:, g % 4 * P:(g % 4 + 1) * P], ones_f[:], diag[:, m, g, :], start=True, stop=True)
            last.then_inc(sem("lims_b"), 1)
            pe.wait_ge(sem("first_diag"), 1)
            pe.wait_ge(sem("edge_table"), 1)
            for t in range(SL_T):
                last = mm(bank[3][:, t * P:(t + 1) * P], ones_f[:], diag[:, 0, t, :], start=True, stop=True)
            last.then_inc(sem("first_b"), 1)
            pe.wait_ge(sem("w1_scaled"), 1)
            for t in range(DT):
                for h in range(DT):
                    last = nc.tensor.transpose(bank[4][:, t * D + h * P:t * D + (h + 1) * P], w1n[:, h, t * P:(t + 1) * P], ident[:])
            last.then_inc(sem("w_tr"), 1)
            for t in range(DT):
                last = mm(bank[5][:, 0:D], ones_f[:], b1_diag[:, t, :], start=t == 0, stop=t == DT - 1)
            last.then_inc(sem("w_tr"), 1)
            for j in range(4):
                t, c = j // 2, j % 2
                if j >= 2:
                    pe.wait_ge(sem("wit_ready"), j - 1)
                for o in range(3):
                    last = nc.tensor.transpose(bank[6 + j % 2][:, o * P:(o + 1) * P], win[:, 3 * c + o, t * P:(t + 1) * P], ident[:])
                last.then_inc(sem("w_tr"), 1)
            pe.wait_ge(sem("edge_table"), 1)
            for j in range(4):
                t, c = j // 2, j % 2
                if j >= 2:
                    pe.wait_ge(sem("w_lo"), j)
                for o in range(3):
                    last = nc.tensor.transpose(bank[j % 2][:, o * P:(o + 1) * P], whn[:, 3 * c + o, t * P:(t + 1) * P], ident[:])
                last.then_inc(sem("w_tr"), 1)
            pe.wait_ge(sem("wit_ready"), 4)
            pe.wait_ge(sem("bound_col"), 1)
            for o in range(GT):
                for t in range(DT):
                    last = mm(bank[2][:, o:o + 1], wit[:, t, o * P:(o + 1) * P], b2_col[:, t:t + 1], start=t == 0, stop=t == DT - 1)
            last.then_inc(sem("w_tr"), 1)
            for j in range(4):
                t, c = j // 2, j % 2
                if j == 0:
                    pe.wait_ge(sem("w_lo"), 1)
                    pe.wait_ge(sem("b1_done"), 1)
                if j >= 2:
                    pe.wait_ge(sem("wc_scaled"), j - 1)
                for m in range(DT):
                    last = mm(bank[4 + j % 2][:, 0:384], w2n[:, m, t * P:(t + 1) * P], wit[:, m, c * 384:(c + 1) * 384],
                              start=m == 0, stop=m == DT - 1)
                last.then_inc(sem("w_tr"), 1)
            pe.wait_ge(sem("picked"), 1)
            pe.wait_ge(sem("w_lo"), 6)
            half_n = NSL // 2 * SLOTS
            for i in range(2):
                for h in range(2):
                    for g in range(CG):
                        last = mm(bank[(2 - 2 * i) + h][:, 0:half_n], e_f[i][:, g, :], picked[:, g, h * half_n:(h + 1) * half_n],
                                  start=g == 0, stop=g == CG - 1)
            last.then_inc(sem("slot_sums"), 1)
            for u in range(USES):
                m = min(2, NT - 2 * u)
                pe.wait_ge(sem("x_norm"), 2 * u + m)
                if u >= 2:
                    pe.wait_ge(sem("xt_lo"), u - 1)
                for t in range(DT):
                    for k in range(m):
                        last = nc.tensor.transpose(bank[6 + u % 2][:, (t * m + k) * P:(t * m + k + 1) * P],
                                                   xa[:, 2 * u + k, t * P:(t + 1) * P], ident[:])
                last.then_inc(sem("xt"), 1)

            pe.wait_ge(sem("w_lo"), 9)
            pe.wait_ge(sem("slot_tables"), 1)
            pe.wait_ge(sem("state_lo"), NW)
            for name, n in (("stage_full", RING), ("hot_free", 2), ("hots_full", GROUP), ("deg_done", 2)):
                mm(bank[5][:, 0:2], ones_h[:], ones_h[:, 0:2], start=True, stop=True).then_inc(sem(name), n)
            def degree_sum(i, p):
                pe.wait_ge(sem("deg_done"), GROUP // 2 * i + (p + 1))
                pe.wait_ge(sem("stage_full"), GROUP * i + (2 * p + 2 + RING))
                mm(bank[5][:, 0:2], ones_h[:], ones_h[:, 0:2], start=True, stop=True)
                for q in range(NT):
                    last = mm(bank[6 + p % 2][:, 0:2 * SW], ones_h[:], stage[p % 2][:, q, :], start=q == 0, stop=q == NT - 1)
                last.then_inc(sem("deg_sum"), 1)

            with pe.Fori(0, TURNS) as i:
                for b in range(GROUP):
                    pe.wait_ge(sem("stage_full"), GROUP * i + (b + 1))
                    pe.wait_ge(sem("hots_full"), GROUP * i + (b + GROUP + 1))
                    for s in range(SLOTS):
                        k = (b % 2) * SLOTS + s
                        ins = mm(bank[b % RING][:, 0:NT * SW], hot_row[k][:], hot_key[k][:], start=s == 0, stop=s == SLOTS - 1)
                    ins.then_inc(sem("slice_full"), 1)
                    mm(bank[5][:, 0:2], ones_h[:], ones_h[:, 0:2], start=True, stop=True).then_inc(sem("hot_free"), 1)
                    if b % 2 and b > 1:
                        degree_sum(i, b // 2 - 1)
                degree_sum(i, GROUP // 2 - 1)
            pe.wait_ge(sem("stage_free"), NSL // 2 + 2)
            pe.wait_ge(sem("more"), 1)
            mm(bank[3][0:1, 0:1], more[:, SL_T + 1:SL_T + 2], ones_f[:, 0:1], start=True, stop=True).then_inc(sem("slow_sum"), 1)
            pe.wait_ge(sem("deg_done"), NSL // 2 + 2)
            slow = read_slow_flag(pe)
            with pe.If(slow > 0):
                for name in ("exact_stored", "exact_hi", "chunk_used"):
                    mm(bank[5][:, 0:2], ones_h[:], ones_h[:, 0:2], start=True, stop=True).then_inc(sem(name), 1)
                taken = pe.alloc_register("pe_taken")
                pe.reg_mov(taken, 0)
                pe.wait_ge(sem("zero_key"), 1)
                with pe.Fori(0, NSL) as sl:
                    first = pe.value_load(bound_row[0:1, bass.ds(2 * sl, 1)], min_val=0, max_val=NCH)
                    end = pe.value_load(bound_row[0:1, bass.ds(2 * sl + 1, 1)], min_val=0, max_val=NCH)
                    pe.wait_ge(sem("exact_hi"), sl + 1)
                    mm(bank[0][:, 0:NT * SW], ones_h[:], hot_key[1][:], start=True, stop=True, skip_group_check=True)
                    with pe.If(end > first):
                        with pe.Fori(first, end) as c:
                            pe.wait_ge(sem("chunk_hot"), pe.snap(taken) + 1)
                            mm(bank[0][:, 0:NT * SW], hot_row[0][:], hot_key[0][:], start=False, stop=True, skip_group_check=True)\
                                .then_inc(sem("chunk_used"), 1)
                            pe.reg_add(taken, taken, 1)
                    mm(bank[5][:, 0:2], ones_h[:], ones_h[:, 0:2], start=True, stop=True).then_inc(sem("exact_full"), 1)
                for w in range(NW):
                    pe.wait_ge(sem("planes_in"), 32 * (w + 1))
                    if w >= 4:
                        pe.wait_ge(sem("exact_deg_done"), w - 3)
                    for q in range(NT):
                        for i in range(2):
                            last = mm(bank[4 + w % 4][:, 0:WIN_LEN[w]], ones_h[:], planes[:, i, q, 0:WIN_LEN[w]],
                                      start=q == 0 and i == 0, stop=q == NT - 1 and i == 1)
                    last.then_inc(sem("exact_deg_sum"), 1)
                pe.wait_ge(sem("exact_deg_done"), NW)

            def relu_sum(t, u):
                m = min(2, NT - 2 * u)
                before_it = max([v for v in range(u) if RELU_BANK[v] == RELU_BANK[u]], default=-1)
                if not isinstance(t, int) or before_it >= 0:
                    pe.wait_ge(sem("relu_lo"), USES * t + before_it + 1)
                if not isinstance(t, int) and RELU_BANK[u] < 2 and before_it < 0:
                    pe.wait_ge(sem("msg_lo"), half(t, 0, 0))
                pe.wait_ge(sem("state_lo"), NW * t + USE_WIN[u] + 1)
                o = bank[RELU_BANK[u]]
                for k in range(m):
                    last = mm(o[:, k * D:(k + 1) * D], ones_r[:], b1_rows[:], start=k == 0, stop=False, skip_group_check=True)
                for k in range(m):
                    n0 = (2 * u + k) * P
                    for t in range(DT):
                        for xs, ws in ((x_hi, w1t[0]), (x_hi, w1t[1]), (x_lo, w1t[0])):
                            last = mm(o[:, k * D:(k + 1) * D], xs[:, t, n0:n0 + P], ws[:, t, :], start=False,
                                      stop=True, skip_group_check=True)
                last.then_inc(sem("relu_sums"), 1)

            def messages(s, w, f, q0, q1, exact):
                n, c0 = WIN_LEN[w], WIN_COL[w]
                if exact:
                    pe.wait_ge(sem("planes_in"), (s + 1) * (32 * NW) + 32 * (w + 1))
                for q in range(q0, q1):
                    counts = [planes[:, i, q, 0:n] for i in range(2)] if exact else [adj[:, q, c0:c0 + n]]
                    todo = [(r, c) for c in counts for r in (r_hi, r_lo)]
                    for i, (r, c) in enumerate(todo):
                        last = mm(bank[2 * (w % 2) + f][:, 0:n], r[:, q, f * P:(f + 1) * P], c,
                                  start=q == 0 and i == 0, stop=q == NT - 1 and i == len(todo) - 1)
                if q1 == NT:
                    last.then_inc(sem("msg_sums"), 1)

            def gates(s, w, f):
                n, c0 = WIN_LEN[w], WIN_COL[w]
                if f == 0:
                    pe.wait_ge(sem("msg_lo"), half(s, w, 2))
                for k, (b, parts) in enumerate(((4, (("h", f), ("m", f))), (5, (("h", 2 + f), ("m", 2 + f))),
                                                (6, (("h", 4 + f),)), (7, (("m", 4 + f),)))):
                    todo = []
                    for what, o in parts:
                        for t in range(DT):
                            if what == "h":
                                hi, lo, wt = x_hi[:, t, c0:c0 + n], x_lo[:, t, c0:c0 + n], wht
                            else:
                                hi, lo, wt = m_hi[:, t, 0:n], m_lo[:, t, 0:n], wct
                            wh, wl = (wt[i][:, t, o * P:(o + 1) * P] for i in range(2))
                            todo += [(wh, hi), (wh, lo), (wl, hi)]
                    pe.wait_ge(sem("gate_ops"), half(s, w, f) * GATE_OPS + (k + 1))
                    for i, (wgt, mov) in enumerate(todo):
                        last = mm(bank[b][:, 0:n], wgt, mov, start=i == 0, stop=i == len(todo) - 1)
                    last.then_inc(sem("gate_sums"), 1)

            late = 2 * EARLY
            for u in range(FILL_B):
                relu_sum(0, u)

            def all_steps(exact):
                with pe.Fori(0, STEPS) as s:
                    for u in range(FILL_B, EARLY):
                        relu_sum(s, u)
                    pe.wait_ge(sem("relu_lo"), USES * s + EARLY)
                    mm(bank[0][:, 0:2], ones_r[:], b1_rows[:, 0:2], start=True, stop=True)
                    messages(s, 0, 0, 0, late, exact)
                    messages(s, 0, 1, 0, late, exact)
                    for u in range(EARLY, USES):
                        relu_sum(s, u)
                    pe.wait_ge(sem("relu_lo"), USES * s + USES)
                    mm(bank[3][:, 0:2], ones_r[:], b1_rows[:, 0:2], start=True, stop=True)
                    messages(s, 0, 0, late, NT, exact)
                    messages(s, 0, 1, late, NT, exact)
                    for w in range(1, NW):
                        messages(s, w, 0, 0, NT, exact)
                        gates(s, w - 1, 0)
                        if w < NW - 1:
                            messages(s, w, 1, 0, NT, exact)
                        gates(s, w - 1, 1)
                    messages(s, NW - 1, 1, 0, NT, exact)
                    for u in range(FILL_A):
                        relu_sum(s + 1, u)
                    gates(s, NW - 1, 0)
                    for u in range(FILL_A, FILL_B):
                        relu_sum(s + 1, u)
                    gates(s, NW - 1, 1)

            with pe.If(slow > 0):
                all_steps(True)
            with pe.If(slow < 1):
                all_steps(False)

            pe.wait_ge(sem("state_lo"), NW * (STEPS + 1))
            pe.wait_ge(sem("ident_r"), 1)
            pe.wait_ge(sem("relu_lo"), USES * STEPS + FILL_B)
            for u in range(USES):
                m = min(2, NT - 2 * u)
                if u >= 2:
                    pe.wait_ge(sem("x1_sum"), u - 1)
                for k in range(m):
                    n0 = (2 * u + k) * P
                    for t in range(DT):
                        for xs in (x_hi, x_lo):
                            last = mm(bank[u % 2][:, k * D + t * P:k * D + (t + 1) * P], xs[:, t, n0:n0 + P], ident_r[:],
                                      start=k == 0 and t == 0 and xs is x_hi, stop=True, skip_group_check=True)
                last.then_inc(sem("rows"), 1)
            pe.wait_ge(sem("gate_in"), 64)
            pe.wait_ge(sem("x1_sum"), USES)
            nc.tensor.transpose(bank[5][:, 0:BLOCKS], hid_bias_rows[:], ident[0:BLOCKS, 0:BLOCKS]).then_inc(sem("hid_bias_t"), 1)
            pe.wait_ge(sem("wg_split"), 1)

            def logits_of(g):
                n = min(4, NT - 4 * g) * P
                pe.wait_ge(sem("x2t_lo"), min(2 * g + 2, USES))
                if g >= 2:
                    pe.wait_ge(sem("logit_rows"), g - 1)
                k = 0
                for t in range(DT):
                    for xs in (x_hi, x_lo):
                        for ws in wg_r:
                            last = mm(bank[6 + g % 2][0:NX, 0:n], ws[:, t, :], xs[:, t, g * 4 * P:g * 4 * P + n], start=k == 0, stop=k == 7)
                            k += 1
                last.then_inc(sem("logits_t"), 1)

            for u in range(USES):
                m = min(2, NT - 2 * u)
                pe.wait_ge(sem("x1_norm"), 2 * u + m)
                if u >= 2:
                    pe.wait_ge(sem("x2t_lo"), u - 1)
                for t in range(DT):
                    for k in range(m):
                        last = nc.tensor.transpose(bank[2 + u % 2][:, (t * m + k) * P:(t * m + k + 1) * P],
                                                   x1[:, 2 * u + k, t * P:(t + 1) * P], ident[:])
                last.then_inc(sem("x2t"), 1)
                if u % 2 == 0 and u:
                    logits_of(u // 2 - 1)
            logits_of(LG - 1)
            for g in range(LG):
                pe.wait_ge(sem("logit_rows"), g + 1)
                for t in range(4 * g, min(4 * g + 4, NT)):
                    last = nc.tensor.transpose(bank[4][:, t * NX:(t + 1) * NX], logit_t[:, t * P:(t + 1) * P], ident[0:NX, 0:NX])
            last.then_inc(sem("logits"), 1)
            pe.wait_ge(sem("chosen"), 1)
            sel = chosen[:].rearrange("p t e -> p (t e)")
            mm(bank[6][:, 0:NT * NX], before[:], sel, start=True, stop=True, skip_group_check=True)
            mm(bank[6][:, NT * NX:2 * NT * NX], all_ones[:], sel, start=False, stop=True, skip_group_check=True).then_inc(sem("earlier"), 1)

            def turn_tile(turn):
                pe.wait_ge(sem("tile_in"), 16 * turn)
                for f in range(DT):
                    for j in range(TT):
                        last = nc.tensor.transpose(bank[4 + f][:, j * P:(j + 1) * P], slot_x[:, j, f * P:(f + 1) * P], ident[:])
                last.then_inc(sem("tile_turned"), 1)

            pe.wait_ge(sem("hid_bias_sb"), 1)
            pe.wait_ge(sem("slot_of"), 1)
            for name, n in (("h_lo", HT), ("y_sums", 2), ("y_ready", 2), ("y_stored", 1)):
                mm(bank[5][:, 0:2], all_ones[:], before[:, 0:2], start=True, stop=True).then_inc(sem(name), n)
            turn_tile(1)
            done = pe.alloc_register("pe_tiles")
            pe.reg_mov(done, 0)
            pe.wait_ge(sem("chunk_lo"), CHUNKS)
            for e in range(NX):
                tiles = pe.value_load(tiles_of[0:1, e:e + 1], min_val=0, max_val=MAX_TILES)
                with pe.If(tiles > 0):
                    with pe.Fori(0, tiles):
                        n = pe.snap(done)
                        pe.wait_ge(sem("xt_split"), 2 * n + 2)
                        for h in range(HT):
                            pe.wait_ge(sem("h_lo"), HT * n + (h + 1))
                            k = 0
                            for t in range(DT):
                                for xs, ws in ((xt_hi, f1w[0]), (xt_lo, f1w[0]), (xt_hi, f1w[1])):
                                    last = mm(bank[h][:], ws[:, t, e, h * P:(h + 1) * P], xs[:, t, :], start=k == 0, stop=k == 5)
                                    k += 1
                            last.then_inc(sem("h_sums"), 1)
                        turn_tile(n + 2)
                        pe.wait_ge(sem("y_ready"), 2 * n + 2)
                        for j in range(TT):
                            for h in range(HT):
                                if j == 0:
                                    pe.wait_ge(sem("h_lo"), HT * n + (HT + h + 1))
                                for k, (hs, ws) in enumerate(((h_hi, f2w[0]), (h_lo, f2w[0]), (h_hi, f2w[1]))):
                                    last = mm(bank[6 + j // 2][:, (j % 2) * D:(j % 2 + 1) * D], hs[:, h, j * P:(j + 1) * P], ws[:, h, e, :],
                                              start=j % 2 == 0 and h == 0 and k == 0, stop=True, skip_group_check=True)
                            if j % 2:
                                last.then_inc(sem("y_sums"), 1)
                        pe.reg_add(done, done, 1)


_INS = ["x", "src", "dst"] + ["L0_gnn_" + n for n in ("W1", "b1", "W2", "b2", "W_ih", "b_ih", "W_hh", "b_hh")] \
    + ["L0_ffn_" + n for n in ("Wg", "bg", "bias", "W1", "b1", "W2", "b2")]


def kernel(**inputs):
    import numpy as _np
    import concourse.bacc as _bacc
    from concourse.bass_utils import run_bass_kernel_spmd as _run

    nc = _bacc.Bacc("TRN2", target_bir_lowering=False, num_devices=1)
    arrays, args = {}, []
    for name in _INS:
        a = _np.ascontiguousarray(inputs[name])
        arrays[f"in_{name}"] = a
        args.append(nc.dram_tensor(f"in_{name}", a.shape, mybir.dt.from_np(a.dtype), kind="ExternalInput").ap())
    args.append(nc.dram_tensor("out_0", (N, D), F32, kind="ExternalOutput").ap())
    gnn_ffn(nc, *args)
    r = _run(nc, [arrays], core_ids=[0])
    return r.results[0]["out_0"]
```
